# Optimizing a Trainium2 kernel written in Bass

```python
import numpy as np
import jax
import jax.numpy as jnp

def _softmax(x, axis=-1):
    return jax.nn.softmax(x, axis=axis)

def _gelu(x):
    return jax.nn.gelu(x, approximate=True)

def _silu(x):
    return jax.nn.silu(x)

def _sigmoid(x):
    return jax.nn.sigmoid(x)

def _layernorm(x, axis=-1, eps=1e-05):
    m = jnp.mean(x, axis=axis, keepdims=True)
    v = jnp.var(x, axis=axis, keepdims=True)
    return (x - m) / jnp.sqrt(v + eps)

def _scatter_add(tgt, idx, src, axis=0):
    return tgt.at[idx].add(src)

def _segment_sum(src, seg, n):
    return jax.ops.segment_sum(src, seg, n)
kernel_name = 'mk_prb_d1_jaxref_r8_83dc16'

def setup_inputs(seed: int=0):
    np.random.seed(seed)
    _w = jnp.asarray

    def _L0_attn_setup():
        import jax, jax.numpy as jnp
        import numpy as np
        EPS = 1e-06

        def elu1(x):
            return jax.nn.elu(x) + 1.0

        def causal_linear_attention(q, k, v, chunk=128):
            b, h, s, d = q.shape
            sq, sk = (elu1(q), elu1(k))
            nc = s // chunk
            rs = lambda x: x.reshape(b, h, nc, chunk, d).transpose(2, 0, 1, 3, 4)
            sqc, skc, vc = (rs(sq), rs(sk), rs(v))
            mask = jnp.tril(jnp.ones((chunk, chunk), dtype=q.dtype))

            def step(carry, xs):
                S, z = carry
                qc, kc, vcc = xs
                scores = jnp.einsum('bhid,bhjd->bhij', qc, kc) * mask
                num = jnp.einsum('bhij,bhje->bhie', scores, vcc) + jnp.einsum('bhid,bhde->bhie', qc, S)
                den = scores.sum(-1) + jnp.einsum('bhid,bhd->bhi', qc, z)
                out = num / jnp.clip(den, EPS)[..., None]
                S = S + jnp.einsum('bhjd,bhje->bhde', kc, vcc)
                z = z + kc.sum(2)
                return ((S, z), out)
            S0 = jnp.zeros((b, h, d, d), q.dtype)
            z0 = jnp.zeros((b, h, d), q.dtype)
            _, outs = jax.lax.scan(step, (S0, z0), (sqc, skc, vc))
            return outs.transpose(1, 2, 0, 3, 4).reshape(b, h, s, d)
        B, S, H, NH, NM = (2, 512, 256, 16, 4)
        HD = H // NH
        key = jax.random.key(seed)
        ks = jax.random.split(key, 12)
        p = lambda k, shp: jax.random.normal(k, shp, dtype=jnp.float32) * 0.02
        return {'hidden_states': jax.random.normal(ks[0], (B, S, H), dtype=jnp.float32), 'w_q': p(ks[1], (H, H)), 'w_k': p(ks[2], (H, H)), 'w_v': p(ks[3], (H, H)), 'w_o': p(ks[4], (H, H)), 'eg_w1': p(ks[5], (H // 4, H)), 'eg_b1': jnp.zeros((H // 4,), jnp.float32), 'eg_w2': p(ks[6], (1, H // 4)), 'eg_b2': jnp.zeros((1,), jnp.float32), 'memory_gate': jnp.zeros((NH,), jnp.float32), 'fine_memories': jax.random.uniform(ks[7], (NM, NH, HD, HD), dtype=jnp.float32) * 0.1, 'fine_memory_norms': jax.random.uniform(ks[8], (NM, NH, HD), dtype=jnp.float32) + 0.1}
    _L0_attn_in = _L0_attn_setup()

    def _L0_ffn_setup():
        import jax, jax.numpy as jnp
        import numpy as np
        B, S, H = (2, 128, 256)
        E, K, F = (8, 2, 176)
        N_SHARED = 2
        FS = F * N_SHARED
        ROUTED_SCALE = 1.0

        def _swiglu_mlp(x, wg, wu, wd):
            return jax.nn.silu(x @ wg.T) * (x @ wu.T) @ wd.T
        key = jax.random.key(seed)
        ks = jax.random.split(key, 8)

        def w(k, shape, fan_in):
            return jax.random.normal(k, shape, jnp.float32) * (1.0 / np.sqrt(fan_in))
        return {'hidden_states': jax.random.normal(ks[0], (B, S, H), jnp.float32), 'gate_weight': w(ks[1], (E, H), H), 'w_gate': w(ks[2], (E, F, H), H), 'w_up': w(ks[3], (E, F, H), H), 'w_down': w(ks[4], (E, H, F), F), 'sw_gate': w(ks[5], (FS, H), H), 'sw_up': w(ks[6], (FS, H), H), 'sw_down': w(ks[7], (H, FS), FS)}
    _L0_ffn_in = _L0_ffn_setup()
    _d = {'L0_attn_hidden_states': _L0_attn_in['hidden_states'], 'L0_attn_w_q': _L0_attn_in['w_q'], 'L0_attn_w_k': _L0_attn_in['w_k'], 'L0_attn_w_v': _L0_attn_in['w_v'], 'L0_attn_w_o': _L0_attn_in['w_o'], 'L0_attn_eg_w1': _L0_attn_in['eg_w1'], 'L0_attn_eg_b1': _L0_attn_in['eg_b1'], 'L0_attn_eg_w2': _L0_attn_in['eg_w2'], 'L0_attn_eg_b2': _L0_attn_in['eg_b2'], 'L0_attn_memory_gate': _L0_attn_in['memory_gate'], 'L0_attn_fine_memories': _L0_attn_in['fine_memories'], 'L0_attn_fine_memory_norms': _L0_attn_in['fine_memory_norms'], 'L0_ffn_gate_weight': _L0_ffn_in['gate_weight'], 'L0_ffn_w_gate': _L0_ffn_in['w_gate'], 'L0_ffn_w_up': _L0_ffn_in['w_up'], 'L0_ffn_w_down': _L0_ffn_in['w_down'], 'L0_ffn_sw_gate': _L0_ffn_in['sw_gate'], 'L0_ffn_sw_up': _L0_ffn_in['sw_up'], 'L0_ffn_sw_down': _L0_ffn_in['sw_down']}
    _x0 = _d['L0_attn_hidden_states']
    _d['L0_attn_hidden_states'] = jax.random.normal(jax.random.fold_in(jax.random.key(seed), 1), (4, 1024, 256), dtype=_x0.dtype)
    del _x0
    return _d

def reference(L0_attn_hidden_states, L0_attn_w_q, L0_attn_w_k, L0_attn_w_v, L0_attn_w_o, L0_attn_eg_w1, L0_attn_eg_b1, L0_attn_eg_w2, L0_attn_eg_b2, L0_attn_memory_gate, L0_attn_fine_memories, L0_attn_fine_memory_norms, L0_ffn_gate_weight, L0_ffn_w_gate, L0_ffn_w_up, L0_ffn_w_down, L0_ffn_sw_gate, L0_ffn_sw_up, L0_ffn_sw_down):

    def _L0_attn_ref(hidden_states, w_q, w_k, w_v, w_o, eg_w1, eg_b1, eg_w2, eg_b2, memory_gate, fine_memories, fine_memory_norms):
        import jax, jax.numpy as jnp
        import numpy as np
        EPS = 1e-06

        def elu1(x):
            return jax.nn.elu(x) + 1.0

        def causal_linear_attention(q, k, v, chunk=128):
            b, h, s, d = q.shape
            sq, sk = (elu1(q), elu1(k))
            nc = s // chunk
            rs = lambda x: x.reshape(b, h, nc, chunk, d).transpose(2, 0, 1, 3, 4)
            sqc, skc, vc = (rs(sq), rs(sk), rs(v))
            mask = jnp.tril(jnp.ones((chunk, chunk), dtype=q.dtype))

            def step(carry, xs):
                S, z = carry
                qc, kc, vcc = xs
                scores = jnp.einsum('bhid,bhjd->bhij', qc, kc) * mask
                num = jnp.einsum('bhij,bhje->bhie', scores, vcc) + jnp.einsum('bhid,bhde->bhie', qc, S)
                den = scores.sum(-1) + jnp.einsum('bhid,bhd->bhi', qc, z)
                out = num / jnp.clip(den, EPS)[..., None]
                S = S + jnp.einsum('bhjd,bhje->bhde', kc, vcc)
                z = z + kc.sum(2)
                return ((S, z), out)
            S0 = jnp.zeros((b, h, d, d), q.dtype)
            z0 = jnp.zeros((b, h, d), q.dtype)
            _, outs = jax.lax.scan(step, (S0, z0), (sqc, skc, vc))
            return outs.transpose(1, 2, 0, 3, 4).reshape(b, h, s, d)
        B, S, H = hidden_states.shape
        NH = memory_gate.shape[0]
        HD = H // NH
        split = lambda x: x.reshape(B, S, NH, HD).transpose(0, 2, 1, 3)
        q = split(hidden_states @ w_q.T)
        k = split(hidden_states @ w_k.T)
        v = split(hidden_states @ w_v.T)
        sq = elu1(q)
        M = fine_memories.sum(0)
        z = fine_memory_norms.sum(0)
        a_c = jnp.einsum('bhsd,hde->bhse', sq, M)
        n_c = jnp.clip(jnp.einsum('bhsd,hd->bhs', sq, z), EPS)[..., None]
        out_coarse = jnp.where(z.sum() < EPS, 0.0, a_c / n_c)
        a_f = jnp.einsum('bhsd,mhde->mbhse', sq, fine_memories)
        n_f = jnp.einsum('bhsd,mhd->mbhs', sq, fine_memory_norms)
        bank_dead = (fine_memory_norms.sum((1, 2)) < EPS)[:, None, None, None, None]
        outs = jnp.where(bank_dead, 0.0, a_f / jnp.clip(n_f, EPS)[..., None])
        rel = n_f.mean(-1)
        w = jax.nn.softmax(rel, axis=0)[..., None, None]
        out_fine = (outs * w).sum(0)
        coarse_repr = out_coarse.transpose(0, 2, 1, 3).reshape(B, S, H)
        gprob = jax.nn.sigmoid(jax.nn.relu(coarse_repr @ eg_w1.T + eg_b1) @ eg_w2.T + eg_b2)
        exp_prob = gprob.transpose(0, 2, 1)[..., None]
        memory_output = exp_prob * out_fine + (1.0 - exp_prob) * out_coarse
        local_output = causal_linear_attention(q, k, v)
        gate = jax.nn.sigmoid(memory_gate).reshape(1, NH, 1, 1)
        output = gate * memory_output + (1.0 - gate) * local_output
        output = output.transpose(0, 2, 1, 3).reshape(B, S, H)
        return output @ w_o.T

    def _L0_ffn_ref(hidden_states, gate_weight, w_gate, w_up, w_down, sw_gate, sw_up, sw_down):
        import jax, jax.numpy as jnp
        import numpy as np
        B, S, H = (2, 128, 256)
        E, K, F = (8, 2, 176)
        N_SHARED = 2
        FS = F * N_SHARED
        ROUTED_SCALE = 1.0

        def _swiglu_mlp(x, wg, wu, wd):
            return jax.nn.silu(x @ wg.T) * (x @ wu.T) @ wd.T
        b, s, h = hidden_states.shape
        x = hidden_states.reshape(-1, h)
        T = x.shape[0]
        logits = x.astype(jnp.float32) @ gate_weight.astype(jnp.float32).T
        scores = jax.nn.softmax(logits, axis=-1)
        topk_w, topk_idx = jax.lax.top_k(scores, K)
        topk_w = topk_w / (jnp.sum(topk_w, axis=-1, keepdims=True) + 1e-20)
        topk_w = topk_w * ROUTED_SCALE
        cw = jnp.zeros((T, E), jnp.float32).at[jnp.arange(T)[:, None], topk_idx].add(topk_w)
        g = jax.nn.silu(jnp.einsum('th,efh->tef', x, w_gate)) * jnp.einsum('th,efh->tef', x, w_up)
        expert_out = jnp.einsum('tef,ehf->teh', g, w_down)
        y = jnp.einsum('te,teh->th', cw, expert_out).reshape(b, s, h)
        y = y + _swiglu_mlp(x, sw_gate, sw_up, sw_down).reshape(b, s, h)
        return y
    x = L0_attn_hidden_states
    xn = _layernorm(x, axis=-1)
    x = x + _L0_attn_ref(xn, L0_attn_w_q, L0_attn_w_k, L0_attn_w_v, L0_attn_w_o, L0_attn_eg_w1, L0_attn_eg_b1, L0_attn_eg_w2, L0_attn_eg_b2, L0_attn_memory_gate, L0_attn_fine_memories, L0_attn_fine_memory_norms) + _L0_ffn_ref(xn, L0_ffn_gate_weight, L0_ffn_w_gate, L0_ffn_w_up, L0_ffn_w_down, L0_ffn_sw_gate, L0_ffn_sw_up, L0_ffn_sw_down)
    return x

_drawn_inputs = setup_inputs


def setup_inputs(seed=0):
    import zlib

    import numpy as np

    out = dict(_drawn_inputs(seed))
    spreads = {'L0_attn_eg_b1': (0.0, 2.0), 'L0_attn_memory_gate': (0.0, 0.8)}
    factors = {'L0_attn_w_q': 8.0,
     'L0_attn_w_k': 8.0,
     'L0_attn_w_v': 8.0,
     'L0_attn_w_o': 4.846,
     'L0_attn_eg_w1': 200.0,
     'L0_attn_eg_w2': 200.0,
     'L0_attn_fine_memories': 200.0,
     'L0_attn_fine_memory_norms': 200.0}
    for name, (base, spread) in spreads.items():
        noise = np.random.default_rng([zlib.crc32(name.encode()), seed]).standard_normal(out[name].shape)
        drawn = base * np.exp(spread * noise) if base else spread * noise
        out[name] = jnp.asarray(drawn.astype(out[name].dtype))
    for name, factor in factors.items():
        out[name] = (out[name] * factor).astype(out[name].dtype)
    return out
```

```python
import numpy as np

import concourse.bass as bass
from concourse import mybir
from contextlib import ExitStack

F32 = mybir.dt.float32
F32R = mybir.dt.float32r
BF16 = mybir.dt.bfloat16
ALU = mybir.AluOpType
ACT = mybir.ActivationFunctionType
AX = mybir.AxisListType

P = 128
B, SEQ, H = 4, 1024, 256
NT = SEQ // P
NS = 2
ST = SEQ // NS
TS = ST // P
KC = H // P
NH, HD, NM = 16, 16, 4
HH = NH // KC
HE = HD + 1
E, F, FS = 8, 176, 352
FR = E * F + FS
NF = -(-FR // P)
G1 = H // 4
EPS = 1e-6
LN_EPS = 1e-5
CW3 = 3 * E + 1

FROWS = [min(P, FR - f * P) for f in range(NF)]

FFN_STEPS = [(s, f, part) for s in range(NS) for f in range(NF) for part in ("gate", "up", "down")]
FFN = []
for _s in range(NS):
    FFN += [x for x in FFN_STEPS if x[0] == _s] + [(_s, NF, "down"), (_s, NF, "out")]


def tile_order():
    order, k = [], 0

    def ffn(n=1):
        nonlocal k
        for _ in range(n):
            if k < len(FFN):
                order.append(("ffn", k, 0))
                k += 1

    for t in range(NT):
        order.append(("norms", t, 0))
        order.append(("keys", t, 0))
        ffn()
        order.append(("scores", t, 0))
        order.append(("scores", t, 1))
        ffn()
        order.append(("scores", t, 2))
        order.append(("scores", t, 3))
        ffn()
        if t:
            order.append(("outT", t - 1, 0))
        order.append(("coarseT", t, 0))
        ffn()
        order.append(("hidden", t, 0))
        ffn()
        order.append(("local", t, 0))
        ffn()
        order.append(("gate", t, 0))
        if t < NT - 1:
            order.append(("state", t, 0))
        ffn()
        order.append(("fine", t, 0))
        ffn()
        order.append(("fine", t, 1))
        ffn()
        ffn()
    ffn(2)
    order.append(("outT", NT - 1, 0))
    ffn(len(FFN))
    return order


ORDER = tile_order()

NR = 3
RING = [("xT", s, kc) for s in range(NS) for kc in range(KC)]
RING += [("q", s, m) for s in range(NS) for m in range(KC)]
RING += [("v", t, 0) for t in range(NT)]
RING += [("mean", 0, 0)]
RING += [("k", s, m) for s in range(NS) for m in range(KC)]
RING += [("cwT", s, 0) for s in range(NS)]
RING += [x for x in ORDER if x[0] != "ffn"]
TURN = {use: n for n, use in enumerate(RING)}
USES = [len(range(r, len(RING), NR)) for r in range(NR)]

DVE_LINKS = 100
POOL_LINKS = 17


def build(nc, d, out_t):
    ctx = ExitStack()
    with ctx:
        def sb(name, shape, dt=F32):
            return ctx.enter_context(nc.sbuf_tensor(name, shape, dt))

        def sem(name):
            return ctx.enter_context(nc.semaphore(name))

        ident = sb("ident", [P, P])
        causal = sb("causal", [P, P])
        parity = sb("parity", [P, 2])
        same_head = sb("same_head", [P, HH])
        rank_e = sb("rank_e", [P, E])
        sel = sb("sel", [CW3, NF * P], BF16)
        ones = sb("ones", [P, P])
        half_neg = sb("half_neg", [P, NT])
        ln_eps = sb("ln_eps", [P, NT])
        varp = sb("varp", [P, NT])
        wg = [sb(f"wg{i}", [P, KC, FR], F32R) for i in range(2)]
        wu = [sb(f"wu{i}", [P, KC, FR], F32R) for i in range(2)]
        wd = [sb(f"wd{i}", [P, NF, H], F32R) for i in range(2)]
        wq = [sb(f"wq{i}", [P, KC, H], F32R) for i in range(2)]
        wk = [sb(f"wk{i}", [P, KC, H], F32R) for i in range(2)]
        wv = [sb(f"wv{i}", [P, KC, H + E], F32R) for i in range(2)]
        wo = sb("wo", [P, KC, H])
        w1 = sb("w1", [P, KC, G1])
        b1 = sb("b1", [G1, 1])
        w2 = sb("w2", [G1, 1])
        b2 = sb("b2", [P, 1])
        gate = sb("gate", [P, NH])
        keep = sb("keep", [P, NH])
        fine_bd = sb("fine_bd", [P, KC, NM, HH, HD])
        coarse_bd = sb("coarse_bd", [P, KC, P + (NM + 1) * HH])
        alive = sb("alive", [P, NM + 1])
        x_in = sb("x_in", [P, NT, H])
        xT = [sb(f"xT{i}", [P, KC, SEQ], F32R) for i in range(2)]
        sqT = sb("sqT", [P, KC, SEQ])
        skT = sb("skT", [P, KC, SEQ])
        v1 = sb("v1", [P, NT, NH, HE])
        stats = sb("stats", [P, NT, 6])
        meanvar = sb("meanvar", [P, NT, 2])
        rstd = sb("rstd", [P, NT])
        qsum = sb("qsum", [P, KC, NS])
        qtot = sb("qtot", [P, KC])
        qmean = sb("qmean", [P, KC, P])
        logit = sb("logit", [P, NT, E])
        r_a = sb("r_a", [P, NT, E])
        r_b = sb("r_b", [P, NT, E])
        r_c = sb("r_c", [P, NT, E])
        r_h1 = sb("r_h1", [P, NT, E], BF16)
        r_h2 = sb("r_h2", [P, NT, E], BF16)
        r_exp = sb("r_exp", [P, NT, E])
        r_sel = sb("r_sel", [P, NT, E])
        r_m = sb("r_m", [P, 6, NT])
        cw3 = sb("cw3", [P, NT, CW3])
        cwT = sb("cwT", [CW3, SEQ], BF16)
        mw = sb("mw", [P, KC, NM, HH])
        mw_m = sb("mw_m", [P, 2, KC, HH])
        qm = sb("qm", [P, KC, 2, P])
        probs = sb("probs", [P, 4, 4, P])
        elu_e = probs[:, 0:2, :, :].rearrange("p k h i -> p k (h i)")
        elu_r = probs[:, 2:4, :, :].rearrange("p k h i -> p k (h i)")
        k_tok = sb("k_tok", [P, H])
        state = sb("state", [P, KC, HH * HE])
        kvm = sb("kvm", [P, KC, HH * HE])
        den = sb("den", [P, NH])
        rn = sb("rn", [P, KC, NM + 1, HH])
        local = sb("local", [P, H])
        coarse = sb("coarse", [P, H])
        coarseT = sb("coarseT", [P, KC, P])
        hid = sb("hid", [G1, P])
        e_t = sb("e_t", [P, 3])
        coef = sb("coef", [P, KC, NM, HH])
        coef_c = sb("coef_c", [P, NH])
        rest = sb("rest", [P, H])
        prod = sb("prod", [P, KC, NM, P])
        part = sb("part", [P, KC, 2, P])
        att = sb("att", [P, H])
        attT = sb("attT", [P, KC, ST])
        silu = sb("silu", [P, ST])
        gu = sb("gu", [P, ST])
        hf = sb("hf", [P, ST])
        hT = [sb(f"hT{i}", [P, ST], F32R) for i in range(2)]
        res = sb("res", [P, KC, ST])

        ring = [ctx.enter_context(nc.psum_tensor(f"ring{i}", [P, 512], F32)) for i in range(NR)]
        ps_g = ctx.enter_context(nc.psum_tensor("ps_g", [P, ST], F32))
        ps_u = ctx.enter_context(nc.psum_tensor("ps_u", [P, ST], F32))
        ps_c = ctx.enter_context(nc.psum_tensor("ps_c", [P, ST], F32))
        ps_y = [ctx.enter_context(nc.psum_tensor(f"ps_y{i}", [P, ST], F32)) for i in range(KC)]

        s_const, s_small = sem("s_const"), sem("s_small")
        s_stage = [sem(f"s_stage{i}") for i in range(2)]
        s_wh, s_wl, s_pro = sem("s_wh"), sem("s_wl"), sem("s_pro")
        s_gexp, s_nsum, s_psel = sem("s_gexp"), sem("s_nsum"), sem("s_psel")
        s_ones, s_half, s_selected = sem("s_ones"), sem("s_half"), sem("s_selected")
        s_dve, s_pool, s_pdve = sem("s_dve"), sem("s_pool"), sem("s_pdve")
        s_x, s_res, s_out = sem("s_x"), sem("s_res"), sem("s_out")
        s_mv, s_rstd, s_xn = sem("s_mv"), sem("s_rstd"), sem("s_xn")
        ready = {name: sem(f"s_ps_{name}") for name in
                 ("xT", "q", "v", "mean", "k", "cwT", "norms", "keys", "scores", "outT", "coarseT",
                  "hidden", "local", "gate", "state", "fine")}
        s_xh, s_xl = sem("s_xh"), sem("s_xl")
        s_elu, s_sq, s_sk = sem("s_elu"), sem("s_sq"), sem("s_sk")
        s_v, s_rx, s_rexp, s_cw3, s_cwT = sem("s_v"), sem("s_rx"), sem("s_rexp"), sem("s_cw3"), sem("s_cwT")
        s_qmean, s_mean, s_mx, s_mexp = sem("s_qmean"), sem("s_mean"), sem("s_mx"), sem("s_mexp")
        s_qm, s_ktok, s_probs, s_kvm, s_state, s_local = (
            sem("s_qm"), sem("s_ktok"), sem("s_probs"), sem("s_kvm"), sem("s_state"), sem("s_local"))
        s_coarse, s_coarseT, s_hid, s_e, s_prod = (
            sem("s_coarse"), sem("s_coarseT"), sem("s_hid"), sem("s_e"), sem("s_prod"))
        s_rest, s_att, s_attT = sem("s_rest"), sem("s_att"), sem("s_attT")
        s_g, s_u, s_c, s_y = sem("s_g"), sem("s_u"), sem("s_c"), sem("s_y")
        s_silu, s_gu, s_hf, s_hh, s_hl, s_down = (
            sem("s_silu"), sem("s_gu"), sem("s_hf"), sem("s_hh"), sem("s_hl"), sem("s_down"))
        s_sum = sem("s_sum")

        x_tok = d["x_tok"].rearrange("(b t p) c -> b p t c", t=NT, p=P)
        x_t = d["x_t"].rearrange("(k p) n -> p k n", p=P)
        out_v = out_t.rearrange("(k p) n -> p k n", p=P)

        stage = [sqT[:, :, :].rearrange("p k n -> p (k n)"), skT[:, :, :].rearrange("p k n -> p (k n)")]
        loads = []
        for name, w, width in (("wq_t", wq, H), ("wk_t", wk, H), ("wvg_t", wv, H + E)):
            loads.append((d[name].rearrange("(k p) n -> p k n", p=P), w, None, KC * width, width))
        for kc in range(KC):
            for name, w in (("wg_t", wg), ("wu_t", wu)):
                loads.append((d[name][kc * P:(kc + 1) * P, :], w, kc, FR, None))
        for lo, hi in ((0, 7), (7, NF - 1)):
            loads.append((d["wd_t"][lo * P:hi * P, :].rearrange("(f p) n -> p f n", p=P),
                          wd, (lo, hi), (hi - lo) * H, H))
        loads.append((d["wd_t"][(NF - 1) * P:FR, :], wd, "last", H, None))

        def staged(n):
            _, w, where, size, inner = loads[n]
            st = stage[n % 2][:, 0:size]
            if where == "last":
                rows = FROWS[-1]
                return st[0:rows, :], w[0][0:rows, NF - 1, :], w[1][0:rows, NF - 1, :]
            if where is None:
                return (st.rearrange("p (k n) -> p k n", n=inner), w[0][:, :, :], w[1][:, :, :])
            if isinstance(where, tuple):
                a, z = where
                return (st.rearrange("p (k n) -> p k n", n=inner), w[0][:, a:z, :], w[1][:, a:z, :])
            return st, w[0][:, where, :], w[1][:, where, :]

        mem_c = prod[:, :, 0, 0:NM * HD]
        nrm_c = part[:, :, 0, 0:NM]
        nsum = part[:, 0, 1, 0:NM + 1]
        csum = part[:, 1, 1, 0:HD]
        csum2 = part[:, 1, 1, HD:2 * HD]
        nc_sum = part[:, 0, 1, 16:16 + KC]
        sel_f = x_in[0:CW3, :, :].rearrange("p t n -> p (t n)")[:, 0:NF * P]

        blocks = NS * NF
        per_batch = [
            (s_x, 16), (s_res, 16 * NS), (s_out, 16 * NS), (s_sum, NS), (s_y, NS),
            (s_mv, 1), (s_rstd, 1), (s_xn, NT), (s_xh, NS * KC), (s_xl, NS * KC),
            (s_elu, 2 * NS * KC), (s_sq, NS * KC), (s_sk, NS * KC), (s_qmean, 1), (s_mean, 1), (s_mx, 1),
            (s_mexp, 1), (s_v, NT), (s_rx, 1), (s_rexp, 1), (s_cw3, 1), (s_cwT, NS), (s_qm, NT),
            (s_ktok, NT), (s_probs, 4 * NT), (s_kvm, NT - 1), (s_state, NT), (s_local, NT), (s_coarse, NT),
            (s_coarseT, NT), (s_hid, NT), (s_e, NT), (s_prod, KC * NT), (s_rest, NT), (s_att, NT),
            (s_attT, NT), (s_g, blocks), (s_u, blocks), (s_c, blocks), (s_silu, blocks), (s_gu, blocks),
            (s_hf, blocks), (s_hh, blocks), (s_hl, blocks), (s_down, blocks),
            (s_dve, DVE_LINKS), (s_pool, POOL_LINKS)]
        per_batch += [(ready[name], n) for name, n in (
            ("xT", NS * KC), ("q", NS * KC), ("v", NT), ("mean", 1), ("k", NS * KC), ("cwT", NS),
            ("norms", NT), ("keys", NT), ("scores", 4 * NT), ("outT", NT), ("coarseT", NT),
            ("hidden", NT), ("local", NT), ("gate", NT), ("state", NT - 1), ("fine", KC * NT))]

        last_reader = {
            "xT": (s_xl, NS * KC), "q": (s_elu, 2 * NS * KC), "k": (s_elu, 2 * NS * KC), "v": (s_v, NT),
            "mean": (s_mean, 1), "cwT": (s_cwT, NS), "norms": (s_coarse, NT), "keys": (s_ktok, NT),
            "scores": (s_probs, 4 * NT), "outT": (s_attT, NT), "coarseT": (s_coarseT, NT),
            "hidden": (s_hid, NT), "local": (s_local, NT), "gate": (s_e, NT), "state": (s_kvm, NT - 1),
            "fine": (s_prod, KC * NT)}

        def reads_until(name, n, j):
            if name in ("xT", "q"):
                return n * KC + j + 1
            if name == "k":
                return NS * KC + n * KC + j + 1
            return {"scores": 4 * n + j, "fine": KC * n + j}.get(name, n) + 1

        def bank(*use):
            return ring[TURN[use] % NR]

        def use_bank(pe, b, *use):
            n = TURN[use]
            if n >= NR:
                before = RING[n - NR]
                signal, times = last_reader[before[0]]
                pe.wait_ge(signal, b * times + reads_until(*before))
            else:
                before = [u for i, u in enumerate(RING) if i % NR == n][-1]
                signal, times = last_reader[before[0]]
                pe.wait_ge(signal, b * times)
            return ring[n % NR]

        block = ctx.enter_context(nc.Block())

        @block.sync
        def _(sp):
            for name, t in (("ident", ident), ("causal", causal), ("parity", parity),
                            ("same_head", same_head), ("rank_e", rank_e)):
                sp.dma_start(t[:, :], d[name]).then_inc(s_const, 16)
            sp.dma_start(wo[:, :, :], d["wo_t"].rearrange("(k p) n -> p k n", p=P)).then_inc(s_small, 16)
            sp.dma_start(w1[:, :, :], d["eg_w1_t"].rearrange("(k p) n -> p k n", p=P)).then_inc(s_small, 16)
            sp.dma_start(b1[:, :], d["eg_b1"]).then_inc(s_small, 16)
            sp.dma_start(w2[:, :], d["eg_w2_t"]).then_inc(s_small, 16)
            sp.dma_start(b2[:, :], d["eg_b2"]).then_inc(s_small, 16)
            sp.dma_start(gate[:, :], d["memory_gate"]).then_inc(s_small, 16)
            sp.dma_start(mem_c, d["mem"].rearrange("(k p) n -> p k n", p=P)).then_inc(s_small, 16)
            sp.dma_start(nrm_c, d["norms"].rearrange("(k p) n -> p k n", p=P)).then_inc(s_small, 16)
            sp.dma_start(sel_f, d["select"]).then_inc(s_psel, 16)
            for n in range(len(loads)):
                if n >= 2:
                    sp.wait_ge(s_wl, n - 1)
                st, _, _ = staged(n)
                sp.dma_start(st, loads[n][0]).then_inc(s_stage[n % 2], 16)
            sp.wait_ge(s_selected, 1)
            with sp.Fori(1, B + 1) as b:
                sp.wait_ge(ready["xT"], b * NS * KC)
                sp.dma_start(x_in[:, :, :], x_tok[bass.ds(b - 1, 1), :, :, :].rearrange("b p t c -> p (b t) c")
                             ).then_inc(s_x, 16)
                for s in range(NS):
                    sp.wait_ge(s_out, b * 16 * NS + 16 * s)
                    sp.dma_start(res[:, :, :], x_t[:, :, bass.ds((b - 1) * SEQ + s * ST, ST)]).then_inc(s_res, 16)
                    sp.wait_ge(s_sum, b * NS + s + 1)
                    sp.dma_start(out_v[:, :, bass.ds((b - 1) * SEQ + s * ST, ST)], res[:, :, :]).then_inc(s_out, 16)
            sp.wait_ge(s_out, (B + 1) * NS * 16)

        @block.tensor
        def _(pe):
            pe.wait_ge(s_ones, 1)
            pe.wait_ge(s_small, 8 * 16)
            for m in range(KC):
                mm = pe.matmul(ps_c[:, 0:NM], ones[:, :], nrm_c[:, m, :], start=(m == 0), stop=(m == KC - 1))
            mm.then_inc(s_nsum, 1)
            pe.wait_ge(s_pro, 1)
            pe.wait_ge(s_selected, 1)
            pe.wait_ge(s_const, 5 * 16)
            pe.wait_ge(s_wh, len(loads))
            pe.wait_ge(s_wl, len(loads))

            def three(out, a, b_, start, stop):
                pe.matmul(out, a[0], b_[0], start=start, stop=False)
                pe.matmul(out, a[0], b_[1], start=False, stop=False)
                return pe.matmul(out, a[1], b_[0], start=False, stop=stop)

            with pe.Fori(1, B + 1) as b:
                for s in range(NS):
                    pe.wait_ge(s_xn, b * NT + (s + 1) * TS)
                    for kc in range(KC):
                        ps = use_bank(pe, b, "xT", s, kc)
                        for j in range(TS):
                            mm = pe.transpose(ps[:, j * P:(j + 1) * P],
                                              x_in[:, s * TS + j, kc * P:(kc + 1) * P], ident[:, :])
                        mm.then_inc(ready["xT"], 1)

                def project(name, w, s, m):
                    ps = use_bank(pe, b, name, s, m)
                    for kc in range(KC):
                        mm = three(ps[:, :], [w[i][:, kc, m * P:(m + 1) * P] for i in range(2)],
                                   [xT[i][:, kc, s * ST:(s + 1) * ST] for i in range(2)],
                                   kc == 0, kc == KC - 1)
                    mm.then_inc(ready[name], 1)

                for s in range(NS):
                    pe.wait_ge(s_xl, b * NS * KC + (s + 1) * KC)
                    for m in range(KC):
                        project("q", wq, s, m)
                for t in range(NT):
                    ps = use_bank(pe, b, "v", t, 0)
                    for kc in range(KC):
                        mm = three(ps[:, 0:H + E], [xT[i][:, kc, t * P:(t + 1) * P] for i in range(2)],
                                   [wv[i][:, kc, :] for i in range(2)], kc == 0, kc == KC - 1)
                    mm.then_inc(ready["v"], 1)
                ps = use_bank(pe, b, "mean", 0, 0)
                pe.wait_ge(s_qmean, b + 1)
                for m in range(KC):
                    mm = pe.matmul(ps[:, m * NM * HH:(m + 1) * NM * HH], qmean[:, m, :],
                                   coarse_bd[:, m, P:P + NM * HH], start=True, stop=True)
                mm.then_inc(ready["mean"], 1)
                for s in range(NS):
                    for m in range(KC):
                        project("k", wk, s, m)
                pe.wait_ge(s_cw3, b + 1)
                for s in range(NS):
                    ps = use_bank(pe, b, "cwT", s, 0)
                    for j in range(TS):
                        mm = pe.transpose(ps[0:CW3, j * P:(j + 1) * P], cw3[:, s * TS + j, :], ident[:, :])
                    mm.then_inc(ready["cwT"], 1)
                pe.wait_ge(s_cwT, b * NS + NS)
                pe.wait_ge(s_sk, b * NS * KC + NS * KC)

                for what, n, j in ORDER:
                    t = n
                    tok = slice(t * P, (t + 1) * P)
                    if what == "ffn":
                        s, f, part_ = FFN[n]
                        k = s * NF + f
                        rows = FROWS[f] if f < NF else 0
                        sup = slice(s * ST, (s + 1) * ST)
                        if part_ == "gate":
                            pe.wait_ge(s_hf, b * NS * NF + k)
                            pe.matmul(ps_c[0:rows, :], sel[:, f * P:f * P + rows], cwT[:, sup],
                                      start=True, stop=True).then_inc(s_c, 1)
                            pe.wait_ge(s_silu, b * NS * NF + k)
                            for kc in range(KC):
                                mm = three(ps_g[0:rows, :], [wg[i][:, kc, f * P:f * P + rows] for i in range(2)],
                                           [xT[i][:, kc, sup] for i in range(2)], kc == 0, kc == KC - 1)
                            mm.then_inc(s_g, 1)
                        elif part_ == "up":
                            pe.wait_ge(s_gu, b * NS * NF + k)
                            for kc in range(KC):
                                mm = three(ps_u[0:rows, :], [wu[i][:, kc, f * P:f * P + rows] for i in range(2)],
                                           [xT[i][:, kc, sup] for i in range(2)], kc == 0, kc == KC - 1)
                            mm.then_inc(s_u, 1)
                        elif part_ == "down":
                            if f == 0:
                                continue
                            g = f - 1
                            if g == 0:
                                pe.wait_ge(s_sum, b * NS + s)
                            pe.wait_ge(s_hl, b * NS * NF + k)
                            pe.wait_ge(s_hh, b * NS * NF + k)
                            for m in range(KC):
                                mm = three(ps_y[m][:, :],
                                           [wd[i][0:FROWS[g], g, m * P:(m + 1) * P] for i in range(2)],
                                           [hT[i][0:FROWS[g], :] for i in range(2)], g == 0, False)
                            mm.then_inc(s_down, 1)
                        else:
                            pe.wait_ge(s_attT, b * NT + (s + 1) * TS)
                            for m in range(KC):
                                for kc in range(KC):
                                    mm = pe.matmul(ps_y[m][:, :], wo[:, kc, m * P:(m + 1) * P], attT[:, kc, :],
                                                   start=False, stop=(kc == KC - 1))
                            mm.then_inc(s_y, 1)
                        continue
                    ps = use_bank(pe, b, what, n, j)
                    if what == "norms":
                        for m in range(KC):
                            w_ = P + (NM + 1) * HH
                            mm = pe.matmul(ps[:, m * w_:(m + 1) * w_], sqT[:, m, tok], coarse_bd[:, m, :],
                                           start=True, stop=True)
                    elif what == "keys":
                        for m in range(KC):
                            mm = pe.transpose(ps[:, m * P:(m + 1) * P], skT[:, m, tok], ident[:, :])
                    elif what == "scores":
                        pe.wait_ge(s_qm, b * NT + t + 1)
                        rows = slice(32 * j, 32 * j + 32)
                        for m in range(KC):
                            mm = pe.matmul(ps[:, 2 * m * P:2 * (m + 1) * P], skT[rows, m, tok],
                                           qm[rows, m, :, :], start=True, stop=True)
                    elif what == "outT":
                        pe.wait_ge(s_att, b * NT + t + 1)
                        for m in range(KC):
                            mm = pe.transpose(ps[:, m * P:(m + 1) * P], att[:, m * P:(m + 1) * P], ident[:, :])
                    elif what == "coarseT":
                        pe.wait_ge(s_coarse, b * NT + t + 1)
                        for m in range(KC):
                            mm = pe.transpose(ps[:, m * P:(m + 1) * P], coarse[:, m * P:(m + 1) * P], ident[:, :])
                    elif what == "hidden":
                        pe.wait_ge(s_coarseT, b * NT + t + 1)
                        for m in range(KC):
                            mm = pe.matmul(ps[0:G1, 0:P], w1[:, m, :], coarseT[:, m, :],
                                           start=(m == 0), stop=(m == KC - 1))
                    elif what == "local":
                        pe.wait_ge(s_state, b * NT + t + 1)
                        for m in range(KC):
                            pe.matmul(ps[:, m * HH * HE:(m + 1) * HH * HE], sqT[:, m, tok], state[:, m, :],
                                      start=(m == 0), stop=False)
                        for g in range(4):
                            pe.wait_ge(s_probs, b * NT * 4 + t * 4 + g + 1)
                            for i in range(4):
                                h = (i // 2) * HH + 2 * g + i % 2
                                mm = pe.matmul(ps[:, h * HE:(h + 1) * HE], probs[:, g, i, :],
                                               v1[:, t, h, :], start=False, stop=(g == 3 and i == 3))
                    elif what == "gate":
                        pe.wait_ge(s_hid, b * NT + t + 1)
                        mm = pe.matmul(ps[:, 0:1], hid[:, :], w2[:, :], start=True, stop=True)
                    elif what == "state":
                        pe.wait_ge(s_ktok, b * NT + t + 1)
                        for m in range(KC):
                            mm = pe.matmul(ps[:, m * HH * HE:(m + 1) * HH * HE], k_tok[:, m * P:(m + 1) * P],
                                           v1[:, t, m * HH:(m + 1) * HH, :], start=True, stop=True)
                    elif what == "fine":
                        mm = pe.matmul(ps[:, :], sqT[:, j, tok],
                                       fine_bd[:, j, :, :, :], start=True, stop=True)
                    mm.then_inc(ready[what], 1)

        @block.scalar
        def _(act):
            act.wait_ge(s_small, 8 * 16)
            act.activation(keep[:, :], gate[:, :], ACT.Exp, scale=-1.0).then_inc(s_gexp, 1)
            for n in range(len(loads)):
                act.wait_ge(s_stage[n % 2], 16 * (n // 2 + 1))
                st, hi, _ = staged(n)
                act.activation(hi, st, ACT.Copy).then_inc(s_wh, 1)
            act.wait_ge(s_wl, len(loads))

            with act.Fori(1, B + 1) as b:
                def elu(name, s, m):
                    ps = bank(name, s, m)
                    k = s * KC + m
                    act.wait_ge(ready[name], b * NS * KC + k + 1)
                    n = k + (name == "k") * NS * KC
                    if n < 2:
                        act.wait_ge(s_sk, b * NS * KC)
                    elif n < NS * KC + 2:
                        act.wait_ge(s_sq, b * NS * KC + n - 1)
                    else:
                        act.wait_ge(s_sk, b * NS * KC + n - NS * KC - 1)
                    act.activation(elu_e[:, n % 2, :], ps[:, :], ACT.Exp)
                    act.activation(elu_r[:, n % 2, :], ps[:, :], ACT.Relu).then_inc(s_elu, 1)

                for s in range(NS):
                    for kc in range(KC):
                        n = s * KC + kc
                        act.wait_ge(ready["xT"], b * NS * KC + n + 1)
                        act.activation(xT[0][:, kc, s * ST:(s + 1) * ST], bank("xT", s, kc)[:, :],
                                       ACT.Copy).then_inc(s_xh, 1)
                for s in range(NS):
                    for m in range(KC):
                        elu("q", s, m)
                for t in range(NT):
                    act.wait_ge(ready["v"], b * NT + t + 1)
                    ps = bank("v", t, 0)
                    act.activation(v1[:, t, :, 0:HD], ps[:, 0:H].rearrange("p (h e) -> p h e", e=HD), ACT.Copy)
                    act.activation(logit[:, t, :], ps[:, H:H + E], ACT.Copy).then_inc(s_v, 1)
                act.wait_ge(s_mx, b + 1)
                act.activation(mw[:, :, :, :], mw[:, :, :, :], ACT.Exp).then_inc(s_mexp, 1)
                act.wait_ge(s_rx, b + 1)
                act.activation(r_exp[:, :, :], r_a[:, :, :], ACT.Exp).then_inc(s_rexp, 1)
                for s in range(NS):
                    for m in range(KC):
                        elu("k", s, m)
                for s in range(NS):
                    act.wait_ge(ready["cwT"], b * NS + s + 1)
                    act.activation(cwT[:, s * ST:(s + 1) * ST], bank("cwT", s, 0)[0:CW3, :],
                                   ACT.Copy).then_inc(s_cwT, 1)

                for what, n, j in ORDER:
                    t = n
                    if what == "ffn":
                        s, f, part_ = FFN[n]
                        k = s * NF + f
                        if part_ == "gate":
                            rows = FROWS[f]
                            act.wait_ge(s_g, b * NS * NF + k + 1)
                            act.wait_ge(s_gu, b * NS * NF + k)
                            act.activation(silu[0:rows, :], ps_g[0:rows, :], ACT.Silu).then_inc(s_silu, 1)
                        elif part_ == "down" and f < NF:
                            rows = FROWS[f]
                            act.wait_ge(s_hf, b * NS * NF + k + 1)
                            act.wait_ge(s_down, b * NS * NF + k)
                            act.activation(hT[0][0:rows, :], hf[0:rows, :], ACT.Copy).then_inc(s_hh, 1)
                    elif what == "keys":
                        act.wait_ge(ready["keys"], b * NT + t + 1)
                        act.wait_ge(ready["state"], b * (NT - 1) + t)
                        act.activation(k_tok[:, :], bank("keys", t, 0)[:, 0:H], ACT.Copy).then_inc(s_ktok, 1)
                    elif what == "outT":
                        act.wait_ge(ready["outT"], b * NT + t + 1)
                        if t % TS == 0:
                            act.wait_ge(s_y, b * NS + t // TS)
                        act.activation(attT[:, :, (t % TS) * P:(t % TS + 1) * P],
                                       bank("outT", t, 0)[:, 0:H].rearrange("p (k n) -> p k n", k=KC),
                                       ACT.Copy).then_inc(s_attT, 1)
                    elif what == "coarseT":
                        act.wait_ge(ready["coarseT"], b * NT + t + 1)
                        act.wait_ge(ready["hidden"], b * NT + t)
                        act.activation(coarseT[:, :, :],
                                       bank("coarseT", t, 0)[:, 0:H].rearrange("p (k n) -> p k n", k=KC),
                                       ACT.Copy).then_inc(s_coarseT, 1)
                    elif what == "hidden":
                        act.wait_ge(ready["hidden"], b * NT + t + 1)
                        act.wait_ge(ready["gate"], b * NT + t)
                        act.activation(hid[:, :], bank("hidden", t, 0)[0:G1, 0:P], ACT.Relu,
                                       bias=b1[:, 0:1]).then_inc(s_hid, 1)
                    elif what == "gate":
                        act.wait_ge(ready["gate"], b * NT + t + 1)
                        act.wait_ge(s_rest, b * NT + t)
                        act.activation(e_t[:, 0:1], bank("gate", t, 0)[:, 0:1], ACT.Tanh,
                                       bias=b2[:, 0:1], scale=0.5).then_inc(s_e, 1)

        @block.vector
        def _(dve):
            links = [0, s_pdve, 0]

            def link(ins):
                links[0] += 1
                ins.then_inc(links[1], 1)
                dve.wait_ge(links[1], links[2] + links[0])

            dve.memset(ones[:, :], 1.0).then_inc(s_ones, 1)
            dve.memset(ln_eps[:, :], LN_EPS)
            dve.memset(half_neg[:, :], -0.5).then_inc(s_half, 1)
            link(dve.memset(v1[:, :, :, HD:HE], 1.0))
            link(dve.memset(cw3[:, :, CW3 - 1:CW3], 1.0))
            dve.wait_ge(s_const, 5 * 16)
            dve.wait_ge(s_small, 8 * 16)
            link(dve.tensor_scalar(b2[:, :], b2[:, :], 0.5, None, ALU.mult))
            dve.wait_ge(s_gexp, 1)
            link(dve.tensor_scalar(den[:, :], keep[:, :], 1.0, None, ALU.add))
            link(dve.reciprocal(gate[:, :], den[:, :]))
            link(dve.tensor_scalar(keep[:, :], gate[:, :], -1.0, 1.0, ALU.mult, ALU.add))
            for m in range(KC):
                for i in range(NM):
                    dve.tensor_tensor(
                        fine_bd[:, m, i, :, :],
                        mem_c[:, m, i * HD:(i + 1) * HD].unsqueeze(1).broadcast_to([P, HH, HD]),
                        same_head[:, :].unsqueeze(2).broadcast_to([P, HH, HD]), ALU.mult)
                    link(dve.tensor_tensor(
                        coarse_bd[:, m, P + i * HH:P + (i + 1) * HH], same_head[:, :],
                        nrm_c[:, m, i:i + 1].broadcast_to([P, HH]), ALU.mult))
                link(dve.tensor_tensor(csum, mem_c[:, m, 0:HD], mem_c[:, m, HD:2 * HD], ALU.add))
                link(dve.tensor_tensor(csum2, csum, mem_c[:, m, 2 * HD:3 * HD], ALU.add))
                link(dve.tensor_tensor(csum, csum2, mem_c[:, m, 3 * HD:4 * HD], ALU.add))
                link(dve.tensor_tensor(
                    coarse_bd[:, m, 0:P].rearrange("p (h e) -> p h e", e=HD),
                    csum.unsqueeze(1).broadcast_to([P, HH, HD]),
                    same_head[:, :].unsqueeze(2).broadcast_to([P, HH, HD]), ALU.mult))
                link(dve.tensor_reduce(nc_sum[:, m:m + 1], nrm_c[:, m, :], AX.X, ALU.add))
                link(dve.tensor_scalar(coarse_bd[:, m, P + NM * HH:P + (NM + 1) * HH], same_head[:, :],
                                       nc_sum[:, m:m + 1], None, ALU.mult))
            dve.wait_ge(s_nsum, 1)
            link(dve.tensor_copy(nsum[:, 0:NM], ps_c[:, 0:NM]))
            link(dve.tensor_reduce(nsum[:, NM:NM + 1], nsum[:, 0:NM], AX.X, ALU.add))
            dve.tensor_scalar(alive[:, :], nsum, EPS, None, ALU.is_ge).then_inc(s_pro, 1)
            dve.wait_ge(s_psel, 16)
            dve.tensor_copy(sel[:, :], sel_f).then_inc(s_selected, 1)
            for n in range(len(loads)):
                dve.wait_ge(s_wh, n + 1)
                st, hi, lo = staged(n)
                dve.tensor_tensor(lo, st, hi.bitcast(F32), ALU.subtract).then_inc(s_wl, 1)


            with dve.Fori(1, B + 1) as b:
                links[:] = [0, s_dve, b * DVE_LINKS]
                dve.wait_ge(s_x, b * 16 + 16)
                for t in range(NT):
                    ins = dve.bn_stats(stats[:, t, :], x_in[:, t, :])
                link(ins)
                dve.memset(state[:, :, :], 0.0).then_inc(s_state, 1)
                for t in range(NT):
                    ins = dve.bn_aggr(meanvar[:, t, :], stats[:, t, :])
                ins.then_inc(s_mv, 1)
                dve.wait_ge(s_rstd, b + 1)
                for t in range(NT):
                    dve.tensor_scalar(x_in[:, t, :], x_in[:, t, :], meanvar[:, t, 0:1], rstd[:, t:t + 1],
                                      ALU.subtract, ALU.mult).then_inc(s_xn, 1)
                for s in range(NS):
                    for kc in range(KC):
                        sup = slice(s * ST, (s + 1) * ST)
                        dve.wait_ge(s_xh, b * NS * KC + s * KC + kc + 1)
                        dve.tensor_tensor(xT[1][:, kc, sup], bank("xT", s, kc)[:, :],
                                          xT[0][:, kc, sup].bitcast(F32), ALU.subtract).then_inc(s_xl, 1)
                for s in range(NS):
                    for m in range(KC):
                        k = s * KC + m
                        dve.wait_ge(s_elu, b * 2 * NS * KC + k + 1)
                        dve.scalar_tensor_tensor(sqT[:, m, s * ST:(s + 1) * ST], elu_e[:, k % 2, :], 1.0,
                                                 elu_r[:, k % 2, :], ALU.min, ALU.add,
                                                 accum_out=qsum[:, m, s:s + 1]).then_inc(s_sq, 1)
                dve.wait_ge(s_sq, b * NS * KC + NS * KC)
                link(dve.tensor_tensor(qtot[:, :], qsum[:, :, 0], qsum[:, :, 1], ALU.add))
                for m in range(KC):
                    ins = dve.tensor_scalar(qmean[:, m, :], ones[:, :], qtot[:, m:m + 1], 1.0 / SEQ,
                                            ALU.mult, ALU.mult)
                ins.then_inc(s_qmean, 1)

                mw_by_memory = mw[:, :, :, :].rearrange("p k n h -> p k h n")
                dve.wait_ge(ready["mean"], b + 1)
                dve.tensor_copy(mw[:, :, :, :].rearrange("p k n h -> p (k n h)"),
                                bank("mean", 0, 0)[:, 0:KC * NM * HH]).then_inc(s_mean, 1)
                dve.wait_ge(s_mean, b + 1)
                link(dve.tensor_reduce(mw_m[:, 0, :, :], mw_by_memory, AX.X, ALU.max))
                dve.tensor_tensor(mw[:, :, :, :], mw[:, :, :, :],
                                  mw_m[:, 0, :, :].unsqueeze(2).broadcast_to([P, KC, NM, HH]),
                                  ALU.subtract).then_inc(s_mx, 1)

                def over_experts(x):
                    return x.unsqueeze(2).broadcast_to([P, NT, E])

                by_rank = rank_e[:, :].unsqueeze(1).broadcast_to([P, NT, E])
                dve.wait_ge(s_v, b * NT + NT)
                link(dve.tensor_reduce(r_m[:, 0, :], logit[:, :, :], AX.X, ALU.max))
                dve.tensor_tensor(r_a[:, :, :], logit[:, :, :], over_experts(r_m[:, 0, :]),
                                  ALU.subtract).then_inc(s_rx, 1)
                link(dve.tensor_tensor(r_b[:, :, :], logit[:, :, :], over_experts(r_m[:, 0, :]), ALU.is_equal))
                link(dve.tensor_tensor(r_b[:, :, :], r_b[:, :, :], by_rank, ALU.mult))
                link(dve.tensor_reduce(r_m[:, 1, :], r_b[:, :, :], AX.X, ALU.max))
                link(dve.tensor_tensor(r_sel[:, :, :], r_b[:, :, :], over_experts(r_m[:, 1, :]), ALU.is_equal))
                link(dve.scalar_tensor_tensor(r_b[:, :, :], r_sel[:, :, :], -3e38, logit[:, :, :],
                                              ALU.mult, ALU.add))
                link(dve.tensor_reduce(r_m[:, 2, :], r_b[:, :, :], AX.X, ALU.max))
                link(dve.tensor_tensor(r_c[:, :, :], r_b[:, :, :], over_experts(r_m[:, 2, :]), ALU.is_equal))
                link(dve.tensor_tensor(r_c[:, :, :], r_c[:, :, :], by_rank, ALU.mult))
                link(dve.tensor_reduce(r_m[:, 3, :], r_c[:, :, :], AX.X, ALU.max))
                link(dve.tensor_tensor(r_c[:, :, :], r_c[:, :, :], over_experts(r_m[:, 3, :]), ALU.is_equal))
                link(dve.tensor_tensor(r_sel[:, :, :], r_sel[:, :, :], r_c[:, :, :], ALU.add))
                dve.wait_ge(s_rexp, b + 1)
                link(dve.tensor_tensor(r_a[:, :, :], r_sel[:, :, :], r_exp[:, :, :], ALU.mult))
                dve.tensor_reduce(r_m[:, 4, :], r_exp[:, :, :], AX.X, ALU.add)
                link(dve.tensor_reduce(r_m[:, 5, :], r_a[:, :, :], AX.X, ALU.add))
                link(dve.scalar_tensor_tensor(r_m[:, 0, :], r_m[:, 4, :], 1e-20, r_m[:, 5, :],
                                              ALU.mult, ALU.add))
                link(dve.reciprocal(r_m[:, 1, :], r_m[:, 0, :]))
                link(dve.tensor_tensor(r_b[:, :, :], r_a[:, :, :], over_experts(r_m[:, 1, :]), ALU.mult))
                link(dve.tensor_copy(r_h1[:, :, :], r_b[:, :, :]))
                dve.tensor_copy(cw3[:, :, 0:E], r_h1[:, :, :])
                link(dve.tensor_tensor(r_a[:, :, :], r_b[:, :, :], r_h1[:, :, :], ALU.subtract))
                link(dve.tensor_copy(r_h2[:, :, :], r_a[:, :, :]))
                dve.tensor_copy(cw3[:, :, E:2 * E], r_h2[:, :, :])
                dve.tensor_tensor(cw3[:, :, 2 * E:3 * E], r_a[:, :, :], r_h2[:, :, :],
                                  ALU.subtract).then_inc(s_cw3, 1)
                dve.wait_ge(s_mexp, b + 1)
                link(dve.tensor_reduce(mw_m[:, 0, :, :], mw_by_memory, AX.X, ALU.add))
                link(dve.reciprocal(mw_m[:, 1, :, :], mw_m[:, 0, :, :]))
                link(dve.tensor_tensor(mw_m[:, 0, :, :], mw_m[:, 1, :, :],
                                       gate[:, :].rearrange("p (k h) -> p k h", k=KC), ALU.mult))
                link(dve.tensor_tensor(mw[:, :, :, :], mw[:, :, :, :],
                                       mw_m[:, 0, :, :].unsqueeze(2).broadcast_to([P, KC, NM, HH]), ALU.mult))
                link(dve.tensor_tensor(mw[:, :, :, :], mw[:, :, :, :],
                                       alive[:, 0:NM].unsqueeze(1).unsqueeze(3).broadcast_to([P, KC, NM, HH]),
                                       ALU.mult))
                for s in range(NS):
                    for m in range(KC):
                        k = s * KC + m
                        dve.wait_ge(s_elu, b * 2 * NS * KC + NS * KC + k + 1)
                        dve.scalar_tensor_tensor(skT[:, m, s * ST:(s + 1) * ST], elu_e[:, k % 2, :], 1.0,
                                                 elu_r[:, k % 2, :], ALU.min, ALU.add).then_inc(s_sk, 1)

                for what, n, j in ORDER:
                    t = n
                    if what == "ffn":
                        s, f, part_ = FFN[n]
                        k = s * NF + f
                        if part_ == "up":
                            rows = FROWS[f]
                            dve.wait_ge(s_silu, b * NS * NF + k + 1)
                            dve.wait_ge(s_u, b * NS * NF + k + 1)
                            dve.tensor_tensor(gu[0:rows, :], ps_u[0:rows, :], silu[0:rows, :],
                                              ALU.mult).then_inc(s_gu, 1)
                            dve.wait_ge(s_gu, b * NS * NF + k + 1)
                            dve.wait_ge(s_c, b * NS * NF + k + 1)
                            dve.wait_ge(s_hl, b * NS * NF + k)
                            dve.tensor_tensor(hf[0:rows, :], ps_c[0:rows, :], gu[0:rows, :],
                                              ALU.mult).then_inc(s_hf, 1)
                        elif part_ == "out":
                            dve.wait_ge(s_y, b * NS + s + 1)
                            dve.wait_ge(s_res, b * 16 * NS + 16 * (s + 1))
                            dve.tensor_tensor(res[:, 0, :], ps_y[0][:, :], res[:, 0, :], ALU.add)
                            dve.tensor_tensor(res[:, 1, :], ps_y[1][:, :], res[:, 1, :],
                                              ALU.add).then_inc(s_sum, 1)
                        continue
                    if what in ("coarseT", "keys", "hidden", "outT"):
                        continue
                    ps = bank(what, n, j)
                    if what == "norms":
                        dve.wait_ge(ready["scores"], b * 4 * NT + 4 * t)
                        for par in range(2):
                            ins = dve.tensor_scalar(qm[:, :, par, :], sqT[:, :, t * P:(t + 1) * P],
                                                    parity[:, par:par + 1], None, ALU.mult)
                        ins.then_inc(s_qm, 1)
                        dve.wait_ge(ready["norms"], b * NT + t + 1)
                        both = ps[:, 0:KC * (P + (NM + 1) * HH)].rearrange("p (k w) -> p k w", k=KC)
                        link(dve.tensor_scalar(rn[:, :, :, :].rearrange("p k n h -> p k (n h)"),
                                               both[:, :, P:], EPS, None, ALU.max))
                        link(dve.reciprocal(rn[:, :, :, :], rn[:, :, :, :]))
                        link(dve.tensor_scalar(rn[:, :, NM, :], rn[:, :, NM, :], alive[:, NM:NM + 1],
                                               None, ALU.mult))
                        dve.wait_ge(ready["coarseT"], b * NT + t)
                        dve.tensor_tensor(coarse[:, :].rearrange("p (k h e) -> p k h e", k=KC, e=HD),
                                          both[:, :, 0:P].rearrange("p k (h e) -> p k h e", e=HD),
                                          rn[:, :, NM, :].unsqueeze(3).broadcast_to([P, KC, HH, HD]),
                                          ALU.mult).then_inc(s_coarse, 1)
                    elif what == "scores":
                        dve.wait_ge(ready["scores"], b * 4 * NT + 4 * t + j + 1)
                        dve.wait_ge(ready["local"], b * NT + t)
                        dve.tensor_tensor(probs[:, j, :, :], ps[:, :].rearrange("p (h i) -> p h i", i=P),
                                          causal[:, :].unsqueeze(1).broadcast_to([P, 4, P]),
                                          ALU.mult).then_inc(s_probs, 1)
                    elif what == "local":
                        heads = ps[:, 0:NH * HE].rearrange("p (h e) -> p h e", e=HE)
                        dve.wait_ge(ready["local"], b * NT + t + 1)
                        link(dve.tensor_scalar(den[:, :], heads[:, :, HD], EPS, None, ALU.max))
                        link(dve.reciprocal(den[:, :], den[:, :]))
                        link(dve.tensor_tensor(den[:, :], den[:, :], keep[:, :], ALU.mult))
                        dve.tensor_tensor(local[:, :].rearrange("p (h e) -> p h e", e=HD), heads[:, :, 0:HD],
                                          den[:, :].unsqueeze(2).broadcast_to([P, NH, HD]),
                                          ALU.mult).then_inc(s_local, 1)
                    elif what == "gate":
                        dve.wait_ge(s_e, b * NT + t + 1)
                        dve.tensor_scalar(e_t[:, 1:2], e_t[:, 0:1], 0.5, 0.5, ALU.mult, ALU.add)
                        link(dve.tensor_scalar(e_t[:, 2:3], e_t[:, 0:1], -0.5, 0.5, ALU.mult, ALU.add))
                        dve.scalar_tensor_tensor(coef[:, :, :, :].rearrange("p k n h -> p k (n h)"),
                                                 rn[:, :, 0:NM, :].rearrange("p k n h -> p k (n h)"),
                                                 e_t[:, 1:2], mw[:, :, :, :].rearrange("p k n h -> p k (n h)"),
                                                 ALU.mult, ALU.mult)
                        link(dve.tensor_scalar(coef_c[:, :], gate[:, :], e_t[:, 2:3], None, ALU.mult))
                        dve.wait_ge(s_att, b * NT + t)
                        link(dve.tensor_tensor(rest[:, :].rearrange("p (h e) -> p h e", e=HD),
                                               coarse[:, :].rearrange("p (h e) -> p h e", e=HD),
                                               coef_c[:, :].unsqueeze(2).broadcast_to([P, NH, HD]), ALU.mult))
                        dve.tensor_tensor(rest[:, :], rest[:, :], local[:, :], ALU.add).then_inc(s_rest, 1)
                    elif what == "state":
                        dve.wait_ge(ready["state"], b * (NT - 1) + t + 1)
                        dve.tensor_tensor(kvm[:, :, :].rearrange("p k (h e) -> p k h e", e=HE),
                                          ps[:, 0:KC * HH * HE].rearrange("p (k h e) -> p k h e", k=KC, e=HE),
                                          same_head[:, :].unsqueeze(1).unsqueeze(3)
                                          .broadcast_to([P, KC, HH, HE]), ALU.mult).then_inc(s_kvm, 1)
                        dve.wait_ge(s_kvm, b * (NT - 1) + t + 1)
                        dve.tensor_tensor(state[:, :, :], state[:, :, :], kvm[:, :, :],
                                          ALU.add).then_inc(s_state, 1)
                    elif what == "fine":
                        dve.wait_ge(ready["fine"], b * KC * NT + KC * t + j + 1)
                        if j == 0:
                            dve.wait_ge(s_att, b * NT + t)
                        dve.tensor_tensor(prod[:, j, :, :].rearrange("p n (h e) -> p (n h) e", e=HD),
                                          ps[:, :].rearrange("p (m e) -> p m e", e=HD),
                                          coef[:, j, :, :].rearrange("p n h -> p (n h)").unsqueeze(2)
                                          .broadcast_to([P, NM * HH, HD]), ALU.mult).then_inc(s_prod, 1)
                assert links[0] == DVE_LINKS, links[0]

        @block.gpsimd
        def _(pool):
            for signal, count in per_batch:
                pool.sem_inc(signal, count)
            pool.wait_ge(s_half, 1)
            with pool.Fori(1, B + 1) as b:
                links = [0]

                def link(ins):
                    links[0] += 1
                    ins.then_inc(s_pool, 1)
                    pool.wait_ge(s_pool, b * POOL_LINKS + links[0])

                pool.wait_ge(s_mv, b + 1)
                link(pool.tensor_tensor(varp[:, :], meanvar[:, :, 1], ln_eps[:, :], ALU.add))
                pool.tensor_tensor(rstd[:, :], varp[:, :], half_neg[:, :], ALU.pow).then_inc(s_rstd, 1)
                for what, n, j in ORDER:
                    t = n
                    if what == "ffn":
                        s, f, part_ = FFN[n]
                        k = s * NF + f
                        if part_ == "down" and f < NF:
                            rows = FROWS[f]
                            pool.wait_ge(s_hh, b * NS * NF + k + 1)
                            pool.tensor_tensor(hT[1][0:rows, :], hf[0:rows, :],
                                               hT[0][0:rows, :].bitcast(F32),
                                               ALU.subtract).then_inc(s_hl, 1)
                    elif what == "fine" and j == KC - 1:
                        pool.wait_ge(s_prod, b * KC * NT + KC * (t + 1))
                        link(pool.tensor_tensor(part[:, :, :, :], prod[:, :, 0:2, :], prod[:, :, 2:4, :], ALU.add))
                        pool.wait_ge(ready["outT"], b * NT + t)
                        link(pool.tensor_tensor(att[:, :].rearrange("p (k n) -> p k n", k=KC),
                                                part[:, :, 0, :], part[:, :, 1, :], ALU.add))
                        pool.tensor_tensor(att[:, :], att[:, :], rest[:, :], ALU.add).then_inc(s_att, 1)
                assert links[0] == POOL_LINKS, links[0]


def kernel(**inputs):
    import concourse.bacc as _bacc
    from concourse.bass_utils import run_bass_kernel_spmd as _run

    a = {k: np.asarray(v) for k, v in inputs.items()}
    x = a["L0_attn_hidden_states"].reshape(B * SEQ, H)
    part = np.arange(P)
    arrays = {
        "x_tok": x,
        "x_t": x.T,
        "wq_t": a["L0_attn_w_q"].T,
        "wk_t": a["L0_attn_w_k"].T,
        "wvg_t": np.concatenate([a["L0_attn_w_v"], a["L0_ffn_gate_weight"]]).T,
        "wo_t": a["L0_attn_w_o"].T,
        "eg_w1_t": a["L0_attn_eg_w1"].T,
        "eg_b1": a["L0_attn_eg_b1"].reshape(G1, 1),
        "eg_w2_t": a["L0_attn_eg_w2"].T,
        "eg_b2": np.broadcast_to(a["L0_attn_eg_b2"].reshape(1, 1), (P, 1)),
        "memory_gate": np.broadcast_to(a["L0_attn_memory_gate"].reshape(1, NH), (P, NH)),
        "mem": a["L0_attn_fine_memories"].transpose(1, 2, 0, 3).reshape(H, NM * HD),
        "norms": a["L0_attn_fine_memory_norms"].transpose(1, 2, 0).reshape(H, NM),
        "wg_t": np.concatenate([a["L0_ffn_w_gate"].reshape(E * F, H), a["L0_ffn_sw_gate"]]).T,
        "wu_t": np.concatenate([a["L0_ffn_w_up"].reshape(E * F, H), a["L0_ffn_sw_up"]]).T,
        "wd_t": np.concatenate([a["L0_ffn_w_down"].transpose(0, 2, 1).reshape(E * F, H),
                                a["L0_ffn_sw_down"].T]),
        "ident": np.eye(P, dtype=np.float32),
        "causal": np.triu(np.ones((P, P), np.float32)),
        "parity": np.stack([part // HD % 2 == 0, part // HD % 2 == 1], 1).astype(np.float32),
        "same_head": (part[:, None] // HD == np.arange(HH)[None, :]).astype(np.float32),
        "rank_e": np.broadcast_to(np.arange(E, 0, -1).astype(np.float32), (P, E)),
        "select": selector(),
    }
    nc = _bacc.Bacc("TRN2", target_bir_lowering=False, num_devices=1)
    arrays = {k: np.ascontiguousarray(v) for k, v in arrays.items()}
    d = {k: nc.dram_tensor("in_" + k, v.shape, mybir.dt.from_np(v.dtype), kind="ExternalInput").ap()
         for k, v in arrays.items()}
    out_t = nc.dram_tensor("out_t", (H, B * SEQ), F32, kind="ExternalOutput").ap()
    build(nc, d, out_t)
    r = _run(nc, [{"in_" + k: v for k, v in arrays.items()}], core_ids=[0])
    return r.results[0]["out_t"].T.reshape(B, SEQ, H)


def selector():
    row = np.arange(NF * P)
    expert = np.where(row < E * F, row // F, -1)
    s = (np.arange(3 * E)[:, None] % E == expert[None, :])
    return np.concatenate([s, (row >= E * F)[None, :]]).astype(np.float32)
```

```python
import numpy as np

import concourse.bass as bass
from concourse import mybir
from contextlib import ExitStack

F32 = mybir.dt.float32
F32R = mybir.dt.float32r
BF16 = mybir.dt.bfloat16
I32 = mybir.dt.int32
ALU = mybir.AluOpType
ACT = mybir.ActivationFunctionType
AX = mybir.AxisListType

P = 128
B, SEQ, H = 4, 1024, 256
T = B * SEQ
NTA = T // P
NT = SEQ // P
NS = 2
ST = SEQ // NS
TS = ST // P
KC = H // P
NH, HD, NM = 16, 16, 4
HH = NH // KC
HE = HD + 1
E, F, FS = 8, 176, 352
TOP = 2
FC = F // 2
G1 = H // 4
EPS = 1e-6
LN_EPS = 1e-5
WN = P + (NM + 1) * HH

SF = (P, P, FS - 2 * P)
SF_ORDER = (2, 0, 1)
NBLK = TOP * T // P + E - 1
UNROLL = 4
SLOTS = -(-(NBLK + 1) // UNROLL) * UNROLL
NI = SLOTS + 8

WUP = KC * E * 2 * F
WQKV = KC * 3 * H
W_PIECE = (WUP + WQKV) // B
D_PIECE = E * 2 * H // B


def places(nc, scope):
    def sb(name, shape, dt=F32):
        return scope.enter_context(nc.sbuf_tensor(name, shape, dt))

    def bank(name):
        return scope.enter_context(nc.psum_tensor(name, [P, 512], F32))

    def sem(name):
        return scope.enter_context(nc.semaphore(name))

    return sb, bank, sem


def three(pe, out, a, b, start, stop):
    pe.matmul(out, a[0], b[0], start=start, stop=False)
    pe.matmul(out, a[0], b[1], start=False, stop=False)
    return pe.matmul(out, a[1], b[0], start=False, stop=stop)


def chain(eng, done, before=0):
    links = [0]

    def link(ins):
        links[0] += 1
        ins.then_inc(done, 1)
        eng.wait_ge(done, before + links[0])

    return link, links


TOKEN_LINKS = 15


def tokens_phase(nc, d, c, w):
    with ExitStack() as scope:
        sb, bank, sem = places(nc, scope)
        x_in = [sb(f"x_in{u}", [P, NT, H]) for u in range(2)]
        xn = [sb(f"xn{u}", [P, NT, H]) for u in range(2)]
        xT = [sb(f"xT{i}", [P, KC, SEQ], F32R) for i in range(2)]
        sg = [sb(f"sg{i}", [P, KC, FS + E], F32R) for i in range(2)]
        su = [sb(f"su{i}", [P, KC, FS], F32R) for i in range(2)]
        sd = [sb(f"sd{i}", [P, len(SF), H], F32R) for i in range(2)]
        stage_w = sb("stage_w", [P, W_PIECE])
        stage_d = sb("stage_d", [FC, D_PIECE])
        silu = sb("silu1", [P, 2, ST])
        hf = sb("hf", [P, 2, ST])
        hT = [sb(f"hT{i}", [P, len(SF), ST], F32R) for i in range(2)]
        base_sb = sb("base_sb", [P, NS, TS, H])
        logitT = sb("logitT", [P, ST])
        stats = sb("stats", [P, NT, 6])
        meanvar = sb("meanvar", [P, NT, 2])
        tick, tick_p, tick_s = sb("tick", [P, 1]), sb("tick_p", [P, 1]), sb("tick_s1", [P, 1])
        ln_eps, half_neg, neg = sb("ln_eps", [P, NT]), sb("half_neg", [P, NT]), sb("neg", [P, NT])
        varp, rstd, shift = sb("varp", [P, NT]), sb("rstd", [P, NT]), sb("shift", [P, NT])
        logit = sb("logit", [P, NT, E])
        r_b, r_c = sb("r_b", [P, NT, E]), sb("r_c", [P, NT, E])
        r_s = sb("r_s", [P, TOP, NT, E])
        r_m = sb("r_m", [P, 4, NT])
        mask = sb("mask", [P, NT + 1, E], BF16)
        ones_bf, before_bf = sb("ones_bf", [P, P], BF16), sb("before_bf", [P, P], BF16)
        pos = sb("pos", [P, NT, E])
        slot_f = sb("slot_f", [P, TOP, NT])
        number = [sb(f"number{u}", [P, NT], I32) for u in range(2)]
        zeros = sb("zeros", [P, E * T // P], I32)
        slot_i = [sb(f"slot_i{u}", [P, TOP, NT], I32) for u in range(2)]

        count_i = sb("count_i", [P, E], I32)

        taken = {"x": 0, "w": 0}
        old = {"x": x_in[1][:, :, :].rearrange("p t n -> p (t n)"), "w": stage_w[:, :]}

        def carve(buffer, n, m=None):
            size = n * (m or 1)
            part = old[buffer][:, taken[buffer]:taken[buffer] + size]
            taken[buffer] += size
            return part if m is None else part.rearrange("p (n m) -> p n m", m=m)

        ge, oh, tmp = (carve("x", NI, E) for _ in range(3))
        count_f, last1 = carve("w", E), carve("w", 1)
        first = carve("w", E + 1)
        blk = carve("w", NI)
        blk_first, blk_e, start = (carve("w", NI) for _ in range(3))
        e_f, pack = carve("w", NI + 2), carve("w", NI // UNROLL)
        shift_e, moved_s = carve("w", E), carve("w", TOP * NTA)
        z = carve("w", 4, NTA)
        ex = carve("w", NTA, E)
        exs = silu[:, 0, 0:TOP * NTA * E].rearrange("p (k t e) -> p k t e", k=TOP, e=E)
        moved = hf[:, 0, 0:TOP * NTA * E].rearrange("p (t e) -> p t e", e=E)

        ps_a = [bank(f"t_a{i}") for i in range(2)]
        ps_g = [bank(f"t_g{i}") for i in range(2)]
        ps_u = [bank(f"t_u{i}") for i in range(2)]
        ps_y = [bank(f"t_y{i}") for i in range(2)]

        s_const, s_sw, s_swh, s_swl, s_pro = (
            sem("t_const"), sem("t_sw"), sem("t_swh"), sem("t_swl"), sem("t_pro"))
        s_stage, s_tick, s_zero, s_listed, s_neg = (
            sem("t_stage"), sem("t_tick"), sem("t_zero"), sem("t_listed"), sem("t_neg"))
        s_x, s_xst, s_sc = ([sem(f"t_{n}{u}") for u in range(2)] for n in ("x", "xst", "sc"))
        s_bst = [sem(f"t_bst{s}") for s in range(NS)]
        s_st, s_mv, s_rstd, s_xn = sem("t_st"), sem("t_mv"), sem("t_rstd"), sem("t_xn")
        s_xT, s_xh, s_xl = sem("t_xT"), sem("t_xh"), sem("t_xl")
        s_g, s_u, s_silu, s_gu, s_hh, s_hl, s_y, s_base = (
            sem("t_g"), sem("t_u"), sem("t_silu"), sem("t_gu"), sem("t_hh"), sem("t_hl"), sem("t_y"),
            sem("t_base"))
        s_lgT, s_lg, s_mask, s_pre, s_pos, s_slot = (
            sem("t_lgT"), sem("t_lg"), sem("t_mask"), sem("t_pre"), sem("t_pos"), sem("t_slot"))
        s_tab, s_exp = sem("t_tab"), sem("t_exp")
        s_wh, s_wl, s_dve, s_pool = sem("t_wh"), sem("t_wl"), sem("t_dve"), sem("t_pool")
        POOL_LINKS = 3

        NB = NS * len(SF)
        per_batch = [
            (s_stage, 32), (s_bst[0], 16), (s_bst[1], 16), (s_mv, 1),
            (s_rstd, 1), (s_xn, NT), (s_xT, NS * KC), (s_xh, NS * KC), (s_xl, NS * KC), (s_g, NB),
            (s_u, NB), (s_silu, NB), (s_gu, NB), (s_hh, NB), (s_hl, NB), (s_y, 2 * NS), (s_base, 2 * NS),
            (s_lgT, NS), (s_lg, NS), (s_mask, 1), (s_pre, 1), (s_pos, 1), (s_slot, 1), (s_wh, 2),
            (s_wl, 2), (s_st, 1), (s_tick, 1), (s_dve, TOKEN_LINKS), (s_pool, POOL_LINKS)]
        per_pass = [(s[u], n) for s, n in ((s_x, 16), (s_xst, 16)) for u in range(2)]

        flat = [xn[u][:, :, :].rearrange("p t n -> p (t n)") for u in range(2)]
        n_g, n_u = KC * (FS + E), KC * FS
        st_g = flat[0][:, 0:n_g].rearrange("p (k n) -> p k n", k=KC)
        st_u = flat[0][:, n_g:n_g + n_u].rearrange("p (k n) -> p k n", k=KC)
        st_d = flat[1][:, 0:len(SF) * H].rearrange("p (f n) -> p f n", f=len(SF))
        shared = [(st_g, [t[:, :, :] for t in sg]), (st_u, [t[:, :, :] for t in su]),
                  (st_d[:, 0:2, :], [t[:, 0:2, :] for t in sd]),
                  (st_d[0:SF[2], 2, :], [t[0:SF[2], 2, :] for t in sd])]

        x_tok = d["x_tok"].rearrange("(b t p) c -> b p t c", t=NT, p=P)
        xn_d = d["xn"].rearrange("(b t p) c -> b p t c", t=NT, p=P)
        base_d = d["base"].rearrange("(s t p) c -> s p t c", t=TS, p=P)

        block = scope.enter_context(nc.Block())

        @block.sync
        def _(sp):
            def tokens(u, index):
                sp.dma_start(x_in[u][:, :, :], x_tok[bass.ds(index, 1), :, :, :]
                             .rearrange("b p t c -> p (b t) c")).then_inc(s_x[u], 16)

            sp.wait_ge(s_x[0], 16)
            tokens(0, 0)
            sp.dma_start(st_g, d["sg_t"].rearrange("(k p) n -> p k n", p=P)).then_inc(s_sw, 16)
            sp.dma_start(st_u, d["su_t"].rearrange("(k p) n -> p k n", p=P)).then_inc(s_sw, 16)
            sp.dma_start(st_d[:, 0:2, :], d["sd_t"][0:2 * P, :].rearrange("(f p) n -> p f n", p=P)
                         ).then_inc(s_sw, 16)
            sp.dma_start(st_d[0:SF[2], 2, :], d["sd_t"][2 * P:FS, :]).then_inc(s_sw, 16)
            sp.wait_ge(s_zero, 1)
            sp.dma_start(d["lists"].rearrange("(p n) c -> p (n c)", p=P), zeros[:, :]).then_inc(s_listed, 16)
            with sp.Fori(0, B // 2) as it:
                for u in range(2):
                    b = it * 2 + (2 + u)
                    sp.wait_ge(s_base, b * 2 * NS)
                    tokens(1 - u, (b - 1) % B)
                    sp.wait_ge(s_wl, b * 2)
                    sp.dma_start(stage_w[:, :], d["w_all"][:, bass.ds((b - 2) * W_PIECE, W_PIECE)]
                                 ).then_inc(s_stage, 16)
                    sp.dma_start(stage_d[:, :], d["wd_all"][:, bass.ds((b - 2) * D_PIECE, D_PIECE)]
                                 ).then_inc(s_stage, 16)
                    sp.wait_ge(s_xn, b * NT + NT)
                    sp.dma_start(xn_d[bass.ds(b - 2, 1), :, :, :].rearrange("b p t c -> p (b t) c"),
                                 xn[u][:, :, :]).then_inc(s_xst[u], 16)
                    for s in range(NS):
                        sp.wait_ge(s_base, b * 2 * NS + 2 * (s + 1))
                        sp.dma_start(base_d[bass.ds((b - 2) * NS + s, 1), :, :, :]
                                     .rearrange("s p t c -> p (s t) c"), base_sb[:, s, :, :]
                                     ).then_inc(s_bst[s], 16)
            for u in range(2):
                sp.wait_ge(s_xst[u], (B // 2 + 1) * 16)
                sp.wait_ge(s_sc[u], B // 2 * 16 * TOP * NT)
            for s in range(NS):
                sp.wait_ge(s_bst[s], (B + 2) * 16)
            sp.wait_ge(c["s_load"], c["n_load"] * 16)

        @block.tensor
        def _(pe):
            pe.wait_ge(s_pro, 1)
            pe.wait_ge(s_swl, len(shared))
            pe.wait_ge(s_swh, len(shared))
            pe.wait_ge(c["s_load"], c["n_load"] * 16)
            with pe.Fori(0, B // 2) as it:
                for u in range(2):
                    b = it * 2 + (2 + u)
                    for s in range(NS):
                        pe.wait_ge(s_xn, b * NT + (s + 1) * TS)
                        for kc in range(KC):
                            if s:
                                pe.wait_ge(s_xl, b * NS * KC + kc + 1)
                            else:
                                pe.wait_ge(s_lg, b * NS)
                            for j in range(TS):
                                mm = pe.transpose(ps_a[kc][:, j * P:(j + 1) * P],
                                                  xn[u][:, s * TS + j, kc * P:(kc + 1) * P],
                                                  c["ident"][:, :])
                            mm.then_inc(s_xT, 1)

                    def hidden(k):
                        s, f = k // len(SF), SF_ORDER[k % len(SF)]
                        sup = slice(s * ST, (s + 1) * ST)
                        rows = SF[f] + (E if f == 2 else 0)
                        if k % len(SF) == 0:
                            pe.wait_ge(s_xl, b * NS * KC + (s + 1) * KC)
                        pe.wait_ge(s_silu, b * NB + k - 1)
                        if k == 0:
                            pe.wait_ge(s_pos, b)
                        for kc in range(KC):
                            mm = three(pe, ps_g[k % 2][0:rows, :],
                                       [sg[i][:, kc, f * P:f * P + rows] for i in range(2)],
                                       [xT[i][:, kc, sup] for i in range(2)], kc == 0, kc == KC - 1)
                        mm.then_inc(s_g, 1)
                        rows = SF[f]
                        pe.wait_ge(s_gu, b * NB + k - 1)
                        for kc in range(KC):
                            mm = three(pe, ps_u[k % 2][0:rows, :],
                                       [su[i][:, kc, f * P:f * P + rows] for i in range(2)],
                                       [xT[i][:, kc, sup] for i in range(2)], kc == 0, kc == KC - 1)
                        mm.then_inc(s_u, 1)

                    def logits(s):
                        pe.wait_ge(s_silu, b * NB + s * len(SF) + 1)
                        pe.wait_ge(s_xl, b * NS * KC + KC + s + 1)
                        if s:
                            pe.wait_ge(s_lg, b * NS + s)
                        for j in range(TS):
                            mm = pe.matmul(ps_a[s][:, j * E:(j + 1) * E],
                                           logitT[SF[2]:SF[2] + E, j * P:(j + 1) * P],
                                           c["ident"][SF[2]:SF[2] + E, SF[2]:SF[2] + E],
                                           start=True, stop=True)
                        mm.then_inc(s_lgT, 1)

                    def down(s):
                        pe.wait_ge(s_hl, b * NB + (s + 1) * len(SF))
                        for j in range(TS):
                            if j % 2 == 0:
                                pe.wait_ge(s_base, b * 2 * NS + 2 * s + j // 2 - 1)
                            for f in range(len(SF)):
                                mm = three(pe, ps_y[j // 2][:, (j % 2) * H:(j % 2 + 1) * H],
                                           [hT[i][0:SF[f], f, j * P:(j + 1) * P] for i in range(2)],
                                           [sd[i][0:SF[f], f, :] for i in range(2)],
                                           f == 0, f == len(SF) - 1)
                            if j % 2:
                                mm.then_inc(s_y, 1)

                    hidden(0)
                    hidden(1)
                    logits(0)
                    hidden(2)
                    hidden(3)
                    hidden(4)
                    logits(1)
                    down(0)
                    hidden(5)
                    down(1)
                    pe.wait_ge(s_mask, b + 1)
                    pe.wait_ge(s_silu, b * NB + NB)
                    pe.matmul(ps_g[0][:, 0:(NT + 1) * E], before_bf[:, :],
                              mask[:, :, :], start=True, stop=False)
                    for i in range(NT):
                        mm = pe.matmul(ps_g[0][:, (i + 1) * E:(NT + 1) * E], ones_bf[:, :],
                                       mask[:, i, :].unsqueeze(1).broadcast_to([P, NT - i, E]),
                                       start=False, stop=(i == NT - 1))
                    mm.then_inc(s_pre, 1)

        @block.scalar
        def _(act):
            for to, source in c["loads"]:
                act.dma_start(to, source).then_inc(c["s_load"], 16)
            act.wait_ge(s_sw, 64)
            act.wait_ge(c["s_load"], c["n_load"] * 16)
            for st, parts in shared:
                act.activation(parts[0], st, ACT.Copy).then_inc(s_swh, 1)
            act.wait_ge(s_swl, len(shared))

            def normed(b, u, stored):
                act.wait_ge(s_rstd, b + 1)
                act.wait_ge(s_xst[u], stored)
                for t in range(NT):
                    act.activation(xn[u][:, t, :], x_in[u][:, t, :], ACT.Identity,
                                   bias=shift[:, t:t + 1], scale=rstd[:, t:t + 1]).then_inc(s_xn, 1)

            act.activation(tick_s[:, :], c["lane"][:, :], ACT.Silu)
            normed(2, 0, 16)
            with act.Fori(0, B // 2) as it:
                for u in range(2):
                    b = it * 2 + (2 + u)
                    for s in range(NS):
                        for kc in range(KC):
                            act.wait_ge(s_xT, b * NS * KC + s * KC + kc + 1)
                            act.activation(xT[0][:, kc, s * ST:(s + 1) * ST], ps_a[kc][:, :],
                                           ACT.Copy).then_inc(s_xh, 1)

                    def silu_of(k):
                        s, f = k // len(SF), SF_ORDER[k % len(SF)]
                        act.wait_ge(s_g, b * NB + k + 1)
                        act.wait_ge(s_gu, b * NB + k - 1)
                        ins = act.activation(silu[0:SF[f], k % 2, :], ps_g[k % 2][0:SF[f], :], ACT.Silu)
                        if f == 2:
                            act.wait_ge(s_lgT, b * NS + s)
                            ins = act.activation(logitT[SF[2]:SF[2] + E, :],
                                                 ps_g[k % 2][SF[2]:SF[2] + E, :], ACT.Copy)
                        ins.then_inc(s_silu, 1)

                    def high(k):
                        s, f = k // len(SF), SF_ORDER[k % len(SF)]
                        act.wait_ge(s_gu, b * NB + k + 1)
                        act.wait_ge(s_y, b * 2 * NS + 2 * s)
                        act.activation(hT[0][0:SF[f], f, :], hf[0:SF[f], k % 2, :], ACT.Copy).then_inc(s_hh, 1)

                    def logits_out(s):
                        act.wait_ge(s_lgT, b * NS + s + 1)
                        act.wait_ge(s_slot, b)
                        act.activation(logit[:, s * TS:(s + 1) * TS, :],
                                       ps_a[s][:, 0:TS * E].rearrange("p (t e) -> p t e", e=E),
                                       ACT.Copy).then_inc(s_lg, 1)

                    silu_of(0)
                    silu_of(1)
                    high(0)
                    logits_out(0)
                    silu_of(2)
                    high(1)
                    silu_of(3)
                    high(2)
                    act.wait_ge(s_stage, b * 32 + 32)
                    act.activation(w["wb"][0][:, bass.ds((b - 2) * W_PIECE, W_PIECE)], stage_w[:, :],
                                   ACT.Copy).then_inc(s_wh, 1)
                    act.activation(w["wd"][0][:, bass.ds((b - 2) * D_PIECE, D_PIECE)], stage_d[:, :],
                                   ACT.Copy).then_inc(s_wh, 1)
                    silu_of(4)
                    logits_out(1)
                    high(3)
                    high(4)
                    silu_of(5)
                    high(5)
                    normed(b + 1, 1 - u, (it + 1 + u) * 16)

            act.wait_ge(s_slot, B + 2)
            act.wait_ge(s_wl, (B + 2) * 2)
            act.activation(ex[:, :, :], c["dist"][:, :, :], ACT.Exp).then_inc(s_exp, 1)

        @block.vector
        def _(dve):
            dve.memset(zeros[:, :], 0).then_inc(s_zero, 1)
            dve.memset(ones_bf[:, :], 1.0)
            dve.memset(mask[:, NT, :], 0.0)
            dve.memset(c["run"][:, :], 0.0)
            dve.memset(ln_eps[:, :], LN_EPS)
            dve.memset(neg[:, :], -1.0)
            dve.memset(half_neg[:, :], -0.5).then_inc(s_neg, 1)

            def norm_stats(b, u, loaded):
                dve.wait_ge(s_x[u], loaded)
                dve.wait_ge(s_xn, b * NT)
                for t in range(NT):
                    ins = dve.bn_stats(stats[:, t, :], x_in[u][:, t, :])
                ins.then_inc(s_st, 1)
                dve.wait_ge(s_st, b + 1)
                dve.memset(tick[:, :], 0.0)
                for t in range(NT):
                    ins = dve.bn_aggr(meanvar[:, t, :], stats[:, t, :])
                ins.then_inc(s_mv, 1)

            norm_stats(2, 0, 32)
            dve.wait_ge(c["s_load"], c["n_load"] * 16)
            dve.tensor_copy(before_bf[:, :], c["before"][:, :]).then_inc(s_pro, 1)
            for n, (st, parts) in enumerate(shared):
                dve.wait_ge(s_swh, n + 1)
                dve.tensor_tensor(parts[1], st, parts[0].bitcast(F32), ALU.subtract).then_inc(s_swl, 1)

            with dve.Fori(0, B // 2) as it:
                for u in range(2):
                    b = it * 2 + (2 + u)
                    link, links = chain(dve, s_dve, b * TOKEN_LINKS)
                    for s in range(NS):
                        for kc in range(KC):
                            sup = slice(s * ST, (s + 1) * ST)
                            dve.wait_ge(s_xh, b * NS * KC + s * KC + kc + 1)
                            dve.tensor_tensor(xT[1][:, kc, sup], ps_a[kc][:, :],
                                              xT[0][:, kc, sup].bitcast(F32), ALU.subtract).then_inc(s_xl, 1)

                    def rows_of(k):
                        f = SF_ORDER[k % len(SF)]
                        dve.wait_ge(s_silu, b * NB + k + 1)
                        dve.wait_ge(s_u, b * NB + k + 1)
                        dve.wait_ge(s_hl, b * NB + k - 1)
                        dve.tensor_tensor(hf[0:SF[f], k % 2, :], ps_u[k % 2][0:SF[f], :],
                                          silu[0:SF[f], k % 2, :], ALU.mult).then_inc(s_gu, 1)

                    def low(k):
                        f = SF_ORDER[k % len(SF)]
                        dve.wait_ge(s_hh, b * NB + k + 1)
                        dve.tensor_tensor(hT[1][0:SF[f], f, :], hf[0:SF[f], k % 2, :],
                                          hT[0][0:SF[f], f, :].bitcast(F32), ALU.subtract).then_inc(s_hl, 1)

                    def residual(s):
                        for j in range(2):
                            dve.wait_ge(s_y, b * 2 * NS + 2 * s + j + 1)
                            dve.wait_ge(s_bst[s], b * 16)
                            t = s * TS + 2 * j
                            dve.tensor_tensor(base_sb[:, s, 2 * j:2 * j + 2, :],
                                              ps_y[j][:, :].rearrange("p (t n) -> p t n", n=H),
                                              x_in[u][:, t:t + 2, :], ALU.add).then_inc(s_base, 1)

                    rows_of(0)
                    rows_of(1)
                    low(0)
                    norm_stats(b + 1, 1 - u, it * 16 + (32 + 16 * u))
                    for k in range(2, 5):
                        rows_of(k)
                        low(k - 1)
                    for n, (st, part, size) in enumerate(((stage_w, "wb", W_PIECE), (stage_d, "wd", D_PIECE))):
                        at = bass.ds((b - 2) * size, size)
                        dve.wait_ge(s_wh, b * 2 + n + 1)
                        dve.tensor_tensor(w[part][1][:, at], st[:, :], w[part][0][:, at].bitcast(F32),
                                          ALU.subtract).then_inc(s_wl, 1)
                    low(4)
                    rows_of(5)
                    low(5)
                    residual(0)
                    def over_experts(x):
                        return x.unsqueeze(2).broadcast_to([P, NT, E])

                    by_rank = c["rank_e"][:, :].unsqueeze(1).broadcast_to([P, NT, E])
                    dve.wait_ge(s_lg, b * NS + NS)
                    link(dve.tensor_reduce(r_m[:, 0, :], logit[:, :, :], AX.X, ALU.max))
                    dve.tensor_tensor(c["dist"][:, bass.ds((b - 2) * NT, NT), :], logit[:, :, :],
                                      over_experts(r_m[:, 0, :]), ALU.subtract)
                    link(dve.tensor_tensor(r_b[:, :, :], logit[:, :, :], over_experts(r_m[:, 0, :]),
                                           ALU.is_equal))
                    link(dve.tensor_tensor(r_b[:, :, :], r_b[:, :, :], by_rank, ALU.mult))
                    link(dve.tensor_reduce(r_m[:, 1, :], r_b[:, :, :], AX.X, ALU.max))
                    link(dve.tensor_tensor(r_s[:, 0, :, :], r_b[:, :, :], over_experts(r_m[:, 1, :]),
                                           ALU.is_equal))
                    link(dve.scalar_tensor_tensor(r_b[:, :, :], r_s[:, 0, :, :], -3e38, logit[:, :, :],
                                                  ALU.mult, ALU.add))
                    link(dve.tensor_reduce(r_m[:, 2, :], r_b[:, :, :], AX.X, ALU.max))
                    link(dve.tensor_tensor(r_c[:, :, :], r_b[:, :, :], over_experts(r_m[:, 2, :]),
                                           ALU.is_equal))
                    link(dve.tensor_tensor(r_c[:, :, :], r_c[:, :, :], by_rank, ALU.mult))
                    link(dve.tensor_reduce(r_m[:, 3, :], r_c[:, :, :], AX.X, ALU.max))
                    link(dve.tensor_tensor(r_s[:, 1, :, :], r_c[:, :, :], over_experts(r_m[:, 3, :]),
                                           ALU.is_equal))
                    dve.tensor_tensor(mask[:, 0:NT, :], r_s[:, 0, :, :], r_s[:, 1, :, :],
                                      ALU.add).then_inc(s_mask, 1)
                    residual(1)
                    dve.wait_ge(s_pre, b + 1)
                    link(dve.tensor_tensor(pos[:, :, :], ps_g[0][:, 0:NT * E]
                                           .rearrange("p (t e) -> p t e", e=E),
                                           c["run"][:, :].unsqueeze(1).broadcast_to([P, NT, E]), ALU.add))
                    dve.tensor_tensor(c["run"][:, :], ps_g[0][:, NT * E:(NT + 1) * E], c["run"][:, :],
                                      ALU.add).then_inc(s_pos, 1)
                    link(dve.tensor_tensor(pos[:, :, :], pos[:, :, :],
                                           c["region"][:, :].unsqueeze(1).broadcast_to([P, NT, E]), ALU.add))
                    dve.tensor_tensor(r_b[:, :, :], r_s[:, 0, :, :], pos[:, :, :], ALU.mult)
                    link(dve.tensor_tensor(r_c[:, :, :], r_s[:, 1, :, :], pos[:, :, :], ALU.mult))
                    dve.tensor_reduce(slot_f[:, 0, :], r_b[:, :, :], AX.X, ALU.add)
                    link(dve.tensor_reduce(slot_f[:, 1, :], r_c[:, :, :], AX.X, ALU.add))
                    dve.tensor_copy(c["slots"][:, :, bass.ds((b - 2) * NT, NT)], slot_f[:, :, :])
                    for k in range(TOP):
                        dve.tensor_copy(c["picks"][:, k, bass.ds((b - 2) * NT, NT), :], r_s[:, k, :, :])
                    dve.wait_ge(s_sc[u], it * 16 * TOP * NT)
                    dve.tensor_copy(number[u][:, :], c["number"][:, bass.ds((b - 2) * NT, NT)])
                    dve.tensor_copy(slot_i[u][:, :, :], slot_f[:, :, :]).then_inc(s_slot, 1)
                    assert links[0] == TOKEN_LINKS, links[0]

            link, links = chain(dve, s_tab)
            dve.wait_ge(s_slot, B + 2)
            dve.wait_ge(s_base, (B + 2) * 2 * NS)
            dve.wait_ge(s_wl, (B + 2) * 2)
            dve.wait_ge(s_hl, (B + 2) * NB)
            def per_block(x):
                return x.unsqueeze(1).broadcast_to([P, NI, E])

            link(dve.tensor_scalar(count_f[:, :], c["run"][:, :], float(P - 1), None, ALU.add))
            link(dve.tensor_copy(count_i[:, :], count_f[:, :]))
            link(dve.tensor_scalar(count_i[:, :], count_i[:, :], 7, None, ALU.logical_shift_right))
            link(dve.tensor_copy(count_f[:, :], count_i[:, :]))
            link(dve.memset(first[:, 0:1], 0.0))
            for e in range(E):
                link(dve.tensor_tensor(first[:, e + 1:e + 2], first[:, e:e + 1], count_f[:, e:e + 1], ALU.add))
            link(dve.tensor_scalar(last1[:, :], first[:, E:E + 1], -1.0, None, ALU.add))
            link(dve.tensor_scalar(blk[:, :], c["blk_row"][:, :], last1[:, 0:1], None, ALU.min))
            link(dve.tensor_tensor(ge[:, :, :], blk[:, :].unsqueeze(2).broadcast_to([P, NI, E]),
                                   per_block(first[:, 0:E]), ALU.is_ge))
            dve.tensor_tensor(oh[:, :, 0:E - 1], ge[:, :, 0:E - 1], ge[:, :, 1:E], ALU.subtract)
            link(dve.tensor_copy(oh[:, :, E - 1:E], ge[:, :, E - 1:E]))
            link(dve.tensor_tensor(tmp[:, :, :], oh[:, :, :], per_block(first[:, 0:E]), ALU.mult))
            link(dve.tensor_reduce(blk_first[:, :], tmp[:, :, :], AX.X, ALU.add))
            link(dve.tensor_reduce(blk_e[:, :], ge[:, :, :], AX.X, ALU.add))
            link(dve.tensor_scalar(blk_e[:, :], blk_e[:, :], -1.0, None, ALU.add))
            link(dve.tensor_tensor(start[:, :], blk[:, :], blk_first[:, :], ALU.subtract))
            link(dve.tensor_scalar(start[:, :], start[:, :], float(P), None, ALU.mult))
            link(dve.scalar_tensor_tensor(start[:, :], blk_e[:, :], float(T), start[:, :], ALU.mult, ALU.add))
            link(dve.memset(e_f[:, 0:2], 0.0))
            link(dve.tensor_copy(e_f[:, 2:NI + 2], blk_e[:, :]))
            passes = NI // UNROLL
            digit = [e_f[:, j:j + (passes - 1) * UNROLL + 1:UNROLL] for j in range(UNROLL + 2)]
            link(dve.tensor_copy(pack[:, :], digit[UNROLL + 1]))
            for j in reversed(range(UNROLL + 1)):
                link(dve.scalar_tensor_tensor(pack[:, :], pack[:, :], float(E), digit[j], ALU.mult, ALU.add))
            link(dve.tensor_copy(c["pack"][:, :], pack[:, :]))
            link(dve.tensor_copy(c["start"][:, :], start[:, :]))
            link(dve.scalar_tensor_tensor(shift_e[:, :], first[:, 0:E], float(P), c["region"][:, :],
                                          ALU.mult, ALU.subtract))
            link(dve.tensor_tensor(moved[:, :, :], c["picks"][:, :, :, :].rearrange("p k t e -> p (k t) e"),
                                   shift_e[:, :].unsqueeze(1).broadcast_to([P, TOP * NTA, E]), ALU.mult))
            link(dve.tensor_reduce(moved_s[:, :], moved[:, :, :], AX.X, ALU.add))
            link(dve.tensor_tensor(moved_s[:, :], moved_s[:, :],
                                   c["slots"][:, :, :].rearrange("p k t -> p (k t)"), ALU.add))
            link(dve.tensor_scalar(moved_s[:, :], moved_s[:, :], float(2 * P), None, ALU.add))
            link(dve.tensor_copy(c["from"][:, :], moved_s[:, :]))
            dve.wait_ge(s_exp, 1)
            for k in range(TOP):
                link(dve.tensor_tensor(exs[:, k, :, :], c["picks"][:, k, :, :], ex[:, :, :], ALU.mult))
                link(dve.tensor_reduce(z[:, k, :], exs[:, k, :, :], AX.X, ALU.add))
            link(dve.tensor_reduce(z[:, 2, :], ex[:, :, :], AX.X, ALU.add))
            link(dve.tensor_tensor(z[:, 3, :], z[:, 0, :], z[:, 1, :], ALU.add))
            link(dve.scalar_tensor_tensor(z[:, 3, :], z[:, 2, :], 1e-20, z[:, 3, :], ALU.mult, ALU.add))
            link(dve.reciprocal(z[:, 2, :], z[:, 3, :]))
            for k in range(TOP):
                link(dve.tensor_tensor(c["cw"][:, k, :], z[:, k, :], z[:, 2, :], ALU.mult))

        @block.gpsimd
        def _(pool):
            for signal, count in per_batch:
                pool.sem_inc(signal, 2 * count)
            for signal, count in per_pass:
                pool.sem_inc(signal, count)
            pool.wait_ge(s_neg, 1)

            def scale_and_shift(b):
                link, links = chain(pool, s_pool, b * POOL_LINKS)
                pool.wait_ge(s_mv, b + 1)
                link(pool.tensor_tensor(varp[:, :], meanvar[:, :, 1], ln_eps[:, :], ALU.add))
                link(pool.tensor_tensor(rstd[:, :], varp[:, :], half_neg[:, :], ALU.pow))
                link(pool.tensor_tensor(shift[:, :], meanvar[:, :, 0], neg[:, :], ALU.mult))
                pool.tensor_tensor(shift[:, :], shift[:, :], rstd[:, :], ALU.mult).then_inc(s_rstd, 1)

            scale_and_shift(2)
            pool.wait_ge(s_listed, 16)
            with pool.Fori(0, B // 2) as it:
                for u in range(2):
                    b = it * 2 + (2 + u)
                    scale_and_shift(b + 1)
                    pool.wait_ge(s_slot, b + 1)
                    pool.wait_ge(c["s_load"], c["n_load"] * 16)
                    pool.wait_ge(s_tick, b)
                    pool.tensor_tensor(tick_p[:, :], c["lane"][:, :], c["lane"][:, :],
                                       ALU.add).then_inc(s_tick, 1)
                    for t in range(NT):
                        for k in range(TOP):
                            pool.indirect_dma_start(
                                d["lists"], bass.IndirectOffsetOnAxis(ap=slot_i[u][:, k, t:t + 1], axis=0),
                                number[u][:, t:t + 1], None).then_inc(s_sc[u], 16)



TABLE_LINKS = 0


def experts_phase(nc, d, c, w):
    with ExitStack() as scope:
        sb, bank, sem = places(nc, scope)
        xg = [sb(f"xg{i}", [P, H]) for i in range(UNROLL)]
        g_i = [sb(f"g_i{i}", [P, 1], I32) for i in range(UNROLL)]
        xb = [[sb(f"xb{q}{i}", [P, KC, P], F32R) for i in range(2)] for q in range(2)]
        silu = [sb(f"silu2{q}", [P, F]) for q in range(2)]
        h_sb = [sb(f"h_sb{q}", [P, F]) for q in range(2)]
        hb = [[sb(f"hb{q}{i}", [FC, 2, P], F32R) for i in range(2)] for q in range(2)]
        y_sb = [sb(f"y_sb{q}", [P, H]) for q in range(2)]

        ps_x = [bank(f"e_x{q}") for q in range(2)]
        ps_up = [bank(f"e_up{q}") for q in range(2)]
        ps_h = [bank(f"e_h{q}") for q in range(2)]
        ps_y = [bank(f"e_y{q}") for q in range(2)]

        s_tab, s_init = sem("e_tab"), sem("e_init")
        tick_s = sb("tick_s", [P, 1])
        tick_e = sb("tick_e", [P, 1])
        s_ga = [sem(f"e_ga{i}") for i in range(UNROLL)]
        s_tick = sem("e_tick")
        s_gi = [sem(f"e_gi{i}") for i in range(UNROLL)]
        s_xT, s_xh, s_xl = sem("e_xT"), sem("e_xh"), sem("e_xl")
        s_up, s_silu, s_h, s_hT, s_hh, s_hl = (
            sem("e_up"), sem("e_silu"), sem("e_h"), sem("e_hT"), sem("e_hh"), sem("e_hl"))
        s_dn, s_y, s_yst = sem("e_dn"), sem("e_y"), [sem(f"e_yst{q}") for q in range(2)]

        start_at = [(s_tick, 4), (s_xT, 4), (s_xh, 4), (s_xl, 4), (s_up, 4), (s_silu, 4), (s_h, 4),
                    (s_hT, 3), (s_hh, 3), (s_hl, 3), (s_dn, 2), (s_y, 2)]
        grouped_y = d["grouped_y"].rearrange("(i p) c -> i p c", p=P)

        block = scope.enter_context(nc.Block())

        @block.sync
        def _(sp):
            def numbers(j, buf):
                at = sp.value_load(c["start"][0:1, j], min_val=0, max_val=E * T - P)
                sp.dma_start(g_i[buf][:, :], d["lists"][bass.ds(at, P), :]).then_inc(s_gi[buf], 16)

            for j in range(UNROLL):
                numbers(slice(j, j + 1), j)
            for j in range(UNROLL, UNROLL + 2):
                sp.wait_ge(s_ga[j % UNROLL], 16)
                numbers(slice(j, j + 1), j % UNROLL)
            with sp.Fori(0, SLOTS // UNROLL) as it:
                for u in range(UNROLL):
                    n = it * UNROLL + (u + 4)
                    q = u % 2
                    sp.wait_ge(s_ga[(u + 2) % UNROLL], it * 16 + (16 if u < 2 else 32))
                    numbers(bass.ds(n + 2, 1), (u + 2) % UNROLL)
                    sp.wait_ge(s_y, n - 1)
                    sp.dma_start(grouped_y[bass.ds(n - 4, 1), :, :].rearrange("i p c -> p (i c)"),
                                 y_sb[q][:, :]).then_inc(s_yst[q], 16)
            sp.wait_ge(s_y, SLOTS + 3)
            sp.dma_start(grouped_y[SLOTS:SLOTS + 1, :, :].rearrange("i p c -> p (i c)"), y_sb[0][:, :]
                         ).then_inc(s_yst[0], 16)
            for q in range(2):
                sp.wait_ge(s_yst[q], 16 + 8 * SLOTS + (16 if q == 0 else 0))
            for i in range(UNROLL):
                sp.wait_ge(s_gi[i], 16 * (SLOTS // UNROLL + 1 + (i < 2)))

        @block.tensor
        def _(pe):
            def transposed(j_buf, q):
                for kc in range(KC):
                    mm = pe.transpose(ps_x[q][:, kc * P:(kc + 1) * P], xg[j_buf][:, kc * P:(kc + 1) * P],
                                      c["ident"][:, :])
                mm.then_inc(s_xT, 1)

            pe.wait_ge(s_init, 1)
            for j in range(2):
                pe.wait_ge(s_ga[j], 16)
                transposed(j, j)

            def down(at_dn, n, q):
                pe.wait_ge(s_hl, n - 1)
                pe.wait_ge(s_y, n - 3)
                for f in range(2):
                    cols = bass.ds(at_dn + f * H, H)
                    mm = three(pe, ps_y[q][:, 0:H], [hb[q][i][:, f, :] for i in range(2)],
                               [w["wd"][i][:, cols] for i in range(2)], f == 0, f == 1)
                mm.then_inc(s_dn, 1)

            with pe.Fori(0, SLOTS // UNROLL) as it:
                word = pe.value_load(c["pack"][0:1, bass.ds(it, 1)], min_val=0, max_val=E ** (UNROLL + 2) - 1)

                def columns(j):
                    expert = word // E ** (j + 2) % E
                    return expert * (2 * F), expert * (2 * H)

                at = [columns(-2), columns(-1), columns(0)]
                for u in range(UNROLL):
                    n = it * UNROLL + (u + 4)
                    q, o = u % 2, (u - 1) % 2
                    at_dn, at_up = at[u][1], at[u + 2][0]
                    pe.wait_ge(s_xl, n + 1)
                    pe.wait_ge(s_h, n - 1)
                    for kc in range(KC):
                        cols = bass.ds(at_up + kc * E * 2 * F, 2 * F)
                        mm = three(pe, ps_up[q][:, 0:2 * F], [xb[q][i][:, kc, :] for i in range(2)],
                                   [w["wb"][i][:, cols] for i in range(2)], kc == 0, kc == KC - 1)
                    mm.then_inc(s_up, 1)
                    if u < UNROLL - 1:
                        at.append(columns(u + 1))
                    pe.wait_ge(s_ga[(u + 2) % UNROLL], it * 16 + (16 if u < 2 else 32))
                    transposed((u + 2) % UNROLL, q)
                    down(at_dn, n, q)
                    pe.wait_ge(s_h, n)
                    for f in range(2):
                        mm = pe.transpose(ps_h[o][0:FC, f * P:(f + 1) * P], h_sb[o][:, f * FC:(f + 1) * FC],
                                          c["ident"][:, :])
                    mm.then_inc(s_hT, 1)
            word = pe.value_load(c["pack"][0:1, SLOTS // UNROLL:SLOTS // UNROLL + 1],
                                 min_val=0, max_val=E ** (UNROLL + 2) - 1)
            down(word % E * (2 * H), SLOTS + 4, 0)

        @block.scalar
        def _(act):
            def high_tokens(q):
                act.activation(xb[q][0][:, :, :], ps_x[q][:, 0:H].rearrange("p (k n) -> p k n", k=KC),
                               ACT.Copy).then_inc(s_xh, 1)

            act.activation(tick_s[:, :], c["lane"][:, :], ACT.Silu)
            for j in range(2):
                act.wait_ge(s_xT, 5 + j)
                high_tokens(j)
            with act.Fori(0, SLOTS // UNROLL) as it:
                for u in range(UNROLL):
                    n = it * UNROLL + (u + 4)
                    q, o = u % 2, (u - 1) % 2
                    act.wait_ge(s_up, n + 1)
                    act.activation(silu[q][:, :], ps_up[q][:, 0:F], ACT.Silu).then_inc(s_silu, 1)
                    act.wait_ge(s_xT, n + 3)
                    high_tokens(q)
                    act.wait_ge(s_hT, n)
                    act.wait_ge(s_dn, n - 2)
                    act.activation(hb[o][0][:, :, :], ps_h[o][0:FC, 0:2 * P].rearrange("p (k n) -> p k n", k=2),
                                   ACT.Copy).then_inc(s_hh, 1)

        @block.vector
        def _(dve):
            link, _ = chain(dve, s_tab)

            for q in range(2):
                link(dve.memset(h_sb[q][:, :], 0.0))
            for i in range(2):
                ins = (dve.tensor_scalar(hb[0][i][:, :, :], c["ident"][0:FC, :].unsqueeze(1).broadcast_to([FC, 2, P]),
                                       0.0, None, ALU.mult))
            ins.then_inc(s_init, 1)
            for j in range(2):
                dve.wait_ge(s_xh, 5 + j)
                dve.tensor_tensor(xb[j][1][:, :, :], ps_x[j][:, 0:H].rearrange("p (k n) -> p k n", k=KC),
                                  xb[j][0][:, :, :].bitcast(F32), ALU.subtract).then_inc(s_xl, 1)
            def result(n, q, stored):
                dve.wait_ge(s_dn, n - 1)
                dve.wait_ge(s_yst[q], stored)
                dve.tensor_copy(y_sb[q][:, :], ps_y[q][:, 0:H]).then_inc(s_y, 1)

            with dve.Fori(0, SLOTS // UNROLL) as it:
                for u in range(UNROLL):
                    n = it * UNROLL + (u + 4)
                    q, o = u % 2, (u - 1) % 2
                    dve.wait_ge(s_silu, n + 1)
                    dve.wait_ge(s_hT, n - 1)
                    dve.tensor_tensor(h_sb[q][:, :], ps_up[q][:, F:2 * F], silu[q][:, :],
                                      ALU.mult).then_inc(s_h, 1)
                    dve.wait_ge(s_xh, n + 3)
                    dve.tensor_tensor(xb[q][1][:, :, :], ps_x[q][:, 0:H].rearrange("p (k n) -> p k n", k=KC),
                                      xb[q][0][:, :, :].bitcast(F32), ALU.subtract).then_inc(s_xl, 1)
                    result(n, q, it * 32 + 16 + (16 if u >= 2 else 0))
                    dve.wait_ge(s_hh, n)
                    dve.tensor_tensor(hb[o][1][:, :, :], ps_h[o][0:FC, 0:2 * P].rearrange("p (k n) -> p k n", k=2),
                                      hb[o][0][:, :, :].bitcast(F32), ALU.subtract).then_inc(s_hl, 1)
            result(SLOTS + 4, 0, SLOTS * 8 + 16)

        @block.gpsimd
        def _(pool):
            for signal, count in start_at:
                pool.sem_inc(signal, count)
            for signal in s_yst:
                pool.sem_inc(signal, 16)

            def fetch(buf, seen, loaded):
                pool.wait_ge(s_gi[buf], loaded)
                pool.wait_ge(s_tick, seen - 1)
                pool.tensor_tensor(tick_e[:, :], c["lane"][:, :], c["lane"][:, :],
                                   ALU.add).then_inc(s_tick, 1)
                pool.indirect_dma_start(xg[buf][:, :], None, d["xn"],
                                        bass.IndirectOffsetOnAxis(ap=g_i[buf][:, :], axis=0)
                                        ).then_inc(s_ga[buf], 16)

            for j in range(UNROLL + 1):
                if j == UNROLL:
                    pool.wait_ge(s_xT, 5)
                fetch(j % UNROLL, 5 + j, 16 + 16 * (j // UNROLL))
            with pool.Fori(0, SLOTS // UNROLL) as it:
                for u in range(UNROLL):
                    n = it * UNROLL + (u + 4)
                    pool.wait_ge(s_xT, n + 2)
                    fetch((u + 1) % UNROLL, n + 6, it * 16 + (32 if u < UNROLL - 1 else 48))
            for i in range(UNROLL):
                pool.wait_ge(s_ga[i], 16 * (SLOTS // UNROLL + 1 + (i < 1)))


def attention_order():
    fill = {t: [] for t in range(NT)}
    fill[0] = [("k", 0, 1, 0), ("v", 0, 4, 0)]
    fill[1] = [("k", 0, 1, 1), ("v", 0, 5, 0)]
    fill[2] = [("v", 0, 6, 0)]
    fill[3] = [("v", 0, 7, 0)]
    fill[4] = [("xT", 1, 0, 0), ("xT", 1, 0, 1), ("q", 1, 0, 0)]
    fill[5] = [("q", 1, 0, 1), ("k", 1, 0, 0)]
    fill[6] = [("k", 1, 0, 1), ("v", 1, 0, 0), ("v", 1, 1, 0)]
    fill[7] = [("v", 1, 2, 0), ("v", 1, 3, 0)]
    order = [("xT", 0, 1, 0), ("xT", 0, 1, 1), ("q", 0, 1, 0), ("q", 0, 1, 1)]
    for t in range(NT):
        more = fill[t] + [None] * 3
        order += [("norms", 0, t, 0), ("keys", 0, t, 0), ("scores", 0, t, 0), ("scores", 0, t, 1)]
        if t == 0:
            order.append(("mean", 0, 0, 0))
        order.append(more[0])
        order += [("coarseT", 0, t, 0), ("scores", 0, t, 2), ("scores", 0, t, 3)]
        if t:
            order.append(("outT", 0, t - 1, 0))
        order += [more[1], ("hidden", 0, t, 0), ("local", 0, t, 0)]
        if t == 0:
            order.append(("weights", 0, 0, 0))
        order += [("gate", 0, t, 0)]
        if t < NT - 1:
            order.append(("state", 0, t, 0))
        order.append(more[2])
        if t:
            order.append(("oproj", 0, t - 1, 0))
        order += [("fine", 0, t, 0), ("fine", 0, t, 1)]
    order += [("outT", 0, NT - 1, 0), ("oproj", 0, NT - 1, 0)]
    return [x for x in order if x]


ATT_ORDER = attention_order()
NR = 8
RING = [x for x in ATT_ORDER if x[0] != "weights"]
TURN = {use: n for n, use in enumerate(RING)}


def attention_phase(nc, d, c, w):
    with ExitStack() as scope:
        sb, bank_, sem = places(nc, scope)
        x_in = sb("xn_in", [P, NT, H])
        xT = [sb(f"a_xT{i}", [P, KC, SEQ], F32R) for i in range(2)]
        sqT, skT = sb("sqT", [P, KC, SEQ]), sb("skT", [P, KC, SEQ])
        v1 = sb("v1", [P, NT, NH, HE])
        keep, gate = sb("keep", [P, NH]), sb("gate_s", [P, NH])
        half_b2 = sb("half_b2", [P, 1])
        ones = sb("ones", [P, P])
        fine_bd = sb("fine_bd", [P, KC, NM, HH, HD])
        coarse_bd = sb("coarse_bd", [P, KC, WN])
        alive = sb("alive", [P, NM + 1])
        nsum = sb("nsum", [P, NM + 1])
        csum, csum2, nc_sum = sb("csum", [P, HD]), sb("csum2", [P, HD]), sb("nc_sum", [P, KC])
        elu_e, elu_r = sb("elu_e", [P, 2, ST]), sb("elu_r", [P, 2, ST])
        qsum, qtot, qmean = sb("qsum", [P, KC, NS]), sb("qtot", [P, KC]), sb("qmean", [P, KC, P])
        mw, mw_m = sb("mw", [P, KC, NM, HH]), sb("mw_m", [P, 2, KC, HH])
        qm = sb("qm", [P, KC, 2, P])
        probs = sb("probs", [P, 4, 4, P])
        k_tok = sb("k_tok", [P, H])
        state, kvm = sb("state", [P, KC, HH * HE]), sb("kvm", [P, KC, HH * HE])
        den, rn = sb("den", [P, NH]), sb("rn", [P, KC, NM + 1, HH])
        local, coarse, coarseT = sb("local", [P, H]), sb("coarse", [P, H]), sb("coarseT", [P, KC, P])
        hid, e_t = sb("hid", [G1, P]), sb("e_t", [P, 3])
        coef, coef_c = sb("coef", [P, KC, NM, HH]), sb("coef_c", [P, NH])
        rest = sb("rest", [P, H])
        prod, part = sb("prod", [P, KC, NM, P]), sb("part", [P, KC, 2, P])
        att = sb("att", [P, H])
        attT = [sb(f"attT{q}", [P, KC, P]) for q in range(2)]
        from_b, cw_b = sb("from_b", [P, TOP, NT], I32), sb("cw_b", [P, TOP, NT])
        yg = [sb(f"yg{i}", [P, TOP, H]) for i in range(4)]
        tick_a = sb("tick_a", [P, 1])
        total = sb("total", [P, NT, H])
        ring = [bank_(f"a_ring{i}") for i in range(NR)]

        s_gexp, s_nsum, s_pro, s_ones, s_pdve = (
            sem("a_gexp"), sem("a_nsum"), sem("a_pro"), sem("a_ones"), sem("a_pdve"))
        s_dve, s_pool = sem("a_dve"), sem("a_pool")
        s_tick = sem("a_tick")
        s_x, s_bx, s_out, s_ga, s_fb, s_yc, s_ysum, s_sum = (
            sem("a_x"), sem("a_bx"), sem("a_out"), sem("a_ga"), sem("a_fb"), sem("a_yc"), sem("a_ysum"),
            sem("a_sum"))
        ready = {name: sem(f"a_ps_{name}") for name in
                 ("xT", "q", "v", "mean", "k", "norms", "keys", "scores", "outT", "coarseT",
                  "hidden", "local", "gate", "state", "fine", "oproj")}
        s_xh, s_xl, s_v = sem("a_xh"), sem("a_xl"), sem("a_v")
        s_elu, s_elu_used, s_sq, s_sk = sem("a_elu"), sem("a_elu_used"), sem("a_sq"), sem("a_sk")
        s_qmean, s_mean, s_mx, s_mexp = sem("a_qmean"), sem("a_mean"), sem("a_mx"), sem("a_mexp")
        s_qm, s_ktok, s_probs, s_kvm, s_state, s_local = (
            sem("a_qm"), sem("a_ktok"), sem("a_probs"), sem("a_kvm"), sem("a_state"), sem("a_local"))
        s_coarse, s_coarseT, s_hid, s_e, s_prod = (
            sem("a_coarse"), sem("a_coarseT"), sem("a_hid"), sem("a_e"), sem("a_prod"))
        s_rest, s_att, s_attT = sem("a_rest"), sem("a_att"), sem("a_attT")

        DVE_LINKS, POOL_LINKS = 79, 25
        per_batch = [
            (s_x, 16), (s_bx, 16), (s_out, 16 * NS), (s_fb, 1), (s_tick, 2), (s_yc, NT),
            (s_ysum, NT), (s_sum, NT), (s_xh, NS * KC), (s_xl, NS * KC), (s_v, NT),
            (s_elu, 2 * NS * KC), (s_sq, NS * KC), (s_sk, NS * KC), (s_qmean, 1), (s_mean, 1), (s_mx, 1),
            (s_mexp, 1), (s_qm, NT), (s_ktok, NT), (s_probs, 4 * NT), (s_kvm, NT - 1), (s_state, NT - 1),
            (s_local, NT), (s_coarse, NT), (s_coarseT, NT), (s_hid, NT), (s_e, NT), (s_prod, KC * NT),
            (s_rest, NT), (s_att, NT), (s_attT, NT), (s_dve, DVE_LINKS), (s_pool, POOL_LINKS)]
        stage_times = {
            "xT": NS * KC, "q": NS * KC, "v": NT, "mean": 1, "k": NS * KC, "norms": NT, "keys": NT,
            "scores": 4 * NT, "outT": NT, "coarseT": NT, "hidden": NT, "local": NT, "gate": NT,
            "state": NT - 1, "fine": KC * NT, "oproj": NT}
        per_batch += [(ready[name], n) for name, n in stage_times.items()]

        elus = [(x[0], x[2], x[3]) for x in ATT_ORDER if x[0] in ("q", "k") and x[1] == 1]
        elus += [(x[0], x[2], x[3]) for x in ATT_ORDER if x[0] in ("q", "k") and x[1] == 0]
        elu_turn = {x: i for i, x in enumerate(elus)}

        last_reader = {
            "xT": s_xl, "q": s_elu, "k": s_elu, "v": s_v, "mean": s_mean, "norms": s_coarse,
            "keys": s_ktok, "scores": s_probs, "outT": s_attT, "coarseT": s_coarseT, "hidden": s_hid,
            "local": s_local, "gate": s_e, "state": s_kvm, "fine": s_prod, "oproj": s_sum}

        def nth(name, n, j):
            return {"xT": n * KC + j, "q": n * KC + j, "k": n * KC + j, "scores": 4 * n + j,
                    "fine": KC * n + j}.get(name, n) + 1

        def read_count(b, name, n, j):
            if name in ("q", "k"):
                return b * len(elus) + elu_turn[(name, n, j)] + 1
            return b * stage_times[name] + nth(name, n, j)

        def bank(name, n, j):
            return ring[[TURN[x] for x in RING if x[0] == name and x[2:] == (n, j)][0] % NR]

        def use_bank(pe, b, item, items):
            n = TURN[item]
            before = [(k, b) for k in range(n - NR, -1, -NR)]
            k = n + NR * ((len(RING) - 1 - n) // NR)
            before += [(k, b - 1)]
            while k - NR > n:
                k -= NR
                before += [(k, b - 1)]
            for k, bb in before:
                name, off, m, j = RING[k]
                if bb is b and RING[k] not in items:
                    continue
                at = read_count(bb + off, name, m, j)
                if not isinstance(at, int) or at > 0:
                    pe.wait_ge(last_reader[name], at)
                break
            return ring[n % NR]

        x_src = d["xn"].rearrange("(b t p) c -> b p t c", t=NT, p=P)
        base_src = d["base"].rearrange("(b t p) c -> b p t c", t=NT, p=P)
        out_v = d["out"].rearrange("(b s t p) c -> b s p t c", s=NS, t=TS, p=P)
        first = [x for x in ATT_ORDER if x[1] == 1]
        final = [x for x in ATT_ORDER if x[1] == 0]

        def over_batches(eng, walk):
            walk(0, first)
            with eng.Fori(1, B) as b:
                walk(b, ATT_ORDER)
            walk(B, final)

        block = scope.enter_context(nc.Block())

        @block.sync
        def _(sp):
            def fetch(b):
                sp.dma_start(x_in[:, :, :], x_src[bass.ds(b - 1, 1), :, :, :].rearrange("b p t c -> p (b t) c")
                             ).then_inc(s_x, 16)

            def rest_of(b, more):
                sp.wait_ge(s_out, b * 16 * NS)
                sp.dma_start(total[:, :, :], base_src[bass.ds(b - 1, 1), :, :, :]
                             .rearrange("b p t c -> p (b t) c")).then_inc(s_bx, 16)
                if more:
                    sp.wait_ge(ready["xT"], b * NS * KC + NS * KC)
                    fetch(b + 1)
                for s in range(NS):
                    sp.wait_ge(s_sum, b * NT + (s + 1) * TS)
                    sp.dma_start(out_v[bass.ds(b - 1, 1), s, :, :, :].rearrange("b p t c -> p (b t) c"),
                                 total[:, s * TS:(s + 1) * TS, :]).then_inc(s_out, 16)

            fetch(1)
            with sp.Fori(1, B) as b:
                rest_of(b, True)
            rest_of(B, False)
            sp.wait_ge(s_out, (B + 1) * NS * 16)

        @block.tensor
        def _(pe):
            pe.wait_ge(s_ones, 1)
            for m in range(KC):
                mm = pe.matmul(ring[NR - 1][:, 0:NM], ones[:, :], c["norms"][:, m, :],
                               start=(m == 0), stop=(m == KC - 1))
            mm.then_inc(s_nsum, 1)
            pe.wait_ge(s_pro, 1)

            def walk(b, items):
                for item in items:
                    what, off, n, j = item
                    if what == "weights":
                        continue
                    bb, t = b + off, n
                    tok = slice(t * P, (t + 1) * P)
                    ps = use_bank(pe, b, item, items)
                    if what == "xT":
                        pe.wait_ge(s_x, bb * 16 + 16)
                        for i in range(TS):
                            mm = pe.transpose(ps[:, i * P:(i + 1) * P],
                                              x_in[:, n * TS + i, j * P:(j + 1) * P], c["ident"][:, :])
                    elif what in ("q", "k"):
                        pe.wait_ge(s_xl, bb * NS * KC + (n + 1) * KC)
                        for kc in range(KC):
                            at = WUP + kc * 3 * H + (what == "k") * H + j * P
                            mm = three(pe, ps[:, :], [w["wb"][i][:, at:at + P] for i in range(2)],
                                       [xT[i][:, kc, n * ST:(n + 1) * ST] for i in range(2)],
                                       kc == 0, kc == KC - 1)
                    elif what == "v":
                        pe.wait_ge(s_xl, bb * NS * KC + (t // TS + 1) * KC)
                        for kc in range(KC):
                            at = WUP + kc * 3 * H + 2 * H
                            mm = three(pe, ps[:, 0:H], [xT[i][:, kc, tok] for i in range(2)],
                                       [w["wb"][i][:, at:at + H] for i in range(2)], kc == 0, kc == KC - 1)
                    elif what == "mean":
                        pe.wait_ge(s_qmean, b + 1)
                        for m in range(KC):
                            mm = pe.matmul(ps[:, m * NM * HH:(m + 1) * NM * HH], qmean[:, m, :],
                                           coarse_bd[:, m, P:P + NM * HH], start=True, stop=True)
                    elif what == "norms":
                        pe.wait_ge(s_sq, b * NS * KC + (t // TS + 1) * KC)
                        for m in range(KC):
                            mm = pe.matmul(ps[:, m * WN:(m + 1) * WN], sqT[:, m, tok], coarse_bd[:, m, :],
                                           start=True, stop=True)
                    elif what == "keys":
                        pe.wait_ge(s_sk, b * NS * KC + (t // TS + 1) * KC)
                        for m in range(KC):
                            mm = pe.transpose(ps[:, m * P:(m + 1) * P], skT[:, m, tok], c["ident"][:, :])
                    elif what == "scores":
                        pe.wait_ge(s_qm, b * NT + t + 1)
                        rows = slice(32 * j, 32 * j + 32)
                        for m in range(KC):
                            mm = pe.matmul(ps[:, 2 * m * P:2 * (m + 1) * P], skT[rows, m, tok],
                                           qm[rows, m, :, :], start=True, stop=True)
                    elif what == "outT":
                        pe.wait_ge(s_att, b * NT + t + 1)
                        for m in range(KC):
                            mm = pe.transpose(ps[:, m * P:(m + 1) * P], att[:, m * P:(m + 1) * P], c["ident"][:, :])
                    elif what == "oproj":
                        pe.wait_ge(s_attT, b * NT + t + 1)
                        for m in range(KC):
                            mm = pe.matmul(ps[:, 0:H], attT[t % 2][:, m, :], c["wo"][:, m, :],
                                           start=(m == 0), stop=(m == KC - 1))
                    elif what == "coarseT":
                        pe.wait_ge(s_coarse, b * NT + t + 1)
                        for m in range(KC):
                            mm = pe.transpose(ps[:, m * P:(m + 1) * P], coarse[:, m * P:(m + 1) * P],
                                              c["ident"][:, :])
                    elif what == "hidden":
                        pe.wait_ge(s_coarseT, b * NT + t + 1)
                        for m in range(KC):
                            mm = pe.matmul(ps[0:G1, 0:P], c["w1"][:, m, :], coarseT[:, m, :],
                                           start=(m == 0), stop=(m == KC - 1))
                    elif what == "local":
                        pe.wait_ge(s_v, b * NT + t + 1)
                        if t:
                            pe.wait_ge(s_state, b * (NT - 1) + t)
                            for m in range(KC):
                                pe.matmul(ps[:, m * HH * HE:(m + 1) * HH * HE], sqT[:, m, tok], state[:, m, :],
                                          start=(m == 0), stop=False)
                        for g in range(4):
                            pe.wait_ge(s_probs, b * NT * 4 + t * 4 + g + 1)
                            for i in range(4):
                                h = (i // 2) * HH + 2 * g + i % 2
                                mm = pe.matmul(ps[:, h * HE:(h + 1) * HE], probs[:, g, i, :], v1[:, t, h, :],
                                               start=(t == 0 and g == 0 and i == 0), stop=(g == 3 and i == 3))
                    elif what == "gate":
                        pe.wait_ge(s_hid, b * NT + t + 1)
                        mm = pe.matmul(ps[:, 0:1], hid[:, :], c["w2"][:, :], start=True, stop=True)
                    elif what == "state":
                        pe.wait_ge(s_ktok, b * NT + t + 1)
                        for m in range(KC):
                            mm = pe.matmul(ps[:, m * HH * HE:(m + 1) * HH * HE], k_tok[:, m * P:(m + 1) * P],
                                           v1[:, t, m * HH:(m + 1) * HH, :], start=True, stop=True)
                    elif what == "fine":
                        mm = pe.matmul(ps[:, :], sqT[:, j, tok], fine_bd[:, j, :, :, :], start=True, stop=True)
                    mm.then_inc(ready[what], 1)

            over_batches(pe, walk)

        @block.scalar
        def _(act):
            act.activation(keep[:, :], c["gate"][:, :], ACT.Exp, scale=-1.0).then_inc(s_gexp, 1)
            act.wait_ge(s_pro, 1)

            def walk(b, items):
                for what, off, n, j in items:
                    bb, t = b + off, n
                    if what not in ("xT", "q", "k", "v", "keys", "outT", "coarseT", "hidden", "gate", "mean",
                                    "norms"):
                        continue
                    if what == "norms":
                        act.wait_ge(s_fb, b + 1)
                        act.wait_ge(s_ga, (b - 1) * 16 * TOP * NT + 16 * TOP * (t + 1 + (3 - t % 4)))
                        for k in range(TOP):
                            ins = act.activation(yg[t % 4][:, k, :], yg[t % 4][:, k, :], ACT.Copy,
                                                 scale=cw_b[:, k, t:t + 1])
                        ins.then_inc(s_yc, 1)
                        continue
                    ps = bank(what, n, j)
                    act.wait_ge(s_mx if what == "mean" else ready[what],
                                b + 1 if what == "mean" else bb * stage_times[what] + nth(what, n, j))
                    if what == "xT":
                        act.activation(xT[0][:, j, n * ST:(n + 1) * ST], ps[:, :], ACT.Copy).then_inc(s_xh, 1)
                    elif what in ("q", "k"):
                        i = elu_turn[(what, n, j)]
                        act.wait_ge(s_elu_used, bb * len(elus) + i - 1)
                        act.activation(elu_e[:, i % 2, :], ps[:, :], ACT.Exp)
                        act.activation(elu_r[:, i % 2, :], ps[:, :], ACT.Relu).then_inc(s_elu, 1)
                    elif what == "v":
                        act.activation(v1[:, t, :, 0:HD], ps[:, 0:H].rearrange("p (h e) -> p h e", e=HD),
                                       ACT.Copy).then_inc(s_v, 1)
                    elif what == "mean":
                        act.activation(mw[:, :, :, :], mw[:, :, :, :], ACT.Exp).then_inc(s_mexp, 1)
                    elif what == "keys":
                        act.wait_ge(ready["state"], b * (NT - 1) + t)
                        act.activation(k_tok[:, :], ps[:, 0:H], ACT.Copy).then_inc(s_ktok, 1)
                    elif what == "outT":
                        act.wait_ge(ready["oproj"], b * NT + t - 1)
                        act.activation(attT[t % 2][:, :, :], ps[:, 0:H].rearrange("p (k n) -> p k n", k=KC),
                                       ACT.Copy).then_inc(s_attT, 1)
                    elif what == "coarseT":
                        act.wait_ge(ready["hidden"], b * NT + t)
                        act.activation(coarseT[:, :, :], ps[:, 0:H].rearrange("p (k n) -> p k n", k=KC),
                                       ACT.Copy).then_inc(s_coarseT, 1)
                    elif what == "hidden":
                        act.wait_ge(ready["gate"], b * NT + t)
                        act.activation(hid[:, :], ps[0:G1, 0:P], ACT.Relu, bias=c["b1"][:, 0:1]).then_inc(s_hid, 1)
                    elif what == "gate":
                        act.wait_ge(s_rest, b * NT + t)
                        act.activation(e_t[:, 0:1], ps[:, 0:1], ACT.Tanh,
                                       bias=half_b2[:, 0:1], scale=0.5).then_inc(s_e, 1)

            over_batches(act, walk)

        @block.vector
        def _(dve):
            link, links = chain(dve, s_pdve)
            dve.memset(ones[:, :], 1.0).then_inc(s_ones, 1)
            link(dve.memset(v1[:, :, :, HD:HE], 1.0))
            link(dve.tensor_scalar(half_b2[:, :], c["b2"][:, :], 0.5, None, ALU.mult))
            dve.wait_ge(s_gexp, 1)
            link(dve.tensor_scalar(den[:, :], keep[:, :], 1.0, None, ALU.add))
            link(dve.reciprocal(gate[:, :], den[:, :]))
            link(dve.tensor_scalar(keep[:, :], gate[:, :], -1.0, 1.0, ALU.mult, ALU.add))
            for m in range(KC):
                for i in range(NM):
                    dve.tensor_tensor(
                        fine_bd[:, m, i, :, :],
                        c["mem"][:, m, i * HD:(i + 1) * HD].unsqueeze(1).broadcast_to([P, HH, HD]),
                        c["same_head"][:, :].unsqueeze(2).broadcast_to([P, HH, HD]), ALU.mult)
                    dve.tensor_tensor(
                        coarse_bd[:, m, P + i * HH:P + (i + 1) * HH], c["same_head"][:, :],
                        c["norms"][:, m, i:i + 1].broadcast_to([P, HH]), ALU.mult)
                link(dve.tensor_tensor(csum[:, :], c["mem"][:, m, 0:HD], c["mem"][:, m, HD:2 * HD], ALU.add))
                link(dve.tensor_tensor(csum2[:, :], csum[:, :], c["mem"][:, m, 2 * HD:3 * HD], ALU.add))
                link(dve.tensor_tensor(csum[:, :], csum2[:, :], c["mem"][:, m, 3 * HD:4 * HD], ALU.add))
                link(dve.tensor_tensor(
                    coarse_bd[:, m, 0:P].rearrange("p (h e) -> p h e", e=HD),
                    csum[:, :].unsqueeze(1).broadcast_to([P, HH, HD]),
                    c["same_head"][:, :].unsqueeze(2).broadcast_to([P, HH, HD]), ALU.mult))
                link(dve.tensor_reduce(nc_sum[:, m:m + 1], c["norms"][:, m, :], AX.X, ALU.add))
                link(dve.tensor_scalar(coarse_bd[:, m, P + NM * HH:P + (NM + 1) * HH], c["same_head"][:, :],
                                       nc_sum[:, m:m + 1], None, ALU.mult))
            dve.wait_ge(s_nsum, 1)
            link(dve.tensor_copy(nsum[:, 0:NM], ring[NR - 1][:, 0:NM]))
            link(dve.tensor_reduce(nsum[:, NM:NM + 1], nsum[:, 0:NM], AX.X, ALU.add))
            dve.tensor_scalar(alive[:, :], nsum[:, :], EPS, None, ALU.is_ge).then_inc(s_pro, 1)
            dve.wait_ge(s_pro, 1)

            def walk(b, items):
                link, links = chain(dve, s_dve, b * DVE_LINKS)
                for what, off, n, j in items:
                    bb, t = b + off, n
                    if what in ("v", "coarseT", "keys", "hidden", "outT"):
                        continue
                    ps = bank(what, n, j) if what != "weights" else None
                    if what == "xT":
                        sup = slice(n * ST, (n + 1) * ST)
                        dve.wait_ge(s_xh, bb * NS * KC + n * KC + j + 1)
                        dve.tensor_tensor(xT[1][:, j, sup], ps[:, :], xT[0][:, j, sup].bitcast(F32),
                                          ALU.subtract).then_inc(s_xl, 1)
                    elif what in ("q", "k"):
                        i = elu_turn[(what, n, j)]
                        dve.wait_ge(s_elu, bb * len(elus) + i + 1)
                        sup = slice(n * ST, (n + 1) * ST)
                        if what == "q":
                            dve.scalar_tensor_tensor(sqT[:, j, sup], elu_e[:, i % 2, :], 1.0, elu_r[:, i % 2, :],
                                                     ALU.min, ALU.add, accum_out=qsum[:, j, n:n + 1]
                                                     ).then_inc(s_sq, 1)
                            dve.wait_ge(s_sq, bb * NS * KC + n * KC + j + 1)
                        else:
                            dve.scalar_tensor_tensor(skT[:, j, sup], elu_e[:, i % 2, :], 1.0, elu_r[:, i % 2, :],
                                                     ALU.min, ALU.add).then_inc(s_sk, 1)
                            dve.wait_ge(s_sk, bb * NS * KC + n * KC + j + 1)
                        dve.sem_inc(s_elu_used, 1)
                        if (what, n, j) == ("q", NS - 1, KC - 1):
                            link(dve.tensor_tensor(qtot[:, :], qsum[:, :, 0], qsum[:, :, 1], ALU.add))
                            for m in range(KC):
                                ins = dve.tensor_scalar(qmean[:, m, :], ones[:, :], qtot[:, m:m + 1], 1.0 / SEQ,
                                                        ALU.mult, ALU.mult)
                            ins.then_inc(s_qmean, 1)
                    elif what == "mean":
                        by_memory = mw[:, :, :, :].rearrange("p k n h -> p k h n")
                        dve.wait_ge(ready["mean"], b + 1)
                        dve.tensor_copy(mw[:, :, :, :].rearrange("p k n h -> p (k n h)"),
                                        ps[:, 0:KC * NM * HH]).then_inc(s_mean, 1)
                        dve.wait_ge(s_mean, b + 1)
                        link(dve.tensor_reduce(mw_m[:, 0, :, :], by_memory, AX.X, ALU.max))
                        dve.tensor_tensor(mw[:, :, :, :], mw[:, :, :, :],
                                          mw_m[:, 0, :, :].unsqueeze(2).broadcast_to([P, KC, NM, HH]),
                                          ALU.subtract).then_inc(s_mx, 1)
                    elif what == "weights":
                        dve.wait_ge(s_mexp, b + 1)
                        link(dve.tensor_reduce(mw_m[:, 0, :, :], by_memory, AX.X, ALU.add))
                        link(dve.reciprocal(mw_m[:, 1, :, :], mw_m[:, 0, :, :]))
                        link(dve.tensor_tensor(mw_m[:, 0, :, :], mw_m[:, 1, :, :],
                                               gate[:, :].rearrange("p (k h) -> p k h", k=KC), ALU.mult))
                        link(dve.tensor_tensor(mw[:, :, :, :], mw[:, :, :, :],
                                               mw_m[:, 0, :, :].unsqueeze(2).broadcast_to([P, KC, NM, HH]),
                                               ALU.mult))
                        link(dve.tensor_tensor(mw[:, :, :, :], mw[:, :, :, :],
                                               alive[:, 0:NM].unsqueeze(1).unsqueeze(3)
                                               .broadcast_to([P, KC, NM, HH]), ALU.mult))
                    elif what == "norms":
                        dve.wait_ge(ready["scores"], b * 4 * NT + 4 * t)
                        if t % TS == 0:
                            dve.wait_ge(s_sq, b * NS * KC + (t // TS + 1) * KC)
                        for par in range(2):
                            ins = dve.tensor_scalar(qm[:, :, par, :], sqT[:, :, t * P:(t + 1) * P],
                                                    c["parity"][:, par:par + 1], None, ALU.mult)
                        ins.then_inc(s_qm, 1)
                        dve.wait_ge(ready["norms"], b * NT + t + 1)
                        both = ps[:, 0:KC * WN].rearrange("p (k w) -> p k w", k=KC)
                        link(dve.tensor_scalar(rn[:, :, :, :].rearrange("p k n h -> p k (n h)"),
                                               both[:, :, P:], EPS, None, ALU.max))
                        link(dve.reciprocal(rn[:, :, :, :], rn[:, :, :, :]))
                        link(dve.tensor_scalar(rn[:, :, NM, :], rn[:, :, NM, :], alive[:, NM:NM + 1],
                                               None, ALU.mult))
                        dve.wait_ge(ready["coarseT"], b * NT + t)
                        dve.tensor_tensor(coarse[:, :].rearrange("p (k h e) -> p k h e", k=KC, e=HD),
                                          both[:, :, 0:P].rearrange("p k (h e) -> p k h e", e=HD),
                                          rn[:, :, NM, :].unsqueeze(3).broadcast_to([P, KC, HH, HD]),
                                          ALU.mult).then_inc(s_coarse, 1)
                    elif what == "scores":
                        dve.wait_ge(ready["scores"], b * 4 * NT + 4 * t + j + 1)
                        dve.wait_ge(ready["local"], b * NT + t)
                        dve.tensor_tensor(probs[:, j, :, :], ps[:, :].rearrange("p (h i) -> p h i", i=P),
                                          c["causal"][:, :].unsqueeze(1).broadcast_to([P, 4, P]),
                                          ALU.mult).then_inc(s_probs, 1)
                    elif what == "local":
                        heads = ps[:, 0:NH * HE].rearrange("p (h e) -> p h e", e=HE)
                        dve.wait_ge(ready["local"], b * NT + t + 1)
                        link(dve.tensor_scalar(den[:, :], heads[:, :, HD], EPS, None, ALU.max))
                        link(dve.reciprocal(den[:, :], den[:, :]))
                        link(dve.tensor_tensor(den[:, :], den[:, :], keep[:, :], ALU.mult))
                        dve.tensor_tensor(local[:, :].rearrange("p (h e) -> p h e", e=HD), heads[:, :, 0:HD],
                                          den[:, :].unsqueeze(2).broadcast_to([P, NH, HD]),
                                          ALU.mult).then_inc(s_local, 1)
                    elif what == "gate":
                        dve.wait_ge(s_e, b * NT + t + 1)
                        dve.tensor_scalar(e_t[:, 1:2], e_t[:, 0:1], 0.5, 0.5, ALU.mult, ALU.add)
                        link(dve.tensor_scalar(e_t[:, 2:3], e_t[:, 0:1], -0.5, 0.5, ALU.mult, ALU.add))
                        dve.scalar_tensor_tensor(coef[:, :, :, :].rearrange("p k n h -> p k (n h)"),
                                                 rn[:, :, 0:NM, :].rearrange("p k n h -> p k (n h)"),
                                                 e_t[:, 1:2], mw[:, :, :, :].rearrange("p k n h -> p k (n h)"),
                                                 ALU.mult, ALU.mult)
                        link(dve.tensor_scalar(coef_c[:, :], gate[:, :], e_t[:, 2:3], None, ALU.mult))
                        dve.wait_ge(s_att, b * NT + t)
                        link(dve.tensor_tensor(rest[:, :].rearrange("p (h e) -> p h e", e=HD),
                                               coarse[:, :].rearrange("p (h e) -> p h e", e=HD),
                                               coef_c[:, :].unsqueeze(2).broadcast_to([P, NH, HD]), ALU.mult))
                        dve.wait_ge(s_local, b * NT + t + 1)
                        dve.tensor_tensor(rest[:, :], rest[:, :], local[:, :], ALU.add).then_inc(s_rest, 1)
                    elif what == "state":
                        dve.wait_ge(ready["state"], b * (NT - 1) + t + 1)
                        kv = kvm if t else state
                        if t == 0:
                            dve.wait_ge(ready["local"], b * NT)
                        else:
                            dve.wait_ge(ready["local"], b * NT + t + 1)
                        ins = dve.tensor_tensor(kv[:, :, :].rearrange("p k (h e) -> p k h e", e=HE),
                                                ps[:, 0:KC * HH * HE].rearrange("p (k h e) -> p k h e", k=KC, e=HE),
                                                c["same_head"][:, :].unsqueeze(1).unsqueeze(3)
                                                .broadcast_to([P, KC, HH, HE]), ALU.mult)
                        ins.then_inc(s_kvm, 1)
                        dve.wait_ge(s_kvm, b * (NT - 1) + t + 1)
                        if t:
                            dve.tensor_tensor(state[:, :, :], state[:, :, :], kvm[:, :, :],
                                              ALU.add).then_inc(s_state, 1)
                        else:
                            dve.sem_inc(s_state, 1)
                    elif what == "fine":
                        dve.wait_ge(ready["fine"], b * KC * NT + KC * t + j + 1)
                        if j == 0:
                            dve.wait_ge(s_att, b * NT + t)
                        dve.tensor_tensor(prod[:, j, :, :].rearrange("p n (h e) -> p (n h) e", e=HD),
                                          ps[:, :].rearrange("p (m e) -> p m e", e=HD),
                                          coef[:, j, :, :].rearrange("p n h -> p (n h)").unsqueeze(2)
                                          .broadcast_to([P, NM * HH, HD]), ALU.mult).then_inc(s_prod, 1)
                    elif what == "oproj":
                        dve.wait_ge(ready["oproj"], b * NT + t + 1)
                        dve.wait_ge(s_ysum, b * NT + t + 1)
                        dve.tensor_tensor(total[:, t, :], ps[:, 0:H], total[:, t, :], ALU.add).then_inc(s_sum, 1)
                assert items is first or links[0] == DVE_LINKS, links[0]

            over_batches(dve, walk)

        @block.gpsimd
        def _(pool):
            for signal, count in per_batch + [(s_elu_used, 2 * NS * KC)]:
                pool.sem_inc(signal, count)

            def walk(b, items):
                if items is first:
                    return
                link, links = chain(pool, s_pool, b * POOL_LINKS)
                pool.wait_ge(s_ga, (b - 1) * 16 * TOP * NT)
                pool.wait_ge(s_yc, b * NT)
                link(pool.tensor_copy(from_b[:, :, :], c["from"][:, :, bass.ds((b - 1) * NT, NT)]))
                pool.tensor_copy(cw_b[:, :, :], c["cw"][:, :, bass.ds((b - 1) * NT, NT)]).then_inc(s_fb, 1)

                def fetch(t):
                    if t % 4 == 0:
                        pool.wait_ge(s_tick, b * 2 + t // 4)
                        pool.tensor_tensor(tick_a[:, :], c["lane"][:, :], c["lane"][:, :],
                                           ALU.add).then_inc(s_tick, 1)
                    for k in range(TOP):
                        pool.indirect_dma_start(
                            yg[t % 4][:, k, :], None, d["grouped_y"],
                            bass.IndirectOffsetOnAxis(ap=from_b[:, k, t:t + 1], axis=0)).then_inc(s_ga, 16)

                pool.wait_ge(s_ysum, b * NT)
                for t in range(4):
                    fetch(t)
                for what, _, t, j in items:
                    if what == "coarseT":
                        pool.wait_ge(s_bx, b * 16 + 16)
                        pool.wait_ge(s_yc, b * NT + t + 1)
                        link(pool.tensor_tensor(yg[t % 4][:, 0, :], yg[t % 4][:, 0, :], yg[t % 4][:, 1, :], ALU.add))
                        pool.tensor_tensor(total[:, t, :], total[:, t, :], yg[t % 4][:, 0, :],
                                           ALU.add).then_inc(s_ysum, 1)
                        if t == 3:
                            pool.wait_ge(s_ysum, b * NT + t + 1)
                            for k in range(4, NT):
                                fetch(k)
                    elif what == "fine" and j == KC - 1:
                        pool.wait_ge(s_prod, b * KC * NT + KC * (t + 1))
                        pool.wait_ge(s_rest, b * NT + t + 1)
                        link(pool.tensor_tensor(part[:, :, :, :], prod[:, :, 0:2, :], prod[:, :, 2:4, :], ALU.add))
                        pool.wait_ge(ready["outT"], b * NT + t)
                        link(pool.tensor_tensor(att[:, :].rearrange("p (k n) -> p k n", k=KC),
                                                part[:, :, 0, :], part[:, :, 1, :], ALU.add))
                        pool.tensor_tensor(att[:, :], att[:, :], rest[:, :], ALU.add).then_inc(s_att, 1)
                assert links[0] == POOL_LINKS, links[0]

            over_batches(pool, walk)


def build(nc, d):
    with ExitStack() as scope:
        sb, _, sem = places(nc, scope)
        c = {name: sb(name, list(shape)) for name, shape in (
            ("ident", (P, P)), ("before", (P, P)), ("causal", (P, P)), ("parity", (P, 2)),
            ("same_head", (P, HH)), ("rank_e", (P, E)), ("region", (P, E)), ("blk_row", (P, NI)),
            ("lane", (P, 1)), ("wo", (P, KC, H)), ("w1", (P, KC, G1)), ("b1", (G1, 1)), ("w2", (G1, 1)),
            ("b2", (P, 1)), ("gate", (P, NH)), ("mem", (P, KC, NM * HD)), ("norms", (P, KC, NM)))}
        c["number"] = sb("number", [P, NTA], I32)
        loads = []
        for name, t in c.items():
            if len(t.shape) == 3:
                loads.append((t[:, :, :], d[name].rearrange("(k p) n -> p k n", p=P)))
            else:
                loads.append((t[:, :], d[name]))
        c["loads"], c["n_load"], c["s_load"] = loads, len(loads), sem("c_load")
        c["picks"], c["dist"] = sb("picks", [P, TOP, NTA, E]), sb("dist", [P, NTA, E])
        c["slots"], c["run"] = sb("slots", [P, TOP, NTA]), sb("run", [P, E])
        c["from"], c["cw"] = sb("from_row", [P, TOP, NTA], I32), sb("cw", [P, TOP, NTA])
        c["start"], c["pack"] = sb("start_i", [P, NI], I32), sb("pack_i", [P, NI // UNROLL], I32)
        w = {"wb": [sb(f"wb{i}", [P, WUP + WQKV], F32R) for i in range(2)],
             "wd": [sb(f"wd{i}", [FC, E * 2 * H], F32R) for i in range(2)]}
        tokens_phase(nc, d, c, w)
        experts_phase(nc, d, c, w)
        attention_phase(nc, d, c, w)


def kernel(**inputs):
    import concourse.bacc as _bacc
    from concourse.bass_utils import run_bass_kernel_spmd as _run

    a = {k: np.asarray(v) for k, v in inputs.items()}
    part = np.arange(P)

    def chunks(x):
        return np.stack([x[k * P:(k + 1) * P] for k in range(KC)], 1)

    gate_up = np.concatenate([a["L0_ffn_w_gate"], a["L0_ffn_w_up"]], 1)
    qkv = np.concatenate([a["L0_attn_w_q"], a["L0_attn_w_k"], a["L0_attn_w_v"]])
    arrays = {
        "x_tok": a["L0_attn_hidden_states"].reshape(T, H),
        "w_all": np.concatenate([chunks(gate_up.transpose(2, 0, 1)).reshape(P, WUP),
                                 chunks(qkv.T).reshape(P, WQKV)], 1),
        "wd_all": a["L0_ffn_w_down"].transpose(0, 2, 1).reshape(E, 2, FC, H).transpose(2, 0, 1, 3)
                  .reshape(FC, E * 2 * H),
        "sg_t": np.concatenate([a["L0_ffn_sw_gate"], a["L0_ffn_gate_weight"]]).T,
        "su_t": a["L0_ffn_sw_up"].T,
        "sd_t": a["L0_ffn_sw_down"].T,
        "wo": a["L0_attn_w_o"].T,
        "w1": a["L0_attn_eg_w1"].T,
        "b1": a["L0_attn_eg_b1"].reshape(G1, 1),
        "w2": a["L0_attn_eg_w2"].T,
        "b2": np.broadcast_to(a["L0_attn_eg_b2"].reshape(1, 1), (P, 1)),
        "gate": np.broadcast_to(a["L0_attn_memory_gate"].reshape(1, NH), (P, NH)),
        "mem": a["L0_attn_fine_memories"].transpose(1, 2, 0, 3).reshape(H, NM * HD),
        "norms": a["L0_attn_fine_memory_norms"].transpose(1, 2, 0).reshape(H, NM),
        "ident": np.eye(P, dtype=np.float32),
        "before": np.triu(np.ones((P, P), np.float32), 1),
        "causal": np.triu(np.ones((P, P), np.float32)),
        "parity": np.stack([part // HD % 2 == 0, part // HD % 2 == 1], 1).astype(np.float32),
        "same_head": (part[:, None] // HD == np.arange(HH)[None, :]).astype(np.float32),
        "rank_e": np.broadcast_to(np.arange(E, 0, -1).astype(np.float32), (P, E)),
        "region": np.broadcast_to((np.arange(E) * T).astype(np.float32), (P, E)),
        "blk_row": np.broadcast_to(np.arange(NI).astype(np.float32), (P, NI)),
        "number": (np.arange(NTA)[None, :] * P + part[:, None]).astype(np.int32),
        "lane": part.astype(np.float32).reshape(P, 1),
    }
    nc = _bacc.Bacc("TRN2", target_bir_lowering=False, num_devices=1)
    arrays = {k: np.ascontiguousarray(v) for k, v in arrays.items()}
    d = {k: nc.dram_tensor("in_" + k, v.shape, mybir.dt.from_np(v.dtype), kind="ExternalInput").ap()
         for k, v in arrays.items()}
    d["lists"] = nc.dram_tensor("d_lists", (E * T, 1), I32, kind="Internal").ap()
    for name, rows in (("xn", T), ("base", T), ("grouped_y", (SLOTS + 1) * P)):
        d[name] = nc.dram_tensor("d_" + name, (rows, H), F32, kind="Internal").ap()
    d["out"] = nc.dram_tensor("out", (T, H), F32, kind="ExternalOutput").ap()
    build(nc, d)
    r = _run(nc, [{"in_" + k: v for k, v in arrays.items()}], core_ids=[0])
    return r.results[0]["out"].reshape(B, SEQ, H)
```

```python
import numpy as np

import concourse.bass as bass
from concourse import mybir
from contextlib import ExitStack

F32 = mybir.dt.float32
F32R = mybir.dt.float32r
BF16 = mybir.dt.bfloat16
I32 = mybir.dt.int32
ALU = mybir.AluOpType
ACT = mybir.ActivationFunctionType
AX = mybir.AxisListType

P = 128
B, SEQ, H = 4, 1024, 256
T = B * SEQ
NTA = T // P
NT = SEQ // P
NS = 2
ST = SEQ // NS
TS = ST // P
KC = H // P
NH, HD, NM = 16, 16, 4
HH = NH // KC
HE = HD + 1
E, F, FS = 8, 176, 352
TOP = 2
FC = F // 2
G1 = H // 4
EPS = 1e-6
LN_EPS = 1e-5
NP = NH // 2
PP = NP // KC
MV = NM * (HD + 1) + HE
CF = NM * 2 * HD
CC = CF + 2 * HD
WN = CC + 2 * (NM + 1)
BP = 512 // WN
NB3 = -(-NP // BP)

SF = (P, P, FS - 2 * P)
SF_ORDER = (2, 0, 1)
NBLK = TOP * T // P + E - 1
UNROLL = 4
SLOTS = -(-(NBLK + 1) // UNROLL) * UNROLL
NI = SLOTS + 8

WUP = KC * E * 2 * F
WQKV = KC * 3 * H
W_PIECE, Q_PIECE = WUP // B, WQKV // B
D_PIECE = E * 2 * H // B


def places(nc, scope):
    def sb(name, shape, dt=F32):
        return scope.enter_context(nc.sbuf_tensor(name, shape, dt))

    def bank(name):
        return scope.enter_context(nc.psum_tensor(name, [P, 512], F32))

    def sem(name):
        return scope.enter_context(nc.semaphore(name))

    return sb, bank, sem


def three(pe, out, a, b, start, stop):
    pe.matmul(out, a[0], b[0], start=start, stop=False)
    pe.matmul(out, a[0], b[1], start=False, stop=False)
    return pe.matmul(out, a[1], b[0], start=False, stop=stop)


def chain(eng, done, before=0):
    links = [0]

    def link(ins):
        links[0] += 1
        ins.then_inc(done, 1)
        eng.wait_ge(done, before + links[0])

    return link, links


TOKEN_LINKS = 15


def tokens_phase(nc, d, c, w):
    with ExitStack() as scope:
        sb, bank, sem = places(nc, scope)
        x_in = [sb(f"x_in{u}", [P, NT, H]) for u in range(2)]
        xn = [sb(f"xn{u}", [P, NT, H]) for u in range(2)]
        xT = [sb(f"xT{i}", [P, KC, SEQ], F32R) for i in range(2)]
        sg = [sb(f"sg{i}", [P, KC, FS + E], F32R) for i in range(2)]
        su = [sb(f"su{i}", [P, KC, FS], F32R) for i in range(2)]
        sd = [sb(f"sd{i}", [P, len(SF), H], F32R) for i in range(2)]
        stage_w = sb("stage_w", [P, W_PIECE + Q_PIECE])
        stage_d = sb("stage_d", [FC, D_PIECE])
        silu = sb("silu1", [P, 2, ST])
        hf = sb("hf", [P, 2, ST])
        hT = [sb(f"hT{i}", [P, len(SF), ST], F32R) for i in range(2)]
        base_sb = c["x_in"][:, :, :].rearrange("p (s t) c -> p s t c", s=NS)
        logitT = sb("logitT", [P, ST])
        stats = sb("stats", [P, NT, 6])
        meanvar = sb("meanvar", [P, NT, 2])
        tick, tick_p, tick_s = sb("tick", [P, 1]), sb("tick_p", [P, 1]), sb("tick_s1", [P, 1])
        ln_eps, half_neg, neg = sb("ln_eps", [P, NT]), sb("half_neg", [P, NT]), sb("neg", [P, NT])
        varp, rstd, shift = sb("varp", [P, NT]), sb("rstd", [P, NT]), sb("shift", [P, NT])
        logit = sb("logit", [P, NT, E])
        r_b, r_c = sb("r_b", [P, NT, E]), sb("r_c", [P, NT, E])
        r_s = sb("r_s", [P, TOP, NT, E])
        r_m = sb("r_m", [P, 4, NT])
        mask = sb("mask", [P, NT + 1, E], BF16)
        ones_bf, before_bf = sb("ones_bf", [P, P], BF16), sb("before_bf", [P, P], BF16)
        pos = sb("pos", [P, NT, E])
        slot_f = sb("slot_f", [P, TOP, NT])
        number = [sb(f"number{u}", [P, NT], I32) for u in range(2)]
        zeros = sb("zeros", [P, E * T // P], I32)
        slot_i = [sb(f"slot_i{u}", [P, TOP, NT], I32) for u in range(2)]

        count_i = sb("count_i", [P, E], I32)

        taken = {"x": 0, "w": 0}
        old = {"x": x_in[1][:, :, :].rearrange("p t n -> p (t n)"), "w": stage_w[:, :]}

        def carve(buffer, n, m=None):
            size = n * (m or 1)
            part = old[buffer][:, taken[buffer]:taken[buffer] + size]
            taken[buffer] += size
            return part if m is None else part.rearrange("p (n m) -> p n m", m=m)

        ge, oh, tmp = (carve("x", NI, E) for _ in range(3))
        count_f, last1 = carve("w", E), carve("w", 1)
        first = carve("w", E + 1)
        blk = carve("w", NI)
        blk_first, blk_e, start = (carve("w", NI) for _ in range(3))
        e_f, pack = carve("w", NI + 2), carve("w", NI // UNROLL)
        shift_e, moved_s = carve("w", E), carve("w", TOP * NTA)
        z = carve("w", 4, NTA)
        ex = carve("w", NTA, E)
        exs = silu[:, 0, 0:TOP * NTA * E].rearrange("p (k t e) -> p k t e", k=TOP, e=E)
        moved = hf[:, 0, 0:TOP * NTA * E].rearrange("p (t e) -> p t e", e=E)

        ps_a = [bank(f"t_a{i}") for i in range(2)]
        ps_g = [bank(f"t_g{i}") for i in range(2)]
        ps_u = [bank(f"t_u{i}") for i in range(2)]
        ps_y = [bank(f"t_y{i}") for i in range(2)]

        s_const, s_sw, s_swh, s_swl, s_pro = (
            sem("t_const"), sem("t_sw"), sem("t_swh"), sem("t_swl"), sem("t_pro"))
        s_stage, s_tick, s_zero, s_listed, s_neg = (
            sem("t_stage"), sem("t_tick"), sem("t_zero"), sem("t_listed"), sem("t_neg"))
        s_x, s_xst, s_sc = ([sem(f"t_{n}{u}") for u in range(2)] for n in ("x", "xst", "sc"))
        s_bst = [sem(f"t_bst{s}") for s in range(NS)]
        s_st, s_mv, s_rstd, s_xn = sem("t_st"), sem("t_mv"), sem("t_rstd"), sem("t_xn")
        s_xT, s_xh, s_xl = sem("t_xT"), sem("t_xh"), sem("t_xl")
        s_g, s_u, s_silu, s_gu, s_hh, s_hl, s_y, s_base = (
            sem("t_g"), sem("t_u"), sem("t_silu"), sem("t_gu"), sem("t_hh"), sem("t_hl"), sem("t_y"),
            sem("t_base"))
        s_lgT, s_lg, s_mask, s_pre, s_pos, s_slot = (
            sem("t_lgT"), sem("t_lg"), sem("t_mask"), sem("t_pre"), sem("t_pos"), sem("t_slot"))
        s_tab, s_exp = sem("t_tab"), sem("t_exp")
        s_wh, s_wl, s_dve, s_pool = sem("t_wh"), sem("t_wl"), sem("t_dve"), sem("t_pool")
        POOL_LINKS = 3

        NB = NS * len(SF)
        per_batch = [
            (s_stage, 48), (s_bst[0], 16), (s_bst[1], 16), (s_mv, 1),
            (s_rstd, 1), (s_xn, NT), (s_xT, NS * KC), (s_xh, NS * KC), (s_xl, NS * KC), (s_g, NB),
            (s_u, NB), (s_silu, NB), (s_gu, NB), (s_hh, NB), (s_hl, NB), (s_y, 2 * NS), (s_base, 2 * NS),
            (s_lgT, NS), (s_lg, NS), (s_mask, 1), (s_pre, 1), (s_pos, 1), (s_slot, 1), (s_wh, 3),
            (s_wl, 3), (s_st, 1), (s_tick, 1), (s_dve, TOKEN_LINKS), (s_pool, POOL_LINKS)]
        per_pass = [(s[u], n) for s, n in ((s_x, 16), (s_xst, 16)) for u in range(2)]

        flat = [xn[u][:, :, :].rearrange("p t n -> p (t n)") for u in range(2)]
        n_g, n_u = KC * (FS + E), KC * FS
        st_g = flat[0][:, 0:n_g].rearrange("p (k n) -> p k n", k=KC)
        st_u = flat[0][:, n_g:n_g + n_u].rearrange("p (k n) -> p k n", k=KC)
        st_d = flat[1][:, 0:len(SF) * H].rearrange("p (f n) -> p f n", f=len(SF))
        shared = [(st_g, [t[:, :, :] for t in sg]), (st_u, [t[:, :, :] for t in su]),
                  (st_d[:, 0:2, :], [t[:, 0:2, :] for t in sd]),
                  (st_d[0:SF[2], 2, :], [t[0:SF[2], 2, :] for t in sd])]

        pieces = (("wb", stage_w[:, 0:W_PIECE], W_PIECE), ("wqkv", stage_w[:, W_PIECE:], Q_PIECE),
                  ("wd", stage_d[:, :], D_PIECE))
        x_tok = d["x_tok"].rearrange("(b t p) c -> b p t c", t=NT, p=P)
        xn_d = d["xn"].rearrange("(b t p) c -> b p t c", t=NT, p=P)
        base_d = d["base"].rearrange("(s t p) c -> s p t c", t=TS, p=P)

        block = scope.enter_context(nc.Block())

        @block.sync
        def _(sp):
            def tokens(u, index):
                sp.dma_start(x_in[u][:, :, :], x_tok[bass.ds(index, 1), :, :, :]
                             .rearrange("b p t c -> p (b t) c")).then_inc(s_x[u], 16)

            sp.wait_ge(s_x[0], 16)
            tokens(0, 0)
            sp.dma_start(st_g, d["sg_t"].rearrange("(k p) n -> p k n", p=P)).then_inc(s_sw, 16)
            sp.dma_start(st_u, d["su_t"].rearrange("(k p) n -> p k n", p=P)).then_inc(s_sw, 16)
            sp.dma_start(st_d[:, 0:2, :], d["sd_t"][0:2 * P, :].rearrange("(f p) n -> p f n", p=P)
                         ).then_inc(s_sw, 16)
            sp.dma_start(st_d[0:SF[2], 2, :], d["sd_t"][2 * P:FS, :]).then_inc(s_sw, 16)
            sp.wait_ge(s_zero, 1)
            sp.dma_start(d["lists"].rearrange("(p n) c -> p (n c)", p=P), zeros[:, :]).then_inc(s_listed, 16)
            with sp.Fori(0, B // 2) as it:
                for u in range(2):
                    b = it * 2 + (2 + u)
                    sp.wait_ge(s_base, b * 2 * NS)
                    tokens(1 - u, (b - 1) % B)
                    sp.wait_ge(s_wl, b * 3)
                    sp.dma_start(stage_w[:, 0:W_PIECE], d["w_up"][:, bass.ds((b - 2) * W_PIECE, W_PIECE)]
                                 ).then_inc(s_stage, 16)
                    sp.dma_start(stage_w[:, W_PIECE:], d["w_qkv"][:, bass.ds((b - 2) * Q_PIECE, Q_PIECE)]
                                 ).then_inc(s_stage, 16)
                    sp.dma_start(stage_d[:, :], d["wd_all"][:, bass.ds((b - 2) * D_PIECE, D_PIECE)]
                                 ).then_inc(s_stage, 16)
                    sp.wait_ge(s_xn, b * NT + NT)
                    sp.dma_start(xn_d[bass.ds(b - 2, 1), :, :, :].rearrange("b p t c -> p (b t) c"),
                                 xn[u][:, :, :]).then_inc(s_xst[u], 16)
                    for s in range(NS):
                        sp.wait_ge(s_base, b * 2 * NS + 2 * (s + 1))
                        sp.dma_start(base_d[bass.ds((b - 2) * NS + s, 1), :, :, :]
                                     .rearrange("s p t c -> p (s t) c"), base_sb[:, s, :, :]
                                     ).then_inc(s_bst[s], 16)
            for u in range(2):
                sp.wait_ge(s_xst[u], (B // 2 + 1) * 16)
                sp.wait_ge(s_sc[u], B // 2 * 16 * TOP * NT)
            for s in range(NS):
                sp.wait_ge(s_bst[s], (B + 2) * 16)
            sp.wait_ge(c["s_load"], c["n_load"] * 16)

        @block.tensor
        def _(pe):
            pe.wait_ge(s_pro, 1)
            pe.wait_ge(s_swl, len(shared))
            pe.wait_ge(s_swh, len(shared))
            pe.wait_ge(c["s_load"], c["n_load"] * 16)
            with pe.Fori(0, B // 2) as it:
                for u in range(2):
                    b = it * 2 + (2 + u)
                    for s in range(NS):
                        pe.wait_ge(s_xn, b * NT + (s + 1) * TS)
                        for kc in range(KC):
                            if s:
                                pe.wait_ge(s_xl, b * NS * KC + kc + 1)
                            else:
                                pe.wait_ge(s_lg, b * NS)
                            for j in range(TS):
                                mm = pe.transpose(ps_a[kc][:, j * P:(j + 1) * P],
                                                  xn[u][:, s * TS + j, kc * P:(kc + 1) * P],
                                                  c["ident"][:, :])
                            mm.then_inc(s_xT, 1)

                    def hidden(k):
                        s, f = k // len(SF), SF_ORDER[k % len(SF)]
                        sup = slice(s * ST, (s + 1) * ST)
                        rows = SF[f] + (E if f == 2 else 0)
                        if k % len(SF) == 0:
                            pe.wait_ge(s_xl, b * NS * KC + (s + 1) * KC)
                        pe.wait_ge(s_silu, b * NB + k - 1)
                        if k == 0:
                            pe.wait_ge(s_pos, b)
                        for kc in range(KC):
                            mm = three(pe, ps_g[k % 2][0:rows, :],
                                       [sg[i][:, kc, f * P:f * P + rows] for i in range(2)],
                                       [xT[i][:, kc, sup] for i in range(2)], kc == 0, kc == KC - 1)
                        mm.then_inc(s_g, 1)
                        rows = SF[f]
                        pe.wait_ge(s_gu, b * NB + k - 1)
                        for kc in range(KC):
                            mm = three(pe, ps_u[k % 2][0:rows, :],
                                       [su[i][:, kc, f * P:f * P + rows] for i in range(2)],
                                       [xT[i][:, kc, sup] for i in range(2)], kc == 0, kc == KC - 1)
                        mm.then_inc(s_u, 1)

                    def logits(s):
                        pe.wait_ge(s_silu, b * NB + s * len(SF) + 1)
                        pe.wait_ge(s_xl, b * NS * KC + KC + s + 1)
                        if s:
                            pe.wait_ge(s_lg, b * NS + s)
                        for j in range(TS):
                            mm = pe.matmul(ps_a[s][:, j * E:(j + 1) * E],
                                           logitT[SF[2]:SF[2] + E, j * P:(j + 1) * P],
                                           c["ident"][SF[2]:SF[2] + E, SF[2]:SF[2] + E],
                                           start=True, stop=True)
                        mm.then_inc(s_lgT, 1)

                    def down(s):
                        pe.wait_ge(s_hl, b * NB + (s + 1) * len(SF))
                        for j in range(TS):
                            if j % 2 == 0:
                                pe.wait_ge(s_base, b * 2 * NS + 2 * s + j // 2 - 1)
                            for f in range(len(SF)):
                                mm = three(pe, ps_y[j // 2][:, (j % 2) * H:(j % 2 + 1) * H],
                                           [hT[i][0:SF[f], f, j * P:(j + 1) * P] for i in range(2)],
                                           [sd[i][0:SF[f], f, :] for i in range(2)],
                                           f == 0, f == len(SF) - 1)
                            if j % 2:
                                mm.then_inc(s_y, 1)

                    hidden(0)
                    hidden(1)
                    logits(0)
                    hidden(2)
                    hidden(3)
                    hidden(4)
                    logits(1)
                    down(0)
                    hidden(5)
                    down(1)
                    pe.wait_ge(s_mask, b + 1)
                    pe.wait_ge(s_silu, b * NB + NB)
                    pe.matmul(ps_g[0][:, 0:(NT + 1) * E], before_bf[:, :],
                              mask[:, :, :], start=True, stop=False)
                    for i in range(NT):
                        mm = pe.matmul(ps_g[0][:, (i + 1) * E:(NT + 1) * E], ones_bf[:, :],
                                       mask[:, i, :].unsqueeze(1).broadcast_to([P, NT - i, E]),
                                       start=False, stop=(i == NT - 1))
                    mm.then_inc(s_pre, 1)

        @block.scalar
        def _(act):
            for to, source in c["loads"]:
                act.dma_start(to, source).then_inc(c["s_load"], 16)
            act.wait_ge(s_sw, 64)
            act.wait_ge(c["s_load"], c["n_load"] * 16)
            for st, parts in shared:
                act.activation(parts[0], st, ACT.Copy).then_inc(s_swh, 1)
            act.wait_ge(s_swl, len(shared))

            def normed(b, u, stored):
                act.wait_ge(s_rstd, b + 1)
                act.wait_ge(s_xst[u], stored)
                for t in range(NT):
                    act.activation(xn[u][:, t, :], x_in[u][:, t, :], ACT.Identity,
                                   bias=shift[:, t:t + 1], scale=rstd[:, t:t + 1]).then_inc(s_xn, 1)

            act.activation(tick_s[:, :], c["lane"][:, :], ACT.Silu)
            normed(2, 0, 16)
            with act.Fori(0, B // 2) as it:
                for u in range(2):
                    b = it * 2 + (2 + u)
                    for s in range(NS):
                        for kc in range(KC):
                            act.wait_ge(s_xT, b * NS * KC + s * KC + kc + 1)
                            act.activation(xT[0][:, kc, s * ST:(s + 1) * ST], ps_a[kc][:, :],
                                           ACT.Copy).then_inc(s_xh, 1)

                    def silu_of(k):
                        s, f = k // len(SF), SF_ORDER[k % len(SF)]
                        act.wait_ge(s_g, b * NB + k + 1)
                        act.wait_ge(s_gu, b * NB + k - 1)
                        ins = act.activation(silu[0:SF[f], k % 2, :], ps_g[k % 2][0:SF[f], :], ACT.Silu)
                        if f == 2:
                            act.wait_ge(s_lgT, b * NS + s)
                            ins = act.activation(logitT[SF[2]:SF[2] + E, :],
                                                 ps_g[k % 2][SF[2]:SF[2] + E, :], ACT.Copy)
                        ins.then_inc(s_silu, 1)

                    def high(k):
                        s, f = k // len(SF), SF_ORDER[k % len(SF)]
                        act.wait_ge(s_gu, b * NB + k + 1)
                        act.wait_ge(s_y, b * 2 * NS + 2 * s)
                        act.activation(hT[0][0:SF[f], f, :], hf[0:SF[f], k % 2, :], ACT.Copy).then_inc(s_hh, 1)

                    def logits_out(s):
                        act.wait_ge(s_lgT, b * NS + s + 1)
                        act.wait_ge(s_slot, b)
                        act.activation(logit[:, s * TS:(s + 1) * TS, :],
                                       ps_a[s][:, 0:TS * E].rearrange("p (t e) -> p t e", e=E),
                                       ACT.Copy).then_inc(s_lg, 1)

                    silu_of(0)
                    silu_of(1)
                    high(0)
                    logits_out(0)
                    silu_of(2)
                    high(1)
                    silu_of(3)
                    high(2)
                    act.wait_ge(s_stage, b * 48 + 48)
                    for part, st, size in pieces:
                        act.activation(w[part][0][:, bass.ds((b - 2) * size, size)], st, ACT.Copy).then_inc(s_wh, 1)
                    silu_of(4)
                    logits_out(1)
                    high(3)
                    high(4)
                    silu_of(5)
                    high(5)
                    normed(b + 1, 1 - u, (it + 1 + u) * 16)

            act.wait_ge(s_slot, B + 2)
            act.wait_ge(s_wl, (B + 2) * 3)
            act.activation(ex[:, :, :], c["dist"][:, :, :], ACT.Exp).then_inc(s_exp, 1)

        @block.vector
        def _(dve):
            dve.memset(zeros[:, :], 0).then_inc(s_zero, 1)
            dve.memset(ones_bf[:, :], 1.0)
            dve.memset(mask[:, NT, :], 0.0)
            dve.memset(c["run"][:, :], 0.0)
            dve.memset(ln_eps[:, :], LN_EPS)
            dve.memset(neg[:, :], -1.0)
            dve.memset(half_neg[:, :], -0.5).then_inc(s_neg, 1)

            def norm_stats(b, u, loaded):
                dve.wait_ge(s_x[u], loaded)
                dve.wait_ge(s_xn, b * NT)
                for t in range(NT):
                    ins = dve.bn_stats(stats[:, t, :], x_in[u][:, t, :])
                ins.then_inc(s_st, 1)
                dve.wait_ge(s_st, b + 1)
                dve.memset(tick[:, :], 0.0)
                for t in range(NT):
                    ins = dve.bn_aggr(meanvar[:, t, :], stats[:, t, :])
                ins.then_inc(s_mv, 1)

            norm_stats(2, 0, 32)
            dve.wait_ge(c["s_load"], c["n_load"] * 16)
            dve.tensor_copy(before_bf[:, :], c["before"][:, :]).then_inc(s_pro, 1)
            for n, (st, parts) in enumerate(shared):
                dve.wait_ge(s_swh, n + 1)
                dve.tensor_tensor(parts[1], st, parts[0].bitcast(F32), ALU.subtract).then_inc(s_swl, 1)

            with dve.Fori(0, B // 2) as it:
                for u in range(2):
                    b = it * 2 + (2 + u)
                    link, links = chain(dve, s_dve, b * TOKEN_LINKS)
                    for s in range(NS):
                        for kc in range(KC):
                            sup = slice(s * ST, (s + 1) * ST)
                            dve.wait_ge(s_xh, b * NS * KC + s * KC + kc + 1)
                            dve.tensor_tensor(xT[1][:, kc, sup], ps_a[kc][:, :],
                                              xT[0][:, kc, sup].bitcast(F32), ALU.subtract).then_inc(s_xl, 1)

                    def rows_of(k):
                        f = SF_ORDER[k % len(SF)]
                        dve.wait_ge(s_silu, b * NB + k + 1)
                        dve.wait_ge(s_u, b * NB + k + 1)
                        dve.wait_ge(s_hl, b * NB + k - 1)
                        dve.tensor_tensor(hf[0:SF[f], k % 2, :], ps_u[k % 2][0:SF[f], :],
                                          silu[0:SF[f], k % 2, :], ALU.mult).then_inc(s_gu, 1)

                    def low(k):
                        f = SF_ORDER[k % len(SF)]
                        dve.wait_ge(s_hh, b * NB + k + 1)
                        dve.tensor_tensor(hT[1][0:SF[f], f, :], hf[0:SF[f], k % 2, :],
                                          hT[0][0:SF[f], f, :].bitcast(F32), ALU.subtract).then_inc(s_hl, 1)

                    def residual(s):
                        for j in range(2):
                            dve.wait_ge(s_y, b * 2 * NS + 2 * s + j + 1)
                            dve.wait_ge(s_bst[s], b * 16)
                            t = s * TS + 2 * j
                            dve.tensor_tensor(base_sb[:, s, 2 * j:2 * j + 2, :],
                                              ps_y[j][:, :].rearrange("p (t n) -> p t n", n=H),
                                              x_in[u][:, t:t + 2, :], ALU.add).then_inc(s_base, 1)

                    rows_of(0)
                    rows_of(1)
                    low(0)
                    norm_stats(b + 1, 1 - u, it * 16 + (32 + 16 * u))
                    for k in range(2, 5):
                        rows_of(k)
                        low(k - 1)
                    for n, (part, st, size) in enumerate(pieces):
                        at = bass.ds((b - 2) * size, size)
                        dve.wait_ge(s_wh, b * 3 + n + 1)
                        dve.tensor_tensor(w[part][1][:, at], st, w[part][0][:, at].bitcast(F32),
                                          ALU.subtract).then_inc(s_wl, 1)
                    low(4)
                    rows_of(5)
                    low(5)
                    residual(0)
                    def over_experts(x):
                        return x.unsqueeze(2).broadcast_to([P, NT, E])

                    by_rank = c["rank_e"][:, :].unsqueeze(1).broadcast_to([P, NT, E])
                    dve.wait_ge(s_lg, b * NS + NS)
                    link(dve.tensor_reduce(r_m[:, 0, :], logit[:, :, :], AX.X, ALU.max))
                    dve.tensor_tensor(c["dist"][:, bass.ds((b - 2) * NT, NT), :], logit[:, :, :],
                                      over_experts(r_m[:, 0, :]), ALU.subtract)
                    link(dve.tensor_tensor(r_b[:, :, :], logit[:, :, :], over_experts(r_m[:, 0, :]),
                                           ALU.is_equal))
                    link(dve.tensor_tensor(r_b[:, :, :], r_b[:, :, :], by_rank, ALU.mult))
                    link(dve.tensor_reduce(r_m[:, 1, :], r_b[:, :, :], AX.X, ALU.max))
                    link(dve.tensor_tensor(r_s[:, 0, :, :], r_b[:, :, :], over_experts(r_m[:, 1, :]),
                                           ALU.is_equal))
                    link(dve.scalar_tensor_tensor(r_b[:, :, :], r_s[:, 0, :, :], -3e38, logit[:, :, :],
                                                  ALU.mult, ALU.add))
                    link(dve.tensor_reduce(r_m[:, 2, :], r_b[:, :, :], AX.X, ALU.max))
                    link(dve.tensor_tensor(r_c[:, :, :], r_b[:, :, :], over_experts(r_m[:, 2, :]),
                                           ALU.is_equal))
                    link(dve.tensor_tensor(r_c[:, :, :], r_c[:, :, :], by_rank, ALU.mult))
                    link(dve.tensor_reduce(r_m[:, 3, :], r_c[:, :, :], AX.X, ALU.max))
                    link(dve.tensor_tensor(r_s[:, 1, :, :], r_c[:, :, :], over_experts(r_m[:, 3, :]),
                                           ALU.is_equal))
                    dve.tensor_tensor(mask[:, 0:NT, :], r_s[:, 0, :, :], r_s[:, 1, :, :],
                                      ALU.add).then_inc(s_mask, 1)
                    residual(1)
                    dve.wait_ge(s_pre, b + 1)
                    link(dve.tensor_tensor(pos[:, :, :], ps_g[0][:, 0:NT * E]
                                           .rearrange("p (t e) -> p t e", e=E),
                                           c["run"][:, :].unsqueeze(1).broadcast_to([P, NT, E]), ALU.add))
                    dve.tensor_tensor(c["run"][:, :], ps_g[0][:, NT * E:(NT + 1) * E], c["run"][:, :],
                                      ALU.add).then_inc(s_pos, 1)
                    link(dve.tensor_tensor(pos[:, :, :], pos[:, :, :],
                                           c["region"][:, :].unsqueeze(1).broadcast_to([P, NT, E]), ALU.add))
                    dve.tensor_tensor(r_b[:, :, :], r_s[:, 0, :, :], pos[:, :, :], ALU.mult)
                    link(dve.tensor_tensor(r_c[:, :, :], r_s[:, 1, :, :], pos[:, :, :], ALU.mult))
                    dve.tensor_reduce(slot_f[:, 0, :], r_b[:, :, :], AX.X, ALU.add)
                    link(dve.tensor_reduce(slot_f[:, 1, :], r_c[:, :, :], AX.X, ALU.add))
                    dve.tensor_copy(c["slots"][:, :, bass.ds((b - 2) * NT, NT)], slot_f[:, :, :])
                    for k in range(TOP):
                        dve.tensor_copy(c["picks"][:, k, bass.ds((b - 2) * NT, NT), :], r_s[:, k, :, :])
                    dve.wait_ge(s_sc[u], it * 16 * TOP * NT)
                    dve.tensor_copy(number[u][:, :], c["number"][:, bass.ds((b - 2) * NT, NT)])
                    dve.tensor_copy(slot_i[u][:, :, :], slot_f[:, :, :]).then_inc(s_slot, 1)
                    assert links[0] == TOKEN_LINKS, links[0]

            link, links = chain(dve, s_tab)
            dve.wait_ge(s_slot, B + 2)
            dve.wait_ge(s_base, (B + 2) * 2 * NS)
            dve.wait_ge(s_wl, (B + 2) * 3)
            dve.wait_ge(s_hl, (B + 2) * NB)
            def per_block(x):
                return x.unsqueeze(1).broadcast_to([P, NI, E])

            link(dve.tensor_scalar(count_f[:, :], c["run"][:, :], float(P - 1), None, ALU.add))
            link(dve.tensor_copy(count_i[:, :], count_f[:, :]))
            link(dve.tensor_scalar(count_i[:, :], count_i[:, :], 7, None, ALU.logical_shift_right))
            link(dve.tensor_copy(count_f[:, :], count_i[:, :]))
            link(dve.memset(first[:, 0:1], 0.0))
            for e in range(E):
                link(dve.tensor_tensor(first[:, e + 1:e + 2], first[:, e:e + 1], count_f[:, e:e + 1], ALU.add))
            link(dve.tensor_scalar(last1[:, :], first[:, E:E + 1], -1.0, None, ALU.add))
            link(dve.tensor_scalar(blk[:, :], c["blk_row"][:, :], last1[:, 0:1], None, ALU.min))
            link(dve.tensor_tensor(ge[:, :, :], blk[:, :].unsqueeze(2).broadcast_to([P, NI, E]),
                                   per_block(first[:, 0:E]), ALU.is_ge))
            dve.tensor_tensor(oh[:, :, 0:E - 1], ge[:, :, 0:E - 1], ge[:, :, 1:E], ALU.subtract)
            link(dve.tensor_copy(oh[:, :, E - 1:E], ge[:, :, E - 1:E]))
            link(dve.tensor_tensor(tmp[:, :, :], oh[:, :, :], per_block(first[:, 0:E]), ALU.mult))
            link(dve.tensor_reduce(blk_first[:, :], tmp[:, :, :], AX.X, ALU.add))
            link(dve.tensor_reduce(blk_e[:, :], ge[:, :, :], AX.X, ALU.add))
            link(dve.tensor_scalar(blk_e[:, :], blk_e[:, :], -1.0, None, ALU.add))
            link(dve.tensor_tensor(start[:, :], blk[:, :], blk_first[:, :], ALU.subtract))
            link(dve.tensor_scalar(start[:, :], start[:, :], float(P), None, ALU.mult))
            link(dve.scalar_tensor_tensor(start[:, :], blk_e[:, :], float(T), start[:, :], ALU.mult, ALU.add))
            link(dve.memset(e_f[:, 0:2], 0.0))
            link(dve.tensor_copy(e_f[:, 2:NI + 2], blk_e[:, :]))
            passes = NI // UNROLL
            digit = [e_f[:, j:j + (passes - 1) * UNROLL + 1:UNROLL] for j in range(UNROLL + 2)]
            link(dve.tensor_copy(pack[:, :], digit[UNROLL + 1]))
            for j in reversed(range(UNROLL + 1)):
                link(dve.scalar_tensor_tensor(pack[:, :], pack[:, :], float(E), digit[j], ALU.mult, ALU.add))
            link(dve.tensor_copy(c["pack"][:, :], pack[:, :]))
            link(dve.tensor_copy(c["start"][:, :], start[:, :]))
            link(dve.scalar_tensor_tensor(shift_e[:, :], first[:, 0:E], float(P), c["region"][:, :],
                                          ALU.mult, ALU.subtract))
            link(dve.tensor_tensor(moved[:, :, :], c["picks"][:, :, :, :].rearrange("p k t e -> p (k t) e"),
                                   shift_e[:, :].unsqueeze(1).broadcast_to([P, TOP * NTA, E]), ALU.mult))
            link(dve.tensor_reduce(moved_s[:, :], moved[:, :, :], AX.X, ALU.add))
            link(dve.tensor_tensor(moved_s[:, :], moved_s[:, :],
                                   c["slots"][:, :, :].rearrange("p k t -> p (k t)"), ALU.add))
            link(dve.tensor_scalar(moved_s[:, :], moved_s[:, :], float(2 * P), None, ALU.add))
            link(dve.tensor_copy(c["from"][:, :], moved_s[:, :]))
            dve.wait_ge(s_exp, 1)
            for k in range(TOP):
                link(dve.tensor_tensor(exs[:, k, :, :], c["picks"][:, k, :, :], ex[:, :, :], ALU.mult))
                link(dve.tensor_reduce(z[:, k, :], exs[:, k, :, :], AX.X, ALU.add))
            link(dve.tensor_reduce(z[:, 2, :], ex[:, :, :], AX.X, ALU.add))
            link(dve.tensor_tensor(z[:, 3, :], z[:, 0, :], z[:, 1, :], ALU.add))
            link(dve.scalar_tensor_tensor(z[:, 3, :], z[:, 2, :], 1e-20, z[:, 3, :], ALU.mult, ALU.add))
            link(dve.reciprocal(z[:, 2, :], z[:, 3, :]))
            for k in range(TOP):
                link(dve.tensor_tensor(c["cw"][:, k, :], z[:, k, :], z[:, 2, :], ALU.mult))

        @block.gpsimd
        def _(pool):
            for signal, count in per_batch:
                pool.sem_inc(signal, 2 * count)
            for signal, count in per_pass:
                pool.sem_inc(signal, count)
            pool.wait_ge(s_neg, 1)

            def scale_and_shift(b):
                link, links = chain(pool, s_pool, b * POOL_LINKS)
                pool.wait_ge(s_mv, b + 1)
                link(pool.tensor_tensor(varp[:, :], meanvar[:, :, 1], ln_eps[:, :], ALU.add))
                link(pool.tensor_tensor(rstd[:, :], varp[:, :], half_neg[:, :], ALU.pow))
                link(pool.tensor_tensor(shift[:, :], meanvar[:, :, 0], neg[:, :], ALU.mult))
                pool.tensor_tensor(shift[:, :], shift[:, :], rstd[:, :], ALU.mult).then_inc(s_rstd, 1)

            scale_and_shift(2)
            pool.wait_ge(s_listed, 16)
            with pool.Fori(0, B // 2) as it:
                for u in range(2):
                    b = it * 2 + (2 + u)
                    scale_and_shift(b + 1)
                    pool.wait_ge(s_slot, b + 1)
                    pool.wait_ge(c["s_load"], c["n_load"] * 16)
                    pool.wait_ge(s_tick, b)
                    pool.tensor_tensor(tick_p[:, :], c["lane"][:, :], c["lane"][:, :],
                                       ALU.add).then_inc(s_tick, 1)
                    for t in range(NT):
                        for k in range(TOP):
                            pool.indirect_dma_start(
                                d["lists"], bass.IndirectOffsetOnAxis(ap=slot_i[u][:, k, t:t + 1], axis=0),
                                number[u][:, t:t + 1], None).then_inc(s_sc[u], 16)



TABLE_LINKS = 0


def experts_phase(nc, d, c, w):
    with ExitStack() as scope:
        sb, bank, sem = places(nc, scope)
        xg = [sb(f"xg{i}", [P, H]) for i in range(UNROLL)]
        g_i = [sb(f"g_i{i}", [P, 1], I32) for i in range(UNROLL)]
        xb = [[sb(f"xb{q}{i}", [P, KC, P], F32R) for i in range(2)] for q in range(2)]
        silu = [sb(f"silu2{q}", [P, F]) for q in range(2)]
        h_sb = [sb(f"h_sb{q}", [P, F]) for q in range(2)]
        hb = [[sb(f"hb{q}{i}", [FC, 2, P], F32R) for i in range(2)] for q in range(2)]
        y_sb = [sb(f"y_sb{q}", [P, H]) for q in range(2)]

        ps_x = [bank(f"e_x{q}") for q in range(2)]
        ps_up = [bank(f"e_up{q}") for q in range(2)]
        ps_h = [bank(f"e_h{q}") for q in range(2)]
        ps_y = [bank(f"e_y{q}") for q in range(2)]

        s_tab, s_init = sem("e_tab"), sem("e_init")
        tick_s = sb("tick_s", [P, 1])
        tick_e = sb("tick_e", [P, 1])
        s_ga = [sem(f"e_ga{i}") for i in range(UNROLL)]
        s_tick = sem("e_tick")
        s_gi = [sem(f"e_gi{i}") for i in range(UNROLL)]
        s_xT, s_xh, s_xl = sem("e_xT"), sem("e_xh"), sem("e_xl")
        s_up, s_silu, s_h, s_hT, s_hh, s_hl = (
            sem("e_up"), sem("e_silu"), sem("e_h"), sem("e_hT"), sem("e_hh"), sem("e_hl"))
        s_dn, s_y, s_yst = sem("e_dn"), sem("e_y"), [sem(f"e_yst{q}") for q in range(2)]

        start_at = [(s_tick, 4), (s_xT, 4), (s_xh, 4), (s_xl, 4), (s_up, 4), (s_silu, 4), (s_h, 4),
                    (s_hT, 3), (s_hh, 3), (s_hl, 3), (s_dn, 2), (s_y, 2)]
        grouped_y = d["grouped_y"].rearrange("(i p) c -> i p c", p=P)

        block = scope.enter_context(nc.Block())

        @block.sync
        def _(sp):
            def numbers(j, buf):
                at = sp.value_load(c["start"][0:1, j], min_val=0, max_val=E * T - P)
                sp.dma_start(g_i[buf][:, :], d["lists"][bass.ds(at, P), :]).then_inc(s_gi[buf], 16)

            for j in range(UNROLL):
                numbers(slice(j, j + 1), j)
            for j in range(UNROLL, UNROLL + 2):
                sp.wait_ge(s_ga[j % UNROLL], 16)
                numbers(slice(j, j + 1), j % UNROLL)
            sp.dma_start(c["x_in"][:, :, :], d["xn"][0:NT * P, :].rearrange("(t p) c -> p t c", p=P)
                         ).then_inc(c["s_x"], 16)
            with sp.Fori(0, SLOTS // UNROLL) as it:
                for u in range(UNROLL):
                    n = it * UNROLL + (u + 4)
                    q = u % 2
                    sp.wait_ge(s_ga[(u + 2) % UNROLL], it * 16 + (16 if u < 2 else 32))
                    numbers(bass.ds(n + 2, 1), (u + 2) % UNROLL)
                    sp.wait_ge(s_y, n - 1)
                    sp.dma_start(grouped_y[bass.ds(n - 4, 1), :, :].rearrange("i p c -> p (i c)"),
                                 y_sb[q][:, :]).then_inc(s_yst[q], 16)
            sp.wait_ge(s_y, SLOTS + 3)
            sp.dma_start(grouped_y[SLOTS:SLOTS + 1, :, :].rearrange("i p c -> p (i c)"), y_sb[0][:, :]
                         ).then_inc(s_yst[0], 16)
            for q in range(2):
                sp.wait_ge(s_yst[q], 16 + 8 * SLOTS + (16 if q == 0 else 0))
            for i in range(UNROLL):
                sp.wait_ge(s_gi[i], 16 * (SLOTS // UNROLL + 1 + (i < 2)))

        @block.tensor
        def _(pe):
            def transposed(j_buf, q):
                for kc in range(KC):
                    mm = pe.transpose(ps_x[q][:, kc * P:(kc + 1) * P], xg[j_buf][:, kc * P:(kc + 1) * P],
                                      c["ident"][:, :])
                mm.then_inc(s_xT, 1)

            pe.wait_ge(s_init, 1)
            for j in range(2):
                pe.wait_ge(s_ga[j], 16)
                transposed(j, j)

            def down(at_dn, n, q):
                pe.wait_ge(s_hl, n - 1)
                pe.wait_ge(s_y, n - 3)
                for f in range(2):
                    cols = bass.ds(at_dn + f * H, H)
                    mm = three(pe, ps_y[q][:, 0:H], [hb[q][i][:, f, :] for i in range(2)],
                               [w["wd"][i][:, cols] for i in range(2)], f == 0, f == 1)
                mm.then_inc(s_dn, 1)

            with pe.Fori(0, SLOTS // UNROLL) as it:
                word = pe.value_load(c["pack"][0:1, bass.ds(it, 1)], min_val=0, max_val=E ** (UNROLL + 2) - 1)

                def columns(j):
                    expert = word // E ** (j + 2) % E
                    return expert * (2 * F), expert * (2 * H)

                at = [columns(-2), columns(-1), columns(0)]
                for u in range(UNROLL):
                    n = it * UNROLL + (u + 4)
                    q, o = u % 2, (u - 1) % 2
                    at_dn, at_up = at[u][1], at[u + 2][0]
                    pe.wait_ge(s_xl, n + 1)
                    pe.wait_ge(s_h, n - 1)
                    for kc in range(KC):
                        cols = bass.ds(at_up + kc * E * 2 * F, 2 * F)
                        mm = three(pe, ps_up[q][:, 0:2 * F], [xb[q][i][:, kc, :] for i in range(2)],
                                   [w["wb"][i][:, cols] for i in range(2)], kc == 0, kc == KC - 1)
                    mm.then_inc(s_up, 1)
                    if u < UNROLL - 1:
                        at.append(columns(u + 1))
                    pe.wait_ge(s_ga[(u + 2) % UNROLL], it * 16 + (16 if u < 2 else 32))
                    transposed((u + 2) % UNROLL, q)
                    down(at_dn, n, q)
                    pe.wait_ge(s_h, n)
                    for f in range(2):
                        mm = pe.transpose(ps_h[o][0:FC, f * P:(f + 1) * P], h_sb[o][:, f * FC:(f + 1) * FC],
                                          c["ident"][:, :])
                    mm.then_inc(s_hT, 1)
            word = pe.value_load(c["pack"][0:1, SLOTS // UNROLL:SLOTS // UNROLL + 1],
                                 min_val=0, max_val=E ** (UNROLL + 2) - 1)
            down(word % E * (2 * H), SLOTS + 4, 0)

        @block.scalar
        def _(act):
            def high_tokens(q):
                act.activation(xb[q][0][:, :, :], ps_x[q][:, 0:H].rearrange("p (k n) -> p k n", k=KC),
                               ACT.Copy).then_inc(s_xh, 1)

            act.activation(tick_s[:, :], c["lane"][:, :], ACT.Silu)
            for j in range(2):
                act.wait_ge(s_xT, 5 + j)
                high_tokens(j)
            with act.Fori(0, SLOTS // UNROLL) as it:
                for u in range(UNROLL):
                    n = it * UNROLL + (u + 4)
                    q, o = u % 2, (u - 1) % 2
                    act.wait_ge(s_up, n + 1)
                    act.activation(silu[q][:, :], ps_up[q][:, 0:F], ACT.Silu).then_inc(s_silu, 1)
                    act.wait_ge(s_xT, n + 3)
                    high_tokens(q)
                    act.wait_ge(s_hT, n)
                    act.wait_ge(s_dn, n - 2)
                    act.activation(hb[o][0][:, :, :], ps_h[o][0:FC, 0:2 * P].rearrange("p (k n) -> p k n", k=2),
                                   ACT.Copy).then_inc(s_hh, 1)

        @block.vector
        def _(dve):
            link, _ = chain(dve, s_tab)

            for q in range(2):
                link(dve.memset(h_sb[q][:, :], 0.0))
            for i in range(2):
                ins = (dve.tensor_scalar(hb[0][i][:, :, :], c["ident"][0:FC, :].unsqueeze(1).broadcast_to([FC, 2, P]),
                                       0.0, None, ALU.mult))
            ins.then_inc(s_init, 1)
            for j in range(2):
                dve.wait_ge(s_xh, 5 + j)
                dve.tensor_tensor(xb[j][1][:, :, :], ps_x[j][:, 0:H].rearrange("p (k n) -> p k n", k=KC),
                                  xb[j][0][:, :, :].bitcast(F32), ALU.subtract).then_inc(s_xl, 1)
            def result(n, q, stored):
                dve.wait_ge(s_dn, n - 1)
                dve.wait_ge(s_yst[q], stored)
                dve.tensor_copy(y_sb[q][:, :], ps_y[q][:, 0:H]).then_inc(s_y, 1)

            with dve.Fori(0, SLOTS // UNROLL) as it:
                for u in range(UNROLL):
                    n = it * UNROLL + (u + 4)
                    q, o = u % 2, (u - 1) % 2
                    dve.wait_ge(s_silu, n + 1)
                    dve.wait_ge(s_hT, n - 1)
                    dve.tensor_tensor(h_sb[q][:, :], ps_up[q][:, F:2 * F], silu[q][:, :],
                                      ALU.mult).then_inc(s_h, 1)
                    dve.wait_ge(s_xh, n + 3)
                    dve.tensor_tensor(xb[q][1][:, :, :], ps_x[q][:, 0:H].rearrange("p (k n) -> p k n", k=KC),
                                      xb[q][0][:, :, :].bitcast(F32), ALU.subtract).then_inc(s_xl, 1)
                    result(n, q, it * 32 + 16 + (16 if u >= 2 else 0))
                    dve.wait_ge(s_hh, n)
                    dve.tensor_tensor(hb[o][1][:, :, :], ps_h[o][0:FC, 0:2 * P].rearrange("p (k n) -> p k n", k=2),
                                      hb[o][0][:, :, :].bitcast(F32), ALU.subtract).then_inc(s_hl, 1)
            result(SLOTS + 4, 0, SLOTS * 8 + 16)

        @block.gpsimd
        def _(pool):
            for signal, count in start_at:
                pool.sem_inc(signal, count)
            for signal in s_yst:
                pool.sem_inc(signal, 16)

            def fetch(buf, seen, loaded):
                pool.wait_ge(s_gi[buf], loaded)
                pool.wait_ge(s_tick, seen - 1)
                pool.tensor_tensor(tick_e[:, :], c["lane"][:, :], c["lane"][:, :],
                                   ALU.add).then_inc(s_tick, 1)
                pool.indirect_dma_start(xg[buf][:, :], None, d["xn"],
                                        bass.IndirectOffsetOnAxis(ap=g_i[buf][:, :], axis=0)
                                        ).then_inc(s_ga[buf], 16)

            for j in range(UNROLL + 1):
                if j == UNROLL:
                    pool.wait_ge(s_xT, 5)
                fetch(j % UNROLL, 5 + j, 16 + 16 * (j // UNROLL))
            with pool.Fori(0, SLOTS // UNROLL) as it:
                for u in range(UNROLL):
                    n = it * UNROLL + (u + 4)
                    pool.wait_ge(s_xT, n + 2)
                    fetch((u + 1) % UNROLL, n + 6, it * 16 + (32 if u < UNROLL - 1 else 48))
            for i in range(UNROLL):
                pool.wait_ge(s_ga[i], 16 * (SLOTS // UNROLL + 1 + (i < 1)))


def attention_order():
    fill = {t: [] for t in range(NT)}
    fill[0] = [("k", 0, 1, 0), ("split", 0, 1, 0), ("v", 0, 4, 0)]
    fill[1] = [("k", 0, 1, 1), None, ("v", 0, 5, 0)]
    fill[2] = [("split", 0, 1, 1), None, ("v", 0, 6, 0)]
    fill[3] = [None, None, ("v", 0, 7, 0)]
    fill[4] = [("xT", 1, 0, 0), ("xT", 1, 0, 1), ("q", 1, 0, 0), ("q", 1, 0, 1)]
    fill[5] = [("split", 1, 0, 0), ("k", 1, 0, 0), ("k", 1, 0, 1), ("v", 1, 0, 0)]
    fill[6] = [("v", 1, 1, 0), ("v", 1, 2, 0), ("v", 1, 3, 0)]
    fill[7] = [("split", 1, 0, 1), ("xT", 1, 1, 0), ("xT", 1, 1, 1)]
    order = [("norms", 0, 0, j) for j in range(NB3)]
    for t in range(NT):
        more = fill[t] + [None] * 4
        order += [("scores", 0, t, 0), ("scores", 0, t, 1)]
        if t:
            order.append(("fine", 0, t - 1, 0))
        else:
            order.append(("mean", 0, 0, 0))
        order += [("scores", 0, t, 2), ("coarseT", 0, t, 0)]
        if t:
            order.append(("fine", 0, t - 1, 1))
        order += [("scores", 0, t, 3)]
        order += [("keys", 0, t, 0), more[0], ("hidden", 0, t, 0)]
        if t > 1:
            order.append(("oproj", 0, t - 2, 0))
        if t < NT - 1:
            order += [("norms", 0, t + 1, j) for j in range(NB3)]
        if t == 0:
            order.append(("weights", 0, 0, 0))
        order += [more[1], ("local", 0, t, 0), more[2], ("gate", 0, t, 0)]
        if t < NT - 1:
            order.append(("state", 0, t, 0))
        order.append(more[3])
        if t:
            order.append(("outT", 0, t - 1, 0))
    last = NT - 1
    order += [("fine", 0, last, 0), ("fine", 0, last, 1), ("q", 1, 1, 0), ("oproj", 0, last - 1, 0),
              ("q", 1, 1, 1), ("outT", 0, last, 0), ("oproj", 0, last, 0)]
    return [x for x in order if x]


ATT_ORDER = attention_order()
NR = 8
RING = [x for x in ATT_ORDER if x[0] not in ("weights", "split", "fine")]
TURN = {use: n for n, use in enumerate(RING)}


def attention_phase(nc, d, c, w):
    with ExitStack() as scope:
        sb, bank_, sem = places(nc, scope)
        x_in = c["x_in"]
        xT = [sb(f"a_xT{i}", [P, KC, ST], F32R) for i in range(2)]
        sqT, skT = sb("sqT", [P, KC, SEQ]), sb("skT", [P, KC, SEQ])
        v1 = sb("v1", [P, NT, NH, HE])
        keep, gate = sb("keep", [P, NH]), sb("gate_s", [P, NH])
        half_b2 = sb("half_b2", [P, 1])
        ones = sb("ones", [P, P])
        q_st = sb("q_st", [P, NP, SEQ], F32R)
        k_st = sb("k_st", [P, NP, SEQ], F32R)
        parts = [sb(f"part_{i}", [P, KC, ST], F32R) for i in range(2)]
        mem = sb("mem_all", [P, NP, MV])
        mem_st = sb("mem_st", [P, NP, WN], F32R)
        with_mem = [sb(f"with_mem{q}", [P, NP, WN]) for q in range(2)]
        mem_part = [with_mem[i][:, :, 0:MV].bitcast(F32R) for i in range(2)]
        norm_bd = sb("norm_bd", [P, KC, PP, NM, 2])
        alive = sb("alive", [P, NM + 1])
        nsum = sb("nsum", [P, NM + 1])
        elu_e, elu_r = sb("elu_e", [P, 2, ST]), sb("elu_r", [P, 2, ST])
        qsum, qtot, qmean = sb("qsum", [P, KC, NS]), sb("qtot", [P, KC]), sb("qmean", [P, KC, P])
        mw, mw_m = sb("mw", [P, NP, NM, 2]), sb("mw_m", [P, 2, NP, 2])
        probs = sb("probs", [P, 4, 4, P])
        k_tok = sb("k_tok", [P, H])
        state, kvm = sb("state", [P, KC, HH * HE]), sb("kvm", [P, KC, HH * HE])
        den = sb("den", [P, NH])
        rn_of = [sb(f"rn{q}", [P, NP, NM + 1, 2]) for q in range(2)]
        local, coarseT = sb("local", [P, H]), sb("coarseT", [P, KC, P])
        coarse_of = [sb(f"coarse{q}", [P, H]) for q in range(2)]
        hid, e_t = sb("hid", [G1, P]), sb("e_t", [P, 3])
        coef, coef_c = sb("coef", [P, NP, NM, 2]), sb("coef_c", [P, NH])
        rest = sb("rest", [P, H])
        prod, part = sb("prod", [P, NP, NM, 2 * HD]), sb("part", [P, NP, 2, 2 * HD])
        att = sb("att", [P, H])
        attT = [sb(f"attT{q}", [P, KC, P]) for q in range(2)]
        from_b, cw_b = sb("from_b", [P, TOP, NT], I32), sb("cw_b", [P, TOP, NT])
        yg = [sb(f"yg{i}", [P, TOP, H]) for i in range(4)]
        tick_a = sb("tick_a", [P, 1])
        total = sb("total", [P, NT, H])
        both_parts = total[:, :, :].rearrange("p t c -> p (t c)").bitcast(F32R)
        first_k = [both_parts[:, i * KC * ST:(i + 1) * KC * ST].rearrange("p (k n) -> p k n", k=KC)
                   for i in range(2)]
        low_rows = probs[:, :, :, :].rearrange("p a b c -> p (a b c)")[:, 0:NP * MV]
        ring = [bank_(f"a_ring{i}") for i in range(NR)]

        s_gexp, s_nsum, s_pro, s_ones, s_pdve = (
            sem("a_gexp"), sem("a_nsum"), sem("a_pro"), sem("a_ones"), sem("a_pdve"))
        s_dve, s_pool = sem("a_dve"), sem("a_pool")
        s_tick, s_qtot = sem("a_tick"), sem("a_qtot")
        s_ga = [sem(f"a_ga{i}") for i in range(4)]
        s_x = c["s_x"]
        s_bx, s_out, s_fb, s_yc, s_ysum, s_sum = (
            sem("a_bx"), sem("a_out"), sem("a_fb"), sem("a_yc"), sem("a_ysum"),
            sem("a_sum"))
        ready = {name: sem(f"a_ps_{name}") for name in
                 ("xT", "q", "v", "mean", "k", "norms", "keys", "scores", "outT", "coarseT",
                  "hidden", "local", "gate", "state", "oproj")}
        s_xh, s_xl, s_v = sem("a_xh"), sem("a_xl"), sem("a_v")
        s_elu, s_elu_used, s_sq, s_sk = sem("a_elu"), sem("a_elu_used"), sem("a_sq"), sem("a_sk")
        s_ph, s_pl, s_st = ({what: sem(f"a_{n}_{what}") for what in ("q", "k")} for n in ("ph", "pl", "st"))
        s_first = {what: sem(f"a_first_{what}") for what in ("q", "k")}
        s_with = sem("a_with")
        s_mem, s_zero = sem("a_mem"), sem("a_zero")
        s_qmean, s_mean, s_mx, s_mexp = sem("a_qmean"), sem("a_mean"), sem("a_mx"), sem("a_mexp")
        s_ktok, s_probs, s_kvm, s_state, s_local = (
            sem("a_ktok"), sem("a_probs"), sem("a_kvm"), sem("a_state"), sem("a_local"))
        s_coarse, s_coarseT, s_hid, s_e, s_prod = (
            sem("a_coarse"), sem("a_coarseT"), sem("a_hid"), sem("a_e"), sem("a_prod"))
        s_rest, s_att, s_attT = sem("a_rest"), sem("a_att"), sem("a_attT")

        DVE_LINKS, POOL_LINKS = 78, 25
        per_batch = [
            (s_x, 16), (s_bx, 16), (s_out, 16 * NS), (s_fb, 1), (s_tick, NT), (s_qtot, 1), (s_yc, NT),
            (s_ysum, NT), (s_sum, NT), (s_xh, NS * KC), (s_xl, NS * KC), (s_v, NT),
            (s_elu, 2 * NS * KC), (s_sq, NS * KC), (s_sk, NS * KC), (s_qmean, 1), (s_mean, 1), (s_mx, 1),
            (s_mexp, 1), (s_with, NB3 * NT), (s_ktok, NT), (s_probs, 4 * NT), (s_kvm, NT - 1), (s_state, NT - 1),
            (s_local, NT), (s_coarse, NT), (s_coarseT, NT), (s_hid, NT), (s_e, NT), (s_prod, KC * NT),
            (s_rest, NT), (s_att, NT), (s_attT, NT), (s_dve, DVE_LINKS), (s_pool, POOL_LINKS)]
        STACKED = 16 * 3 * NP
        per_batch += [(s_ph[what], NS) for what in "qk"] + [(s_pl[what], NS) for what in "qk"]
        of_sync, of_pool = ((0, 0), (0, 1), (1, 0), (1, 1), (2, 0)), ((2, 1), (3, 0), (3, 1))
        FIRST = 16 * 3 * len(of_pool)
        per_batch += [(s_st[what], NS * STACKED + FIRST) for what in "qk"]
        stage_times = {
            "xT": NS * KC, "q": NS * KC, "v": NT, "mean": 1, "k": NS * KC, "norms": NB3 * NT, "keys": NT,
            "scores": 4 * NT, "outT": NT, "coarseT": NT, "hidden": NT, "local": NT, "gate": NT,
            "state": NT - 1, "oproj": NT}
        per_batch += [(ready[name], n) for name, n in stage_times.items()]

        elus = [(x[0], x[2], x[3]) for x in ATT_ORDER if x[0] in ("q", "k") and x[1] == 1]
        elus += [(x[0], x[2], x[3]) for x in ATT_ORDER if x[0] in ("q", "k") and x[1] == 0]
        elu_turn = {x: i for i, x in enumerate(elus)}

        last_reader = {
            "xT": s_xl, "q": s_elu, "k": s_elu, "v": s_v, "mean": s_mean, "norms": s_with,
            "keys": s_ktok, "scores": s_probs, "outT": s_attT, "coarseT": s_coarseT, "hidden": s_hid,
            "local": s_local, "gate": s_e, "state": s_kvm, "oproj": s_sum}

        def nth(name, n, j):
            return {"xT": n * KC + j, "q": n * KC + j, "k": n * KC + j, "scores": 4 * n + j,
                    "norms": NB3 * n + j}.get(name, n) + 1

        def read_count(b, name, n, j):
            if name in ("q", "k"):
                return b * len(elus) + elu_turn[(name, n, j)] + 1
            return b * stage_times[name] + nth(name, n, j)

        def bank(name, n, j):
            if name == "fine":
                return None
            return ring[[TURN[x] for x in RING if x[0] == name and x[2:] == (n, j)][0] % NR]

        def use_bank(pe, b, item, items):
            n = TURN[item]
            before = [(k, b) for k in range(n - NR, -1, -NR)]
            k = n + NR * ((len(RING) - 1 - n) // NR)
            before += [(k, b - 1)]
            while k - NR > n:
                k -= NR
                before += [(k, b - 1)]
            for k, bb in before:
                name, off, m, j = RING[k]
                if bb is b and RING[k] not in items:
                    continue
                at = read_count(bb + off, name, m, j)
                if not isinstance(at, int) or at > 0:
                    pe.wait_ge(last_reader[name], at)
                break
            return ring[n % NR]

        x_src = d["xn"].rearrange("(b t p) c -> b p t c", t=NT, p=P)
        base_src = d["base"].rearrange("(b t p) c -> b p t c", t=NT, p=P)
        out_v = d["out"].rearrange("(b s t p) c -> b s p t c", s=NS, t=TS, p=P)
        first = [x for x in ATT_ORDER if x[1] == 1]
        final = [x for x in ATT_ORDER if x[1] == 0]

        def over_batches(eng, walk, after_first=None):
            walk(0, first)
            if after_first:
                after_first()
            with eng.Fori(1, B) as b:
                walk(b, ATT_ORDER)
            walk(B, final)

        def stack_rows(eng, what, s, heads, signal, parts=parts):
            to = {"q": q_st, "k": k_st}[what]
            for g, r in heads:
                for slot, i in enumerate((0, 1, 0) if what == "q" else (0, 0, 1)):
                    eng.dma_start(to[64 * r + HD * slot:64 * r + HD * (slot + 1), g:NP:PP,
                                     s * ST:(s + 1) * ST].bitcast(F32),
                                  parts[i][(2 * g + r) * HD:(2 * g + r + 1) * HD, :, :].bitcast(F32)
                                  ).then_inc(signal, 16)

        block = scope.enter_context(nc.Block())

        @block.sync
        def _(sp):
            def fetch(b):
                sp.dma_start(x_in[:, :, :], x_src[bass.ds(b - 1, 1), :, :, :].rearrange("b p t c -> p (b t) c")
                             ).then_inc(s_x, 16)

            def stack(what, b, s, heads=tuple((g, r) for g in range(PP) for r in range(2)), of=parts):
                sp.wait_ge(s_pl[what], b * NS + s + 1)
                sp.wait_ge(ready["scores"], (b - 1) * 4 * NT + (s + 1) * 4 * TS)
                stack_rows(sp, what, s, heads, s_st[what], of)

            def rest_of(b, more):
                sp.wait_ge(s_out, b * 16 * NS)
                sp.dma_start(total[:, :, :], base_src[bass.ds(b - 1, 1), :, :, :]
                             .rearrange("b p t c -> p (b t) c")).then_inc(s_bx, 16)
                if more:
                    sp.wait_ge(ready["xT"], b * NS * KC + NS * KC)
                    fetch(b + 1)
                for what in "qk":
                    stack(what, b, 1)
                for s in range(NS):
                    if s and more:
                        for what in "qk":
                            stack(what, b + 1, 0)
                    sp.wait_ge(s_sum, b * NT + (s + 1) * TS)
                    sp.dma_start(out_v[bass.ds(b - 1, 1), s, :, :, :].rearrange("b p t c -> p (b t) c"),
                                 total[:, s * TS:(s + 1) * TS, :]).then_inc(s_out, 16)

            memory = [mem[:, :, 0:NM * HD], mem[:, :, NM * HD:NM * (HD + 1)]]
            for to, name in zip(memory, ("mem", "mem_norms")):
                sp.dma_start(to, d[name].rearrange("p (g n) -> p g n", g=NP)).then_inc(s_mem, 16)
            sp.wait_ge(s_pl["k"], NS)
            sp.wait_ge(s_zero, 2)
            stack("q", 1, 0, of_sync)
            stack("k", 1, 0, of_sync, first_k)
            sp.wait_ge(s_st["k"], NS * STACKED + STACKED)
            sp.wait_ge(s_first["k"], FIRST)
            sp.wait_ge(s_zero, 4)
            with sp.Fori(1, B) as b:
                rest_of(b, True)
            rest_of(B, False)
            sp.wait_ge(s_out, (B + 1) * NS * 16)

        @block.tensor
        def _(pe):
            pe.wait_ge(s_ones, 1)
            for m in range(KC):
                mm = pe.matmul(ring[NR - 1][:, 0:NM], ones[:, :], c["norms"][:, m, :],
                               start=(m == 0), stop=(m == KC - 1))
            mm.then_inc(s_nsum, 1)
            pe.wait_ge(s_nsum, 2)

            def walk(b, items):
                for item in items:
                    what, off, n, j = item
                    if what in ("weights", "split", "fine"):
                        continue
                    bb, t = b + off, n
                    tok = slice(t * P, (t + 1) * P)
                    ps = use_bank(pe, b, item, items)
                    if what == "xT":
                        pe.wait_ge(s_x, bb * 16 + 16)
                        for i in range(TS):
                            mm = pe.transpose(ps[:, i * P:(i + 1) * P],
                                              x_in[:, n * TS + i, j * P:(j + 1) * P], c["ident"][:, :])
                    elif what in ("q", "k"):
                        pe.wait_ge(s_xl, bb * NS * KC + (n + 1) * KC)
                        for kc in range(KC):
                            at = kc * 3 * H + (what == "k") * H + j * P
                            mm = three(pe, ps[:, :], [w["wqkv"][i][:, at:at + P] for i in range(2)],
                                       [xT[i][:, kc, :] for i in range(2)],
                                       kc == 0, kc == KC - 1)
                    elif what == "v":
                        pe.wait_ge(s_xl, bb * NS * KC + (t // TS + 1) * KC)
                        for kc in range(KC):
                            at = kc * 3 * H + 2 * H
                            mm = three(pe, ps[:, 0:H], [xT[i][:, kc, (t % TS) * P:(t % TS + 1) * P] for i in range(2)],
                                       [w["wqkv"][i][:, at:at + H] for i in range(2)], kc == 0, kc == KC - 1)
                    elif what == "mean":
                        pe.wait_ge(s_qmean, b + 1)
                        for m in range(KC):
                            mm = pe.matmul(ps[:, m * NM * HH:(m + 1) * NM * HH], qmean[:, m, :],
                                           norm_bd[:, m, :, :, :], start=True, stop=True)
                    elif what == "norms":
                        pe.wait_ge(s_st["q"], b * NS * STACKED + (t // TS + 1) * STACKED)
                        if t == 0:
                            pe.wait_ge(s_first["q"], FIRST)
                        for i, g in enumerate(range(j * BP, min((j + 1) * BP, NP))):
                            mm = pe.matmul(ps[:, i * WN:(i + 1) * WN], q_st[:, g, tok], mem_st[:, g, :],
                                           start=True, stop=True)
                    elif what == "keys":
                        pe.wait_ge(s_sk, b * NS * KC + (t // TS + 1) * KC)
                        for m in range(KC):
                            mm = pe.transpose(ps[:, m * P:(m + 1) * P], skT[:, m, tok], c["ident"][:, :])
                    elif what == "scores":
                        pe.wait_ge(s_st["k"], b * NS * STACKED + (t // TS + 1) * STACKED)
                        if t == 0:
                            pe.wait_ge(s_first["k"], FIRST)
                        rows = slice(64 * (j % 2), 64 * (j % 2) + 3 * HD)
                        for i in range(PP):
                            g = (j // 2) * PP + i
                            mm = pe.matmul(ps[:, i * P:(i + 1) * P], k_st[rows, g, tok], q_st[rows, g, tok],
                                           start=True, stop=True)
                    elif what == "outT":
                        pe.wait_ge(s_att, b * NT + t + 1)
                        for m in range(KC):
                            mm = pe.transpose(ps[:, m * P:(m + 1) * P], att[:, m * P:(m + 1) * P], c["ident"][:, :])
                    elif what == "oproj":
                        pe.wait_ge(s_attT, b * NT + t + 1)
                        for m in range(KC):
                            mm = pe.matmul(ps[:, 0:H], attT[t % 2][:, m, :], c["wo"][:, m, :],
                                           start=(m == 0), stop=(m == KC - 1))
                    elif what == "coarseT":
                        pe.wait_ge(s_coarse, b * NT + t + 1)
                        for m in range(KC):
                            mm = pe.transpose(ps[:, m * P:(m + 1) * P], coarse_of[t % 2][:, m * P:(m + 1) * P],
                                              c["ident"][:, :])
                    elif what == "hidden":
                        pe.wait_ge(s_coarseT, b * NT + t + 1)
                        for m in range(KC):
                            mm = pe.matmul(ps[0:G1, 0:P], c["w1"][:, m, :], coarseT[:, m, :],
                                           start=(m == 0), stop=(m == KC - 1))
                    elif what == "local":
                        pe.wait_ge(s_v, b * NT + t + 1)
                        if t:
                            pe.wait_ge(s_state, b * (NT - 1) + t)
                            for m in range(KC):
                                pe.matmul(ps[:, m * HH * HE:(m + 1) * HH * HE], sqT[:, m, tok], state[:, m, :],
                                          start=(m == 0), stop=False)
                        for g in range(4):
                            pe.wait_ge(s_probs, b * NT * 4 + t * 4 + g + 1)
                            for i in range(4):
                                h = 2 * ((g // 2) * PP + i) + g % 2
                                mm = pe.matmul(ps[:, h * HE:(h + 1) * HE], probs[:, g, i, :], v1[:, t, h, :],
                                               start=(t == 0 and g == 0 and i == 0), stop=(g == 3 and i == 3))
                    elif what == "gate":
                        pe.wait_ge(s_hid, b * NT + t + 1)
                        mm = pe.matmul(ps[:, 0:1], hid[:, :], c["w2"][:, :], start=True, stop=True)
                    elif what == "state":
                        pe.wait_ge(s_ktok, b * NT + t + 1)
                        for m in range(KC):
                            mm = pe.matmul(ps[:, m * HH * HE:(m + 1) * HH * HE], k_tok[:, m * P:(m + 1) * P],
                                           v1[:, t, m * HH:(m + 1) * HH, :], start=True, stop=True)
                    mm.then_inc(ready[what], 1)

            over_batches(pe, walk, lambda: pe.wait_ge(s_pro, 1))

        @block.scalar
        def _(act):
            act.activation(keep[:, :], c["gate"][:, :], ACT.Exp, scale=-1.0).then_inc(s_gexp, 1)

            def walk(b, items):
                for what, off, n, j in items:
                    bb, t = b + off, n
                    if what == "split":
                        name = "qk"[j]
                        act.wait_ge({"q": s_sq, "k": s_sk}[name], bb * NS * KC + (n + 1) * KC)
                        act.wait_ge(s_st["k"], (bb * NS + n) * STACKED)
                        if items is not first:
                            act.wait_ge(s_st["q"], (bb * NS + n + j) * STACKED)
                            for of in "qk":
                                act.wait_ge(s_first[of], FIRST)
                        of = first_k if items is first and j else parts
                        act.activation(of[0][:, :, :],
                                       {"q": sqT, "k": skT}[name][:, :, n * ST:(n + 1) * ST],
                                       ACT.Copy).then_inc(s_ph[name], 1)
                        continue
                    if what not in ("xT", "q", "k", "v", "keys", "outT", "coarseT", "hidden", "gate", "mean",
                                    "norms"):
                        continue
                    ps = bank(what, n, j)
                    act.wait_ge(s_mx if what == "mean" else ready[what],
                                b + 1 if what == "mean" else bb * stage_times[what] + nth(what, n, j))
                    if what == "xT":
                        act.wait_ge(ready["v"], bb * NT + n * TS)
                        act.activation(xT[0][:, j, :], ps[:, :], ACT.Copy).then_inc(s_xh, 1)
                    elif what in ("q", "k"):
                        i = elu_turn[(what, n, j)]
                        act.wait_ge(s_elu_used, bb * len(elus) + i - 1)
                        act.activation(elu_e[:, i % 2, :], ps[:, :], ACT.Exp)
                        act.activation(elu_r[:, i % 2, :], ps[:, :], ACT.Relu).then_inc(s_elu, 1)
                    elif what == "v":
                        act.activation(v1[:, t, :, 0:HD], ps[:, 0:H].rearrange("p (h e) -> p h e", e=HD),
                                       ACT.Copy).then_inc(s_v, 1)
                    elif what == "mean":
                        act.activation(mw[:, :, :, :], mw[:, :, :, :], ACT.Exp).then_inc(s_mexp, 1)
                    elif what == "norms":
                        g = min(BP, NP - j * BP)
                        act.wait_ge(s_prod, b * KC * NT + KC * (t - 1))
                        act.activation(with_mem[t % 2][:, j * BP:j * BP + g, :],
                                       ps[:, 0:g * WN].rearrange("p (g w) -> p g w", g=g),
                                       ACT.Copy).then_inc(s_with, 1)
                    elif what == "keys":
                        act.wait_ge(ready["state"], b * (NT - 1) + t)
                        act.activation(k_tok[:, :], ps[:, 0:H], ACT.Copy).then_inc(s_ktok, 1)
                    elif what == "outT":
                        act.wait_ge(ready["oproj"], b * NT + t - 1)
                        act.activation(attT[t % 2][:, :, :], ps[:, 0:H].rearrange("p (k n) -> p k n", k=KC),
                                       ACT.Copy).then_inc(s_attT, 1)
                        act.wait_ge(s_fb, b + 1)
                        act.wait_ge(s_ga[t % 4], (b - 1) * 32 * TOP + 16 * TOP * (t // 4 + 1))
                        for k in range(TOP):
                            ins = act.activation(yg[t % 4][:, k, :], yg[t % 4][:, k, :], ACT.Copy,
                                                 scale=cw_b[:, k, t:t + 1])
                        ins.then_inc(s_yc, 1)
                    elif what == "coarseT":
                        act.wait_ge(ready["hidden"], b * NT + t)
                        act.activation(coarseT[:, :, :], ps[:, 0:H].rearrange("p (k n) -> p k n", k=KC),
                                       ACT.Copy).then_inc(s_coarseT, 1)
                    elif what == "hidden":
                        act.wait_ge(ready["gate"], b * NT + t)
                        act.activation(hid[:, :], ps[0:G1, 0:P], ACT.Relu, bias=c["b1"][:, 0:1]).then_inc(s_hid, 1)
                    elif what == "gate":
                        act.wait_ge(s_rest, b * NT + t)
                        act.activation(e_t[:, 0:1], ps[:, 0:1], ACT.Tanh,
                                       bias=half_b2[:, 0:1], scale=0.5).then_inc(s_e, 1)

            over_batches(act, walk, lambda: act.wait_ge(s_pro, 1))

        @block.vector
        def _(dve):
            link, links = chain(dve, s_pdve)
            dve.memset(ones[:, :], 1.0).then_inc(s_ones, 1)
            link(dve.memset(v1[:, :, :, HD:HE], 1.0))
            link(dve.tensor_scalar(half_b2[:, :], c["b2"][:, :], 0.5, None, ALU.mult))
            dve.wait_ge(s_gexp, 1)
            link(dve.tensor_scalar(den[:, :], keep[:, :], 1.0, None, ALU.add))
            link(dve.reciprocal(gate[:, :], den[:, :]))
            link(dve.tensor_scalar(keep[:, :], gate[:, :], -1.0, 1.0, ALU.mult, ALU.add))
            dve.wait_ge(s_nsum, 1)
            link(dve.tensor_copy(nsum[:, 0:NM], ring[NR - 1][:, 0:NM]))
            link(dve.tensor_reduce(nsum[:, NM:NM + 1], nsum[:, 0:NM], AX.X, ALU.add))
            link(dve.tensor_scalar(alive[:, :], nsum[:, :], EPS, None, ALU.is_ge))
            dve.sem_inc(s_nsum, 1)

            hi, lo = mem[:, :, :], low_rows[:, :].rearrange("p (g n) -> p g n", g=NP)

            def memory_parts():
                for m in range(KC):
                    for i in range(NM):
                        dve.tensor_tensor(norm_bd[:, m, :, i, :],
                                          c["same_head"][:, :].rearrange("p (g r) -> p g r", r=2),
                                          c["norms"][:, m, i:i + 1].unsqueeze(2).broadcast_to([P, PP, 2]), ALU.mult)
                fine, norms_ = mem[:, :, 0:NM * HD], mem[:, :, NM * HD:NM * (HD + 1)]
                coarse_m, coarse_n = mem[:, :, NM * (HD + 1):MV - 1], mem[:, :, MV - 1]
                dve.wait_ge(s_mem, 32)
                link(dve.tensor_tensor(coarse_m, fine[:, :, 0:HD], fine[:, :, HD:2 * HD], ALU.add))
                for i in range(2, NM):
                    link(dve.tensor_tensor(coarse_m, coarse_m, fine[:, :, i * HD:(i + 1) * HD], ALU.add))
                link(dve.tensor_reduce(coarse_n, norms_, AX.X, ALU.add))
                link(dve.tensor_copy(mem_part[0], mem[:, :, :]))
                link(dve.tensor_tensor(mem_part[1], mem[:, :, :], with_mem[0][:, :, 0:MV], ALU.subtract))

            def memory_rows():
                for r in range(2):
                    dve.tensor_scalar(hi, with_mem[0][:, :, 0:MV], c["hi_of"][:, r:r + 1], None, ALU.mult)
                    link(dve.tensor_scalar(lo, with_mem[1][:, :, 0:MV], c["lo_of"][:, r:r + 1], None, ALU.mult))
                    of_fine = mem_st[:, :, 0:CF].rearrange("p g (n r e) -> p g n r e", r=2, e=HD)
                    of_norms = mem_st[:, :, CC:WN].rearrange("p g (n r) -> p g n r", r=2)
                    by_memory = [x[:, :, 0:NM * HD].rearrange("p g (n e) -> p g n e", e=HD) for x in (hi, lo)]
                    dve.tensor_tensor(of_fine[:, :, :, r, :], by_memory[0], by_memory[1], ALU.add)
                    z = slice(NM * (HD + 1), MV - 1)
                    dve.tensor_tensor(mem_st[:, :, CF + r * HD:CF + (r + 1) * HD], hi[:, :, z], lo[:, :, z], ALU.add)
                    z = slice(NM * HD, NM * (HD + 1))
                    dve.tensor_tensor(of_norms[:, :, 0:NM, r], hi[:, :, z], lo[:, :, z], ALU.add)
                    link(dve.tensor_tensor(of_norms[:, :, NM, r], hi[:, :, MV - 1], lo[:, :, MV - 1], ALU.add))
                dve.sem_inc(s_pro, 1)

            def walk(b, items):
                link, links = chain(dve, s_dve, b * DVE_LINKS)
                for what, off, n, j in items:
                    bb, t = b + off, n
                    if what in ("v", "coarseT", "keys", "hidden", "outT"):
                        continue
                    if what == "split":
                        name = "qk"[j]
                        if items is first and j:
                            memory_rows()
                        dve.wait_ge(s_ph[name], bb * NS + n + 1)
                        of = first_k if items is first and j else parts
                        dve.tensor_tensor(of[1][:, :, :],
                                          {"q": sqT, "k": skT}[name][:, :, n * ST:(n + 1) * ST],
                                          of[0][:, :, :].bitcast(F32), ALU.subtract
                                          ).then_inc(s_pl[name], 1)
                        continue
                    ps = bank(what, n, j) if what != "weights" else None
                    rn, coarse = rn_of[t % 2], coarse_of[t % 2]
                    if what == "xT":
                        dve.wait_ge(s_xh, bb * NS * KC + n * KC + j + 1)
                        dve.tensor_tensor(xT[1][:, j, :], ps[:, :], xT[0][:, j, :].bitcast(F32),
                                          ALU.subtract).then_inc(s_xl, 1)
                    elif what in ("q", "k"):
                        if items is first and (what, n, j) == ("q", 0, 0):
                            memory_parts()
                        i = elu_turn[(what, n, j)]
                        dve.wait_ge(s_elu, bb * len(elus) + i + 1)
                        sup = slice(n * ST, (n + 1) * ST)
                        if what == "q":
                            dve.scalar_tensor_tensor(sqT[:, j, sup], elu_e[:, i % 2, :], 1.0, elu_r[:, i % 2, :],
                                                     ALU.min, ALU.add, accum_out=qsum[:, j, n:n + 1]
                                                     ).then_inc(s_sq, 1)
                            dve.wait_ge(s_sq, bb * NS * KC + n * KC + j + 1)
                        else:
                            dve.scalar_tensor_tensor(skT[:, j, sup], elu_e[:, i % 2, :], 1.0, elu_r[:, i % 2, :],
                                                     ALU.min, ALU.add).then_inc(s_sk, 1)
                            dve.wait_ge(s_sk, bb * NS * KC + n * KC + j + 1)
                        dve.sem_inc(s_elu_used, 1)
                        if (what, n, j) == ("q", NS - 1, KC - 1):
                            dve.tensor_tensor(qtot[:, :], qsum[:, :, 0], qsum[:, :, 1], ALU.add).then_inc(s_qtot, 1)
                            dve.wait_ge(s_qtot, bb + 1)
                            for m in range(KC):
                                ins = dve.tensor_scalar(qmean[:, m, :], ones[:, :], qtot[:, m:m + 1], 1.0 / SEQ,
                                                        ALU.mult, ALU.mult)
                            ins.then_inc(s_qmean, 1)
                    elif what == "mean":
                        by_memory = mw[:, :, :, :].rearrange("p g n r -> p g r n")
                        dve.wait_ge(ready["mean"], b + 1)
                        dve.tensor_copy(mw[:, :, :, :].rearrange("p g n r -> p (g n r)"),
                                        ps[:, 0:KC * NM * HH]).then_inc(s_mean, 1)
                        dve.wait_ge(s_mean, b + 1)
                        link(dve.tensor_reduce(mw_m[:, 0, :, :], by_memory, AX.X, ALU.max))
                        dve.tensor_tensor(mw[:, :, :, :], mw[:, :, :, :],
                                          mw_m[:, 0, :, :].unsqueeze(2).broadcast_to([P, NP, NM, 2]),
                                          ALU.subtract).then_inc(s_mx, 1)
                    elif what == "weights":
                        dve.wait_ge(s_mexp, b + 1)
                        link(dve.tensor_reduce(mw_m[:, 0, :, :], by_memory, AX.X, ALU.add))
                        link(dve.reciprocal(mw_m[:, 1, :, :], mw_m[:, 0, :, :]))
                        link(dve.tensor_tensor(mw_m[:, 0, :, :], mw_m[:, 1, :, :],
                                               gate[:, :].rearrange("p (g r) -> p g r", r=2), ALU.mult))
                        link(dve.tensor_tensor(mw[:, :, :, :], mw[:, :, :, :],
                                               mw_m[:, 0, :, :].unsqueeze(2).broadcast_to([P, NP, NM, 2]),
                                               ALU.mult))
                        link(dve.tensor_tensor(mw[:, :, :, :], mw[:, :, :, :],
                                               alive[:, 0:NM].unsqueeze(1).unsqueeze(3)
                                               .broadcast_to([P, NP, NM, 2]), ALU.mult))
                    elif what == "norms":
                        if j < NB3 - 1:
                            continue
                        dve.wait_ge(s_with, b * NB3 * NT + NB3 * (t + 1))
                        both = with_mem[t % 2]
                        link(dve.tensor_scalar(rn[:, :, :, :].rearrange("p g n r -> p g (n r)"),
                                               both[:, :, CC:], EPS, None, ALU.max))
                        link(dve.reciprocal(rn[:, :, :, :], rn[:, :, :, :]))
                        link(dve.tensor_scalar(rn[:, :, NM, :], rn[:, :, NM, :], alive[:, NM:NM + 1],
                                               None, ALU.mult))
                        dve.wait_ge(ready["coarseT"], b * NT + t - 1)
                        dve.wait_ge(s_rest, b * NT + t - 1)
                        dve.tensor_tensor(coarse[:, :].rearrange("p (g r e) -> p g r e", r=2, e=HD),
                                          both[:, :, CF:CC].rearrange("p g (r e) -> p g r e", e=HD),
                                          rn[:, :, NM, :].unsqueeze(3).broadcast_to([P, NP, 2, HD]),
                                          ALU.mult).then_inc(s_coarse, 1)
                    elif what == "scores":
                        dve.wait_ge(ready["scores"], b * 4 * NT + 4 * t + j + 1)
                        dve.wait_ge(ready["local"], b * NT + t)
                        dve.tensor_tensor(probs[:, j, :, :], ps[:, :].rearrange("p (h i) -> p h i", i=P),
                                          c["causal"][:, :].unsqueeze(1).broadcast_to([P, 4, P]),
                                          ALU.mult).then_inc(s_probs, 1)
                    elif what == "local":
                        heads = ps[:, 0:NH * HE].rearrange("p (h e) -> p h e", e=HE)
                        dve.wait_ge(ready["local"], b * NT + t + 1)
                        link(dve.tensor_scalar(den[:, :], heads[:, :, HD], EPS, None, ALU.max))
                        link(dve.reciprocal(den[:, :], den[:, :]))
                        link(dve.tensor_tensor(den[:, :], den[:, :], keep[:, :], ALU.mult))
                        dve.tensor_tensor(local[:, :].rearrange("p (h e) -> p h e", e=HD), heads[:, :, 0:HD],
                                          den[:, :].unsqueeze(2).broadcast_to([P, NH, HD]),
                                          ALU.mult).then_inc(s_local, 1)
                    elif what == "gate":
                        dve.wait_ge(s_e, b * NT + t + 1)
                        dve.tensor_scalar(e_t[:, 1:2], e_t[:, 0:1], 0.5, 0.5, ALU.mult, ALU.add)
                        link(dve.tensor_scalar(e_t[:, 2:3], e_t[:, 0:1], -0.5, 0.5, ALU.mult, ALU.add))
                        dve.scalar_tensor_tensor(coef[:, :, :, :].rearrange("p g n r -> p g (n r)"),
                                                 rn[:, :, 0:NM, :].rearrange("p g n r -> p g (n r)"),
                                                 e_t[:, 1:2], mw[:, :, :, :].rearrange("p g n r -> p g (n r)"),
                                                 ALU.mult, ALU.mult)
                        link(dve.tensor_scalar(coef_c[:, :], gate[:, :], e_t[:, 2:3], None, ALU.mult))
                        dve.wait_ge(s_att, b * NT + t)
                        link(dve.tensor_tensor(rest[:, :].rearrange("p (h e) -> p h e", e=HD),
                                               coarse[:, :].rearrange("p (h e) -> p h e", e=HD),
                                               coef_c[:, :].unsqueeze(2).broadcast_to([P, NH, HD]), ALU.mult))
                        dve.wait_ge(s_local, b * NT + t + 1)
                        dve.tensor_tensor(rest[:, :], rest[:, :], local[:, :], ALU.add).then_inc(s_rest, 1)
                    elif what == "state":
                        dve.wait_ge(ready["state"], b * (NT - 1) + t + 1)
                        kv = kvm if t else state
                        if t == 0:
                            dve.wait_ge(ready["local"], b * NT)
                        else:
                            dve.wait_ge(ready["local"], b * NT + t + 1)
                        ins = dve.tensor_tensor(kv[:, :, :].rearrange("p k (h e) -> p k h e", e=HE),
                                                ps[:, 0:KC * HH * HE].rearrange("p (k h e) -> p k h e", k=KC, e=HE),
                                                c["same_head"][:, :].unsqueeze(1).unsqueeze(3)
                                                .broadcast_to([P, KC, HH, HE]), ALU.mult)
                        ins.then_inc(s_kvm, 1)
                        dve.wait_ge(s_kvm, b * (NT - 1) + t + 1)
                        if t:
                            dve.tensor_tensor(state[:, :, :], state[:, :, :], kvm[:, :, :],
                                              ALU.add).then_inc(s_state, 1)
                        else:
                            dve.sem_inc(s_state, 1)
                    elif what == "fine":
                        if j == 0:
                            dve.wait_ge(s_att, b * NT + t)
                        half = slice(j * PP, (j + 1) * PP)
                        dve.tensor_tensor(prod[:, half, :, :].rearrange("p g n (r e) -> p g (n r) e", e=HD),
                                          with_mem[t % 2][:, half, 0:CF].rearrange("p g (m e) -> p g m e", e=HD),
                                          coef[:, half, :, :].rearrange("p g n r -> p g (n r)").unsqueeze(3)
                                          .broadcast_to([P, PP, NM * 2, HD]), ALU.mult).then_inc(s_prod, 1)
                    elif what == "oproj":
                        dve.wait_ge(ready["oproj"], b * NT + t + 1)
                        dve.wait_ge(s_ysum, b * NT + t + 1)
                        dve.tensor_tensor(total[:, t, :], ps[:, 0:H], total[:, t, :], ALU.add).then_inc(s_sum, 1)
                assert items is first or links[0] == DVE_LINKS, links[0]

            over_batches(dve, walk)

        @block.gpsimd
        def _(pool):
            for signal, count in per_batch + [(s_elu_used, 2 * NS * KC)]:
                pool.sem_inc(signal, count)
            for s in range(NS):
                for r in range(2):
                    pool.memset(q_st[64 * r + 2 * HD:64 * (r + 1), :, s * ST:(s + 1) * ST].bitcast(F32), 0.0
                                ).then_inc(s_zero, 1)
                    pool.wait_ge(s_zero, 2 * s + r + 1)
                if s == 0:
                    for what, of in (("q", parts), ("k", first_k)):
                        pool.wait_ge(s_pl[what], NS + 1)
                        stack_rows(pool, what, 0, of_pool, s_first[what], of)

            def walk(b, items):
                if items is first:
                    return
                link, links = chain(pool, s_pool, b * POOL_LINKS)
                for i in range(4):
                    pool.wait_ge(s_ga[i], (b - 1) * 32 * TOP)
                pool.wait_ge(s_yc, b * NT)
                link(pool.tensor_copy(from_b[:, :, :], c["from"][:, :, bass.ds((b - 1) * NT, NT)]))
                pool.tensor_copy(cw_b[:, :, :], c["cw"][:, :, bass.ds((b - 1) * NT, NT)]).then_inc(s_fb, 1)

                def fetch(t):
                    pool.wait_ge(s_tick, b * NT + t)
                    pool.tensor_tensor(tick_a[:, :], c["lane"][:, :], c["lane"][:, :],
                                       ALU.add).then_inc(s_tick, 1)
                    for k in range(TOP):
                        pool.indirect_dma_start(
                            yg[t % 4][:, k, :], None, d["grouped_y"],
                            bass.IndirectOffsetOnAxis(ap=from_b[:, k, t:t + 1], axis=0)).then_inc(s_ga[t % 4], 16)

                pool.wait_ge(s_ysum, b * NT)
                for t in range(4):
                    fetch(t)
                for what, _, t, j in [x for x in items if x[1] == 0]:
                    if what == "outT":
                        pool.wait_ge(s_bx, b * 16 + 16)
                        pool.wait_ge(s_yc, b * NT + t + 1)
                        link(pool.tensor_tensor(yg[t % 4][:, 0, :], yg[t % 4][:, 0, :], yg[t % 4][:, 1, :], ALU.add))
                        pool.tensor_tensor(total[:, t, :], total[:, t, :], yg[t % 4][:, 0, :],
                                           ALU.add).then_inc(s_ysum, 1)
                        if t < 4:
                            pool.wait_ge(s_ysum, b * NT + t + 1)
                            fetch(t + 4)
                    elif what == "fine" and j == KC - 1:
                        pool.wait_ge(s_prod, b * KC * NT + KC * (t + 1))
                        pool.wait_ge(s_rest, b * NT + t + 1)
                        link(pool.tensor_tensor(part[:, :, :, :], prod[:, :, 0:2, :], prod[:, :, 2:4, :], ALU.add))
                        pool.wait_ge(ready["outT"], b * NT + t)
                        link(pool.tensor_tensor(att[:, :].rearrange("p (g n) -> p g n", g=NP),
                                                part[:, :, 0, :], part[:, :, 1, :], ALU.add))
                        pool.tensor_tensor(att[:, :], att[:, :], rest[:, :], ALU.add).then_inc(s_att, 1)
                assert links[0] == POOL_LINKS, links[0]

            over_batches(pool, walk)


def build(nc, d):
    with ExitStack() as scope:
        sb, _, sem = places(nc, scope)
        c = {name: sb(name, list(shape)) for name, shape in (
            ("ident", (P, P)), ("before", (P, P)), ("causal", (P, P)), ("same_head", (P, HH)), ("hi_of", (P, 2)), ("lo_of", (P, 2)), ("rank_e", (P, E)), ("region", (P, E)), ("blk_row", (P, NI)),
            ("lane", (P, 1)), ("wo", (P, KC, H)), ("w1", (P, KC, G1)), ("b1", (G1, 1)), ("w2", (G1, 1)),
            ("b2", (P, 1)), ("gate", (P, NH)), ("norms", (P, KC, NM)))}
        c["number"] = sb("number", [P, NTA], I32)
        loads = []
        for name, t in c.items():
            if len(t.shape) == 3:
                loads.append((t[:, :, :], d[name].rearrange("(k p) n -> p k n", p=P)))
            else:
                loads.append((t[:, :], d[name]))
        c["loads"], c["n_load"], c["s_load"] = loads, len(loads), sem("c_load")
        c["from"], c["cw"] = sb("from_row", [P, TOP, NTA], I32), sb("cw", [P, TOP, NTA])
        c["x_in"], c["s_x"] = sb("xn_in", [P, NT, H]), sem("a_x")
        w = {"wqkv": [sb(f"wqkv{i}", [P, WQKV], F32R) for i in range(2)]}
        with ExitStack() as experts:
            sb, _, _ = places(nc, experts)
            c["picks"], c["dist"] = sb("picks", [P, TOP, NTA, E]), sb("dist", [P, NTA, E])
            c["slots"], c["run"] = sb("slots", [P, TOP, NTA]), sb("run", [P, E])
            c["start"], c["pack"] = sb("start_i", [P, NI], I32), sb("pack_i", [P, NI // UNROLL], I32)
            w["wb"] = [sb(f"wb{i}", [P, WUP], F32R) for i in range(2)]
            w["wd"] = [sb(f"wd{i}", [FC, E * 2 * H], F32R) for i in range(2)]
            tokens_phase(nc, d, c, w)
            experts_phase(nc, d, c, w)
        attention_phase(nc, d, c, w)


def kernel(**inputs):
    import concourse.bacc as _bacc
    from concourse.bass_utils import run_bass_kernel_spmd as _run

    a = {k: np.asarray(v) for k, v in inputs.items()}
    part = np.arange(P)

    def chunks(x):
        return np.stack([x[k * P:(k + 1) * P] for k in range(KC)], 1)

    def stacked(x):
        x = x.reshape(NP, 2, 1, HD, -1).transpose(1, 2, 3, 0, 4)
        return np.broadcast_to(x, (2, 4, HD, NP, x.shape[-1])).reshape(P, -1)

    gate_up = np.concatenate([a["L0_ffn_w_gate"], a["L0_ffn_w_up"]], 1)
    qkv = np.concatenate([a["L0_attn_w_q"], a["L0_attn_w_k"], a["L0_attn_w_v"]])
    arrays = {
        "x_tok": a["L0_attn_hidden_states"].reshape(T, H),
        "w_up": chunks(gate_up.transpose(2, 0, 1)).reshape(P, WUP),
        "w_qkv": chunks(qkv.T).reshape(P, WQKV),
        "wd_all": a["L0_ffn_w_down"].transpose(0, 2, 1).reshape(E, 2, FC, H).transpose(2, 0, 1, 3)
                  .reshape(FC, E * 2 * H),
        "sg_t": np.concatenate([a["L0_ffn_sw_gate"], a["L0_ffn_gate_weight"]]).T,
        "su_t": a["L0_ffn_sw_up"].T,
        "sd_t": a["L0_ffn_sw_down"].T,
        "wo": a["L0_attn_w_o"].T,
        "w1": a["L0_attn_eg_w1"].T,
        "b1": a["L0_attn_eg_b1"].reshape(G1, 1),
        "w2": a["L0_attn_eg_w2"].T,
        "b2": np.broadcast_to(a["L0_attn_eg_b2"].reshape(1, 1), (P, 1)),
        "gate": np.broadcast_to(a["L0_attn_memory_gate"].reshape(1, NH), (P, NH)),
        "mem": stacked(a["L0_attn_fine_memories"].transpose(1, 2, 0, 3).reshape(NH, HD, NM * HD)),
        "mem_norms": stacked(a["L0_attn_fine_memory_norms"].transpose(1, 2, 0)),
        "norms": a["L0_attn_fine_memory_norms"].transpose(1, 2, 0).reshape(H, NM),
        "ident": np.eye(P, dtype=np.float32),
        "before": np.triu(np.ones((P, P), np.float32), 1),
        "causal": np.triu(np.ones((P, P), np.float32)),
        "hi_of": np.stack([(part // 64 == k) & (part // HD % 4 < 2) for k in range(2)], 1).astype(np.float32),
        "lo_of": np.stack([(part // 64 == k) & (part // HD % 4 == 2) for k in range(2)], 1).astype(np.float32),
        "same_head": (part[:, None] // HD == np.arange(HH)[None, :]).astype(np.float32),
        "rank_e": np.broadcast_to(np.arange(E, 0, -1).astype(np.float32), (P, E)),
        "region": np.broadcast_to((np.arange(E) * T).astype(np.float32), (P, E)),
        "blk_row": np.broadcast_to(np.arange(NI).astype(np.float32), (P, NI)),
        "number": (np.arange(NTA)[None, :] * P + part[:, None]).astype(np.int32),
        "lane": part.astype(np.float32).reshape(P, 1),
    }
    nc = _bacc.Bacc("TRN2", target_bir_lowering=False, num_devices=1)
    arrays = {k: np.ascontiguousarray(v) for k, v in arrays.items()}
    d = {k: nc.dram_tensor("in_" + k, v.shape, mybir.dt.from_np(v.dtype), kind="ExternalInput").ap()
         for k, v in arrays.items()}
    d["lists"] = nc.dram_tensor("d_lists", (E * T, 1), I32, kind="Internal").ap()
    for name, rows in (("xn", T), ("base", T), ("grouped_y", (SLOTS + 1) * P)):
        d[name] = nc.dram_tensor("d_" + name, (rows, H), F32, kind="Internal").ap()
    d["out"] = nc.dram_tensor("out", (T, H), F32, kind="ExternalOutput").ap()
    build(nc, d)
    r = _run(nc, [{"in_" + k: v for k, v in arrays.items()}], core_ids=[0])
    return r.results[0]["out"].reshape(B, SEQ, H)
```
